# Optimizing a Trainium2 kernel written in Bass

```python
import numpy as np
import jax
import jax.numpy as jnp

def _softmax(x, axis=-1):
    return jax.nn.softmax(x, axis=axis)

def _gelu(x):
    return jax.nn.gelu(x, approximate=True)

def _silu(x):
    return jax.nn.silu(x)

def _sigmoid(x):
    return jax.nn.sigmoid(x)

def _layernorm(x, axis=-1, eps=1e-05):
    m = jnp.mean(x, axis=axis, keepdims=True)
    v = jnp.var(x, axis=axis, keepdims=True)
    return (x - m) / jnp.sqrt(v + eps)

def _scatter_add(tgt, idx, src, axis=0):
    return tgt.at[idx].add(src)

def _segment_sum(src, seg, n):
    return jax.ops.segment_sum(src, seg, n)
kernel_name = 'mk_prb_d1_jaxref_r2_944f6e'

def setup_inputs(seed: int=0):
    np.random.seed(seed)
    _w = jnp.asarray

    def _L0_attn_setup():
        import jax, jax.numpy as jnp
        import numpy as np
        D_MODEL = 512
        D_STATE = 64
        HEADDIM = 32
        D_INNER = 1024
        NHEADS = D_INNER // HEADDIM
        NUM_ROPE = 16
        A_FLOOR = 0.0001
        EPS = 1e-05
        D_IN_PROJ = 2 * D_INNER + 2 * D_STATE + 3 * NHEADS + NUM_ROPE
        B, S = (2, 512)

        def _rms(v, w):
            return v * jax.lax.rsqrt(jnp.mean(v * v, axis=-1, keepdims=True) + EPS) * w
        key = jax.random.key(seed)
        ks = jax.random.split(key, 4)
        u = jax.random.normal(ks[0], (B, S, D_MODEL), jnp.float32)
        W_in = jax.random.normal(ks[1], (D_IN_PROJ, D_MODEL), jnp.float32) / np.sqrt(D_MODEL).astype(np.float32)
        W_out = jax.random.normal(ks[2], (D_MODEL, D_INNER), jnp.float32) / np.sqrt(D_INNER).astype(np.float32)
        dt_init = jnp.clip(jnp.exp(jax.random.uniform(ks[3], (NHEADS,), jnp.float32) * (np.log(0.1) - np.log(0.001)) + np.log(0.001)), 0.0001, None)
        dt_bias = dt_init + jnp.log(-jnp.expm1(-dt_init))
        return {'u': u, 'W_in': W_in, 'dt_bias': dt_bias, 'B_bias': jnp.ones((NHEADS, D_STATE), jnp.float32), 'C_bias': jnp.ones((NHEADS, D_STATE), jnp.float32), 'Bn_w': jnp.ones((D_STATE,), jnp.float32), 'Cn_w': jnp.ones((D_STATE,), jnp.float32), 'D': jnp.ones((NHEADS,), jnp.float32), 'W_out': W_out}
    _L0_attn_in = _L0_attn_setup()

    def _L0_ffn_setup():
        import jax, jax.numpy as jnp
        import numpy as np
        D_MODEL = 512
        M = 64
        INNER = 16
        key = jax.random.key(seed)
        ks = jax.random.split(key, 9)

        def init(k, shape, fan_in):
            bound = 1.0 / np.sqrt(fan_in)
            return jax.random.uniform(k, shape, jnp.float32, -bound, bound)
        x = jax.random.normal(ks[0], (16, 2048, D_MODEL), dtype=jnp.float32)
        Win = init(ks[1], (D_MODEL, M), D_MODEL)
        bin_ = init(ks[2], (M,), D_MODEL)
        W1 = init(ks[3], (M, INNER), 1)
        b1 = init(ks[4], (M, INNER), 1)
        W2 = init(ks[5], (M, INNER), INNER)
        b2 = init(ks[6], (M,), INNER)
        Wout = init(ks[7], (M, D_MODEL), M)
        bout = init(ks[8], (D_MODEL,), M)
        return {'x': x, 'Win': Win, 'bin_': bin_, 'W1': W1, 'b1': b1, 'W2': W2, 'b2': b2, 'Wout': Wout, 'bout': bout}
    _L0_ffn_in = _L0_ffn_setup()
    _d = {'L0_attn_u': _L0_attn_in['u'], 'L0_attn_W_in': _L0_attn_in['W_in'], 'L0_attn_dt_bias': _L0_attn_in['dt_bias'], 'L0_attn_B_bias': _L0_attn_in['B_bias'], 'L0_attn_C_bias': _L0_attn_in['C_bias'], 'L0_attn_Bn_w': _L0_attn_in['Bn_w'], 'L0_attn_Cn_w': _L0_attn_in['Cn_w'], 'L0_attn_D': _L0_attn_in['D'], 'L0_attn_W_out': _L0_attn_in['W_out'], 'L0_ffn_Win': _L0_ffn_in['Win'], 'L0_ffn_bin_': _L0_ffn_in['bin_'], 'L0_ffn_W1': _L0_ffn_in['W1'], 'L0_ffn_b1': _L0_ffn_in['b1'], 'L0_ffn_W2': _L0_ffn_in['W2'], 'L0_ffn_b2': _L0_ffn_in['b2'], 'L0_ffn_Wout': _L0_ffn_in['Wout'], 'L0_ffn_bout': _L0_ffn_in['bout']}
    _x0 = _d['L0_attn_u']
    _d['L0_attn_u'] = jax.random.normal(jax.random.fold_in(jax.random.key(seed), 1), (4, 4096, 512), dtype=_x0.dtype)
    del _x0
    return _d

def reference(L0_attn_u, L0_attn_W_in, L0_attn_dt_bias, L0_attn_B_bias, L0_attn_C_bias, L0_attn_Bn_w, L0_attn_Cn_w, L0_attn_D, L0_attn_W_out, L0_ffn_Win, L0_ffn_bin_, L0_ffn_W1, L0_ffn_b1, L0_ffn_W2, L0_ffn_b2, L0_ffn_Wout, L0_ffn_bout):

    def _L0_attn_ref(u, W_in, dt_bias, B_bias, C_bias, Bn_w, Cn_w, D, W_out):
        import jax, jax.numpy as jnp
        import numpy as np
        D_MODEL = 512
        D_STATE = 64
        HEADDIM = 32
        D_INNER = 1024
        NHEADS = D_INNER // HEADDIM
        NUM_ROPE = 16
        A_FLOOR = 0.0001
        EPS = 1e-05
        D_IN_PROJ = 2 * D_INNER + 2 * D_STATE + 3 * NHEADS + NUM_ROPE
        B, S = (2, 512)

        def _rms(v, w):
            return v * jax.lax.rsqrt(jnp.mean(v * v, axis=-1, keepdims=True) + EPS) * w
        b, s, _ = u.shape
        proj = jnp.einsum('bsd,kd->bsk', u, W_in)
        sp = np.cumsum([D_INNER, D_INNER, D_STATE, D_STATE, NHEADS, NHEADS, NHEADS])
        z, x, B_raw, C_raw, dd_dt, dd_A, trap_raw, angles = jnp.split(proj, sp, axis=-1)
        x = x.reshape(b, s, NHEADS, HEADDIM)
        z = z.reshape(b, s, NHEADS, HEADDIM)
        Bm = _rms(B_raw, Bn_w)[:, :, None, :] + B_bias
        Cm = _rms(C_raw, Cn_w)[:, :, None, :] + C_bias
        cos = jnp.cos(angles)[:, :, None, :]
        sin = jnp.sin(angles)[:, :, None, :]

        def rot(v):
            v1, v2 = (v[..., :NUM_ROPE], v[..., NUM_ROPE:2 * NUM_ROPE])
            return jnp.concatenate([v1 * cos - v2 * sin, v1 * sin + v2 * cos, v[..., 2 * NUM_ROPE:]], axis=-1)
        Bm, Cm = (rot(Bm), rot(Cm))
        A = jnp.minimum(-jax.nn.softplus(dd_A), -A_FLOOR)
        dt = jax.nn.softplus(dd_dt + dt_bias)
        trap = jax.nn.sigmoid(trap_raw)
        g = 1.0 - 0.5 * trap
        a = g * jnp.exp(A * dt) + 0.5 * trap
        gdtB = (g * dt)[..., None] * Bm

        def step(h, inp):
            a_t, gb_t, c_t, x_t = inp
            h = a_t[:, :, None, None] * h + x_t[..., None] * gb_t[:, :, None, :]
            y = jnp.einsum('bhpn,bhn->bhp', h, c_t) + D[None, :, None] * x_t
            return (h, y)
        h0 = jnp.zeros((b, NHEADS, HEADDIM, D_STATE), jnp.float32)
        xs = (a.transpose(1, 0, 2), gdtB.transpose(1, 0, 2, 3), Cm.transpose(1, 0, 2, 3), x.transpose(1, 0, 2, 3))
        _, ys = jax.lax.scan(step, h0, xs)
        y = ys.transpose(1, 0, 2, 3) * jax.nn.silu(z)
        return jnp.einsum('bsk,dk->bsd', y.reshape(b, s, D_INNER), W_out)

    def _L0_ffn_ref(x, Win, bin_, W1, b1, W2, b2, Wout, bout):
        import jax, jax.numpy as jnp
        import numpy as np
        D_MODEL = 512
        M = 64
        INNER = 16
        s = jnp.einsum('btd,dm->btm', x, Win) + bin_
        h = jax.nn.relu(s[..., None] * W1 + b1)
        g = jnp.einsum('btmh,mh->btm', h, W2) + b2
        out = jnp.einsum('btm,md->btd', g, Wout) + bout
        return out
    x = L0_attn_u
    xn = _layernorm(x, axis=-1)
    x = x + _L0_attn_ref(xn, L0_attn_W_in, L0_attn_dt_bias, L0_attn_B_bias, L0_attn_C_bias, L0_attn_Bn_w, L0_attn_Cn_w, L0_attn_D, L0_attn_W_out) + _L0_ffn_ref(xn, L0_ffn_Win, L0_ffn_bin_, L0_ffn_W1, L0_ffn_b1, L0_ffn_W2, L0_ffn_b2, L0_ffn_Wout, L0_ffn_bout)
    return x

_drawn_inputs = setup_inputs


def setup_inputs(seed=0):
    import zlib

    import numpy as np

    out = dict(_drawn_inputs(seed))
    spreads = {'L0_attn_B_bias': (1.0, 0.6),
     'L0_attn_C_bias': (1.0, 0.6),
     'L0_attn_Bn_w': (1.0, 0.6),
     'L0_attn_Cn_w': (1.0, 0.6),
     'L0_attn_D': (1.0, 0.6)}
    factors = {'L0_ffn_Win': 8.0,
     'L0_ffn_bin_': 8.0,
     'L0_ffn_W1': 8.0,
     'L0_ffn_b1': 8.0,
     'L0_ffn_W2': 8.0,
     'L0_ffn_b2': 25.864,
     'L0_ffn_Wout': 8.0,
     'L0_ffn_bout': 200.0}
    for name, (base, spread) in spreads.items():
        noise = np.random.default_rng([zlib.crc32(name.encode()), seed]).standard_normal(out[name].shape)
        drawn = base * np.exp(spread * noise) if base else spread * noise
        out[name] = jnp.asarray(drawn.astype(out[name].dtype))
    for name, factor in factors.items():
        out[name] = (out[name] * factor).astype(out[name].dtype)
    return out
```

```python
from contextlib import ExitStack

import numpy as np

import concourse.bass as bass
from concourse import mybir

F32, F32R, F16, I32 = mybir.dt.float32, mybir.dt.float32r, mybir.dt.float16, mybir.dt.int32
ALU = mybir.AluOpType
ACT = mybir.ActivationFunctionType
AX_X = mybir.AxisListType.X
RMAX = bass.bass_isa.ReduceOp.max

P = 128
NB, T = 4, 128
TOK = NB * T
DM, KD = 512, 4
NH, HD, DS = 32, 32, 64
DI = NH * HD
HG = 4
NG = NH // HG
ROPE = 16
MID, INNER = 64, 16
NF = DS + 2 * ROPE + 1
WCOLS = 2 * DI + 3 * P
C_DTA, C_BC, C_FFN = 2 * DI, 2 * DI + P, 2 * DI + 2 * P
A_FLOOR, EPS = 1e-4, 1e-5
XN_SCALE, W_SCALE = 256.0, 4096.0
MAGIC = 1.5 * 2.0**23
TWO_PI_HI, TWO_PI_LO = 6.28125, 2 * np.pi - 6.28125
SIN_MAX = 3.1415925
A_LEAST = 1e-18

PC = {}
for _name, _n in (("normw", 1), ("dtbias", 1), ("phase", 1), ("onerow", 1), ("eps", 1), ("bin", 1), ("b2", 1),
                  ("W1", INNER), ("b1", INNER), ("W2", INNER), ("D", NG),
                  ("cA_B", 16), ("cB_B", 16), ("cA_C", 16), ("cB_C", 16)):
    PC[_name] = (sum(n for _, n in PC.values()), _n)
N_PCOLS = sum(n for _, n in PC.values())

CC = {}
for _name, _n in (("ident", P), ("dupB", P), ("dupBs", P), ("dupC", P), ("dupCs", P), ("mean", P),
                  ("selcos", P), ("selsin", P), ("ind", NH), ("mmask", DS), ("mone", DS)):
    CC[_name] = (sum(n for _, n in CC.values()), _n)
N_CONST = sum(n for _, n in CC.values())


def constants():
    c = np.zeros((P, N_CONST), np.float32)
    part = {k: c[:, a:a + n] for k, (a, n) in CC.items()}
    part["ident"][:] = np.eye(P)
    for m in range(P):
        n = m % DS
        swap = (n + ROPE) % (2 * ROPE)
        part["dupB"][n, m] = 1
        part["dupC"][DS + n, m] = 1
        part["mean"][m - n:m - n + DS, m] = 1 / DS
        if n < 2 * ROPE:
            part["dupBs"][swap, m] = 1
            part["dupCs"][DS + swap, m] = 1
            part["selsin"][DS + n % ROPE, m] = -1 if n < ROPE else 1
            part["selcos"][DS + ROPE + n % ROPE, m] = 1
    for k in range(2 * NH):
        part["ind"][k, k % NH] = 1
    for i in range(ROPE):
        part["mmask"][DS + i, i] = -1
        part["mmask"][DS + i, ROPE + i] = 1
        part["mmask"][DS + ROPE + i, i] = 1
        part["mmask"][DS + ROPE + i, ROPE + i] = 1
    part["mmask"][NF - 1, 2 * ROPE:] = 1
    part["mone"][:DS] = np.eye(DS)
    return c


class Count:

    def __init__(self, sem, events, unit=1):
        self.sem, self.events, self.unit = sem, events, unit

    def at(self, it, k):
        return it * (self.events * self.unit) + k * self.unit


def mixer(nc, u, w_in, w_out, w_ffn, pcols, bout, mh_bias, consts, scanmask, out, n_iter):
    with ExitStack() as ctx:
        def sb(name, shape, dt=F32):
            return ctx.enter_context(nc.sbuf_tensor(name, shape, dt))

        def sem(name):
            return ctx.enter_context(nc.semaphore(name))

        counts = []

        def count(name, events, unit=1):
            c = Count(sem(name), events, unit)
            counts.append(c)
            return c

        w_hi = sb("w_hi", [P, KD, WCOLS], F16)
        w_lo = sb("w_lo", [P, KD, WCOLS], F16)
        wo = sb("wo", [P, NG, DM])
        wf = sb("wf", [P, DM])
        cst = sb("cst", [P, N_CONST])
        pc = sb("pc", [P, N_PCOLS])
        scan_keep = sb("scan_keep", [NH, TOK])
        bout_bc = sb("bout_bc", [P, DM])
        mh = sb("mh", [NF, NH, DS])
        ind_r = sb("ind_r", [2 * NH, NH], F32R)
        ind_ch = sb("ind_ch", [2 * NH, NH, HD], F32R)
        ones_r = sb("ones_r", [2 * NH, P], F32R)
        scales = sb("scales", [P, 16])
        xn = sb("xn", [P, NB, DM])
        stats = sb("stats", [P, NB, 6])
        mv = sb("mv", [P, NB, 2])
        nt = sb("nt", [P, 5, NB])
        x_hi = sb("x_hi", [P, KD, TOK], F16)
        x_lo = sb("x_lo", [P, KD, TOK], F16)
        cum_r = sb("cum_r", [2 * NH, TOK], F32R)
        ncum_r = sb("ncum_r", [2 * NH, TOK], F32R)
        dend_r = sb("dend_r", [2 * NH, NB, NH], F32R)
        hm = sb("hm", [2 * NH, TOK])
        gw = sb("gw", [P, NB, 2 * NH])
        dec = sb("dec", [P, NB, NH])
        rms_a = sb("rms_a", [P, TOK])
        cosx = sb("cosx", [P, TOK])
        sinx = sb("sinx", [P, TOK])
        bshare = sb("bshare", [P, TOK])
        cshare = sb("cshare", [P, TOK])
        feat = sb("feat", [P, TOK])
        feat_t = sb("feat_t", [P, NB, NF])
        s_mid = sb("s_mid", [P, TOK // 2])
        relu = sb("relu", [P, 2, TOK // 2])
        acc = sb("acc", [P, TOK // 2])
        bh = sb("bh", [P, 2, 2, TOK])
        ch = sb("ch", [P, 2, 2, TOK])
        decay = sb("decay", [P, 2, 2, 2, 2, T])
        x_t = sb("x_t", [P, 2, TOK])
        xs = sb("xs", [P, 2, 2, NB, P])
        sig = sb("sig", [P, TOK])
        gate = sb("gate", [P, 2, TOK])
        ecum = sb("ecum", [P, 2, TOK])
        yc = sb("yc", [P, TOK])
        dx = sb("dx", [P, TOK])
        y = sb("y", [P, NG, TOK])
        fs = sb("fs", [NF, NB, P])
        state = sb("state", [P, NH, NB, HD])
        res = sb("res", [P, 2, DM])

        rms_b = sig
        lt = decay[:, :, :, :, :, :].rearrange("p u j b q t -> p (u j b q t)")
        xb, lg = xn[0:64, 0, :], xn[0:64, 1, :]
        th, kr, kk = xn[64:96, 0, :], xn[64:96, 1, :], xn[64:96, 2, :]
        tr2, gg = xn[0:NH, 2, :], xn[0:NH, 3, :]
        dt_, av, cum, wd = (lt[0:NH, i * TOK:(i + 1) * TOK] for i in range(4))

        banks = [ctx.enter_context(nc.psum_tensor(f"bank{i}", [P, TOK], F32)) for i in range(8)]
        gp0, gp1, dA, dB, cA, cB, y0, y1 = banks
        dbank, cbank, ybank = (dA, dB), (cA, cB), (y0, y1)
        xt_bank = (dA, dB, cA, cB)

        def col(name, i=0, rows=slice(0, P)):
            a, _ = PC[name]
            return pc[rows, a + i:a + i + 1]

        def const(name, rows=slice(0, P)):
            a, n = CC[name]
            return cst[rows, a:a + n]

        ds_col = scales[:, 0:1]
        nds_col = scales[:, 1:2]
        wds_col = scales[:, 2:3]

        loaded, ind_ready, st_zero = sem("loaded"), sem("ind_ready"), sem("st_zero")
        stage_in = [sem(f"stage_in{i}") for i in range(2)]
        absmax_done, allmax_done, scale_done = sem("absmax_done"), sem("allmax_done"), sem("scale_done")
        stage_scaled, hi_done, lo_done, mh_done = sem("stage_scaled"), sem("hi_done"), sem("lo_done"), sem("mh_done")
        u_in = count("u_in", 1, 16)
        bn1, bn2 = count("bn1", NB), count("bn2", NB)
        var_ln, rstd0, newton, normed = count("var_ln", 1), count("rstd0", 1), count("newton", 4), count("normed", NB)
        xt_mm, hi_ok, lo_ok = count("xt_mm", KD), count("hi_ok", KD), count("lo_ok", KD)
        dta_mm, bc_mm, ffn_mm = count("dta_mm", 1), count("bc_mm", 1), count("ffn_mm", 1)
        xb_ok, soft, trap_e, trap = count("xb_ok", 1), count("soft", 3), count("trap_e", 1), count("trap", 4)
        angle, sin_ok = count("angle", 7), count("sin_ok", 1)
        dt_ok, decay_rate, ea_ok, a_ok, lna_ok = count("dt_ok", 2), count("decay_rate", 1), count("ea_ok", 1), count("a_ok", 2), count("lna_ok", 1)
        cum_ok, cum_hi, cum_lo = count("cum_ok", 1), count("cum_hi", 2), count("cum_lo", 2)
        wd_ok, we_ok, gdt_ok, hm_ok, hm_mm, gw_ok = count("wd_ok", 1), count("we_ok", 1), count("gdt_ok", 1), count("hm_ok", 1), count("hm_mm", 1), count("gw_ok", 1)
        dend_ok, dend_mm, dec_ok = count("dend_ok", NB), count("dend_mm", 1), count("dec_ok", 1)
        sq_ok, ms_mm, ms_ln, rms_ok, bcn_ok = count("sq_ok", 1), count("ms_mm", 1), count("ms_ln", 1), count("rms_ok", 1), count("bcn_ok", 1)
        cos_mm, sin_mm, cos_ok, sinx_ok = count("cos_mm", 1), count("sin_mm", 1), count("cos_ok", 1), count("sinx_ok", 1)
        dup_mm, share, top_ok, ft_mm, ft_ok = count("dup_mm", 4), count("share", 6), count("top_ok", 1), count("ft_mm", 1), count("ft_ok", 1)
        s_ok, relu_ok, acc_ok = count("s_ok", 2), count("relu_ok", INNER), count("acc_ok", INNER)
        x_mm, z_mm, xt_ok, tr_mm, xs_ok = count("x_mm", NG), count("z_mm", NG), count("xt_ok", NG), count("tr_mm", NG), count("xs_ok", 2 * NG)
        sig_ok, gate_ok = count("sig_ok", 3 * NG), count("gate_ok", NG)
        h1_ok, h2_ok = count("h1_ok", 4 * NG), count("h2_ok", 4 * NG)
        diff_mm, cb_mm, exp_ok, mask_ok, s_mul = count("diff_mm", 2 * NG), count("cb_mm", 2 * NG), count("exp_ok", 2 * NG), count("mask_ok", 2 * NG), count("s_mul", 2 * NG)
        pool_step, dve_step, sp_step = sem("pool_step"), sem("dve_step"), sem("sp_step")
        y_mm, t1_ok, yc_ok = count("y_mm", 2 * NG), count("t1_ok", 2 * NG), count("yc_ok", 2 * NG)
        e_mm, e_ok = count("e_mm", NG), count("e_ok", NG)
        dx_ok, ysum_ok, y_ok = count("dx_ok", NG), count("ysum_ok", NG), count("y_ok", NG)
        f_mm, fs_ok, h_mm, faded, state_ok = count("f_mm", NG), count("fs_ok", NG), count("h_mm", NG), count("faded", NG), count("state_ok", 2 * NG)
        out_mm, res_ok, out_ok = count("out_mm", NB), count("res_ok", NB), count("out_ok", NB)
        res_in = [count(f"res_in{i}", 2, 16) for i in range(2)]
        stored = [count(f"stored{i}", 2, 16) for i in range(2)]

        def wait(eng, c, it, k):
            eng.wait_ge(c.sem, c.at(it, k))

        def loop(eng, main, tail):
            tail(0, False, True)
            if n_iter > 1:
                with eng.Fori(1, n_iter) as it:
                    main(it, True)
                    tail(it, True, True)
            main(n_iter, False)
            tail(n_iter, True, False)

        u_chunk = u.rearrange("b (c t) d -> c t b d", t=T)
        out_chunk = out.rearrange("b (c t) d -> c t b d", t=T)
        w_in_k = w_in.rearrange("(k p) n -> k p n", p=P)
        n_loads = 9
        stage = [y[:, :, :].rearrange("p g t -> p (g t)")[:, 0:WCOLS],
                 state[:, :, :, :].rearrange("p h b d -> p (h b d)")[:, 0:WCOLS]]
        stage_blocks = [0, 1, 2, 3, 0, 1]
        split_blocks = [(2, 0), (3, 1), (0, 0), (1, 1)]

        block = ctx.enter_context(nc.Block())

        @block.sync
        def _(sp):
            for c in counts:
                sp.sem_inc(c.sem, c.events * c.unit)
            for i, k in enumerate(stage_blocks[:2]):
                sp.dma_start(stage[i], w_in_k[k]).then_inc(stage_in[i % 2], 16)
            sp.dma_start(cst[:, :], consts).then_inc(loaded, 16)
            sp.dma_start(pc[:, :], pcols).then_inc(loaded, 16)
            sp.dma_start(scan_keep[:, :], scanmask).then_inc(loaded, 16)
            sp.dma_start(bout_bc[:, :], bout.broadcast_to([P, DM])).then_inc(loaded, 16)
            sp.dma_start(mh[DS:DS + ROPE, :, :], mh_bias[0:1].broadcast_to([ROPE, NH, DS])).then_inc(loaded, 16)
            sp.dma_start(mh[DS + ROPE:NF, :, :], mh_bias[1:2].broadcast_to([ROPE + 1, NH, DS])).then_inc(loaded, 16)
            sp.dma_start(mh[0:DS, :, :], mh_bias[1:2].broadcast_to([DS, NH, DS])).then_inc(loaded, 16)
            sp.dma_start(wo[:, :, :], w_out.rearrange("(k p) n -> p k n", p=P)).then_inc(loaded, 16)
            sp.dma_start(wf[:, :], w_ffn).then_inc(loaded, 16)
            for i, k in enumerate(stage_blocks):
                if 2 <= i < 4:
                    sp.wait_ge(absmax_done, i - 1)
                    sp.dma_start(stage[i % 2], w_in_k[k]).then_inc(stage_in[i % 2], 16)
                if i >= 4:
                    sp.wait_ge(lo_done, i - 3)
                    sp.dma_start(stage[i % 2], w_in_k[k]).then_inc(stage_in[i % 2], 16)

            def sp_wait(c, it, k):
                wait(sp, c, it, k)
                sp.sem_inc(sp_step, 1)

            def load_u(n):
                sp_wait(normed, n - 1, NB)
                sp_wait(xt_mm, n - 1, KD)
                sp_wait(gdt_ok, n - 1, 1)
                sp_wait(a_ok, n - 1, 2)
                sp_wait(sin_ok, n - 1, 1)
                sp.dma_start(xn[:, :, :], u_chunk[n - 1]).then_inc(u_in.sem, 16)

            def main(it, pre):
                if pre:
                    load_u(it + 1)
                for b in range(2):
                    sp_wait(stored[b], it, 0)
                    sp.dma_start(res[:, b, :], u_chunk[it - 1, :, b, :]).then_inc(res_in[b].sem, 16)

            def tail(it, outs, pre):
                if not outs:
                    load_u(1)
                    return
                for b in range(NB):
                    sp_wait(out_ok, it, b + 1)
                    sp.dma_start(out_chunk[it - 1, :, b, :], res[:, b % 2, :]).then_inc(stored[b % 2].sem, 16)
                    if b < 2:
                        sp_wait(stored[b], it, 1)
                        sp.dma_start(res[:, b, :], u_chunk[it - 1, :, b + 2, :]).then_inc(res_in[b].sem, 16)

            loop(sp, main, tail)
            for b in range(2):
                sp_wait(stored[b], n_iter, 2)

        @block.gpsimd
        def _(pool):
            pool.wait_ge(absmax_done, KD)
            pool.wait_ge(scale_done, 1)
            nc.gpsimd.partition_all_reduce(scales[:, 9:10], scales[:, 8:9], P, RMAX).then_inc(allmax_done, 1)
            pool.wait_ge(lo_done, KD)
            nc.gpsimd.memset(state[:, :, :, :], 0.0).then_inc(st_zero, 1)

            def mask(it, n):
                wait(pool, exp_ok, it, n)
                pool.sem_inc(pool_step, 1)
                v = decay[:, (n - 1) % 2].rearrange("p j b q t -> p (j b q) t")
                nc.gpsimd.affine_select(out=v, in_=v, compare_op=ALU.is_ge, fill=0.0, base=0,
                                        pattern=[[0, 8], [1, T]], channel_multiplier=-1).then_inc(mask_ok.sem, 1)

            def finish(it, g):
                wait(pool, xt_ok, it, g + 1)
                wait(pool, y_ok, it, g)
                pool.sem_inc(pool_step, 1)
                nc.gpsimd.tensor_scalar(dx[:, :], x_t[:, g % 2, :], col("D", g), None, ALU.mult).then_inc(dx_ok.sem, 1)
                wait(pool, dx_ok, it, g + 1)
                wait(pool, yc_ok, it, 2 * g + 2)
                nc.gpsimd.tensor_tensor(dx[:, :], dx[:, :], yc[:, :], ALU.add).then_inc(ysum_ok.sem, 1)
                wait(pool, ysum_ok, it, g + 1)
                wait(pool, gate_ok, it, g + 1)
                wait(pool, out_mm, it, 0)
                nc.gpsimd.tensor_tensor(y[:, g, :], dx[:, :], gate[:, g % 2, :], ALU.mult).then_inc(y_ok.sem, 1)

            def main(it, pre):
                for g in range(NG):
                    mask(it, 2 * g + 1)
                    if g:
                        finish(it, g - 1)
                    mask(it, 2 * g + 2)
                    wait(pool, y_mm, it, 2 * g + 2)
                    wait(pool, dec_ok, it, 1)
                    wait(pool, state_ok, it, 2 * (g + 1) - 2 * NG)
                    s = state[:, g * HG:(g + 1) * HG]
                    d = dec[:, :, g * HG:(g + 1) * HG].rearrange("p b h -> p h b").unsqueeze(3).broadcast_to([P, HG, NB, HD])
                    nc.gpsimd.tensor_tensor(s, s, d, ALU.mult).then_inc(faded.sem, 1)
                finish(it, NG - 1)

            def tail(it, outs, pre):
                if not outs:
                    pool.wait_ge(st_zero, 1)
                    return
                for b in range(NB):
                    wait(pool, res_in[b % 2], it, b // 2 + 1)
                    nc.gpsimd.tensor_tensor(res[:, b % 2, :], res[:, b % 2, :], bout_bc[:, :], ALU.add).then_inc(res_ok.sem, 1)

            pool.wait_ge(loaded, 16 * n_loads)
            loop(pool, main, tail)

        @block.scalar
        def _(act):
            nc.scalar.preload_act_table_set("natural_log_exp_and_others")
            act.wait_ge(loaded, 16 * n_loads)
            for i, (k, s) in enumerate(split_blocks):
                act.wait_ge(stage_scaled, i + 1)
                nc.scalar.activation(w_hi[:, k, :], stage[s], ACT.Copy).then_inc(hi_done, 1)

            def norm(n):
                wait(act, bn2, n, NB)
                nc.scalar.activation(nt[:, 0, :], mv[:, :, 1], ACT.Ln, bias=col("eps")).then_inc(var_ln.sem, 1)
                wait(act, var_ln, n, 1)
                wait(act, normed, n - 1, NB)
                nc.scalar.activation(nt[:, 1, :], nt[:, 0, :], ACT.Exp, scale=-0.5).then_inc(rstd0.sem, 1)

            def exp_diff(it, n):
                wait(act, diff_mm, it, n)
                wait(act, y_mm, it, n - 2)
                v = decay[:, (n - 1) % 2]
                for j in range(2):
                    e = nc.scalar.activation(v[:, j], dbank[j][:, :].rearrange("p (b q t) -> p b q t", b=2, q=2), ACT.Exp)
                e.then_inc(exp_ok.sem, 1)

            def x_out(it, g):
                wait(act, x_mm, it, g + 1)
                wait(act, dx_ok, it, g - 1)
                wait(act, tr_mm, it, g - 1)
                nc.scalar.activation(x_t[:, g % 2, :], gp0[:, :], ACT.Copy, scale=ds_col).then_inc(xt_ok.sem, 1)

            def sigmoid(it, g):
                wait(act, z_mm, it, g + 1)
                wait(act, gate_ok, it, g)
                nc.scalar.activation(sig[:, :], gp1[:, :], ACT.Exp, scale=nds_col).then_inc(sig_ok.sem, 1)
                wait(act, sig_ok, it, 3 * g + 1)
                nc.scalar.activation(sig[:, :], sig[:, :], ACT.Ln, bias=1.0).then_inc(sig_ok.sem, 1)
                wait(act, sig_ok, it, 3 * g + 2)
                nc.scalar.activation(sig[:, :], sig[:, :], ACT.Exp, scale=-1.0).then_inc(sig_ok.sem, 1)

            def e_out(it, g):
                wait(act, e_mm, it, g + 1)
                wait(act, yc_ok, it, 2 * g - 2)
                nc.scalar.activation(ecum[:, g % 2, :], cA[:, :], ACT.Exp).then_inc(e_ok.sem, 1)

            def hidden(it, j):
                wait(act, s_ok, it, 2)
                wait(act, acc_ok, it, j - 1)
                nc.scalar.activation(relu[:, j % 2, :], s_mid[:, :], ACT.Relu, bias=col("b1", j),
                                     scale=col("W1", j)).then_inc(relu_ok.sem, 1)

            def main(it, pre):
                for g in range(NG):
                    exp_diff(it, 2 * g + 1)
                    if g + 1 < NG:
                        x_out(it, g + 1)
                    exp_diff(it, 2 * g + 2)
                    hidden(it, 2 * g)
                    hidden(it, 2 * g + 1)
                    if g + 1 < NG:
                        sigmoid(it, g + 1)
                    if g == NG - 2 and pre:
                        norm(it + 1)
                    wait(act, f_mm, it, g + 1)
                    wait(act, h_mm, it, g)
                    nc.scalar.activation(fs[:, :, :], gp0[0:NF, :].rearrange("p (b c) -> p b c", b=NB),
                                         ACT.Copy).then_inc(fs_ok.sem, 1)
                    if g + 1 < NG:
                        e_out(it, g + 1)

            def tail(it, outs, pre):
                n = it + 1
                if not pre:
                    return
                if not outs:
                    norm(n)
                wait(act, z_mm, it, NG)
                for k in range(KD):
                    wait(act, xt_mm, n, k + 1)
                    nc.scalar.activation(x_hi[:, k, :], xt_bank[k][:, :], ACT.Copy).then_inc(hi_ok.sem, 1)
                wait(act, dta_mm, n, 1)
                wait(act, xt_mm, n, KD)
                nc.scalar.activation(xb, gp0[0:64, :], ACT.Identity, bias=col("dtbias", 0, slice(0, 64)),
                                     scale=scales[0:64, 0:1]).then_inc(xb_ok.sem, 1)
                wait(act, xb_ok, n, 1)
                nc.scalar.activation(lg, xb, ACT.Abs).then_inc(soft.sem, 1)
                wait(act, soft, n, 1)
                nc.scalar.activation(lg, lg, ACT.Exp, scale=-1.0).then_inc(soft.sem, 1)
                wait(act, soft, n, 2)
                nc.scalar.activation(lg, lg, ACT.Ln, bias=1.0).then_inc(soft.sem, 1)
                nc.scalar.activation(tr2, gp0[64:96, :], ACT.Exp, scale=scales[64:96, 1:2]).then_inc(trap_e.sem, 1)
                wait(act, bc_mm, n, 1)
                wait(act, bcn_ok, n - 1, 1)
                wait(act, dup_mm, n - 1, 4)
                nc.scalar.activation(rms_a[:, :], gp1[:, :], ACT.Square, scale=ds_col).then_inc(sq_ok.sem, 1)
                wait(act, ffn_mm, n, 1)
                wait(act, relu_ok, it, INNER)
                for h in range(2):
                    r = slice(MID * h, MID * h + MID)
                    nc.scalar.activation(s_mid[r, :], dA[r, h * 256:h * 256 + 256], ACT.Identity,
                                         bias=col("bin", 0, r), scale=scales[r, 0:1]).then_inc(s_ok.sem, 1)
                wait(act, angle, n, 7)
                wait(act, ft_mm, n - 1, 1)
                wait(act, sin_mm, n - 1, 1)
                nc.scalar.activation(feat[DS:DS + 2 * ROPE, :], th, ACT.Sin).then_inc(sin_ok.sem, 1)
                nc.scalar.preload_act_table_set("natural_log_exp_and_others")
                wait(act, decay_rate, n, 1)
                nc.scalar.activation(av, av, ACT.Exp, scale=-1.0).then_inc(ea_ok.sem, 1)
                wait(act, a_ok, n, 2)
                nc.scalar.activation(av, av, ACT.Ln).then_inc(lna_ok.sem, 1)
                wait(act, cum_ok, n, 1)
                wait(act, diff_mm, it, 2 * NG)
                wait(act, e_mm, it, NG)
                wait(act, dend_ok, it, NB)
                nc.scalar.activation(cum_r[0:NH, :], cum, ACT.Copy).then_inc(cum_hi.sem, 1)
                nc.scalar.activation(ncum_r[0:NH, :], cum, ACT.Copy, scale=-1.0).then_inc(cum_hi.sem, 1)
                wait(act, wd_ok, n, 1)
                nc.scalar.activation(wd, wd, ACT.Exp).then_inc(we_ok.sem, 1)
                wait(act, ms_mm, n, 1)
                wait(act, gate_ok, it, NG)
                nc.scalar.activation(rms_b[:, :], dB[:, :], ACT.Ln, bias=col("eps")).then_inc(ms_ln.sem, 1)
                wait(act, ms_ln, n, 1)
                nc.scalar.activation(rms_b[:, :], rms_b[:, :], ACT.Exp, scale=-0.5).then_inc(rms_ok.sem, 1)
                wait(act, cos_mm, n, 1)
                wait(act, h2_ok, it, 4 * NG)
                nc.scalar.activation(cosx[:, :], gp0[:, :], ACT.Identity, bias=col("onerow")).then_inc(cos_ok.sem, 1)
                wait(act, sin_mm, n, 1)
                nc.scalar.activation(sinx[:, :], gp1[:, :], ACT.Copy).then_inc(sinx_ok.sem, 1)
                wait(act, hm_mm, n, 1)
                wait(act, xs_ok, it, 2 * NG)
                nc.scalar.activation(gw[:, :, :], gp0[:, 0:NB * 2 * NH].rearrange("p (b h) -> p b h", b=NB),
                                     ACT.Copy).then_inc(gw_ok.sem, 1)
                wait(act, dend_mm, n, 1)
                wait(act, faded, it, NG)
                nc.scalar.activation(dec[:, :, :], gp1[:, 0:NB * NH].rearrange("p (b h) -> p b h", b=NB),
                                     ACT.Exp).then_inc(dec_ok.sem, 1)
                wait(act, share, n, 3)
                nc.scalar.activation(feat[0:DS, :], bshare[0:DS, :], ACT.Copy).then_inc(top_ok.sem, 1)
                wait(act, ft_mm, n, 1)
                wait(act, f_mm, it, NG)
                nc.scalar.activation(feat_t[:, :, :], dB[:, 0:NB * NF].rearrange("p (b f) -> p b f", b=NB),
                                     ACT.Copy).then_inc(ft_ok.sem, 1)
                x_out(n, 0)
                wait(act, share, n, 6)
                sigmoid(n, 0)
                e_out(n, 0)

            loop(act, main, tail)

        @block.vector
        def _(dve):
            dve.wait_ge(loaded, 16 * n_loads)
            nc.vector.tensor_tensor(mh[:, :, :], mh[:, :, :], const("mmask", slice(0, NF)).unsqueeze(1).broadcast_to([NF, NH, DS]),
                                    ALU.mult).then_inc(mh_done, 1)
            dve.wait_ge(mh_done, 1)
            nc.vector.tensor_tensor(mh[:, :, :], mh[:, :, :], const("mone", slice(0, NF)).unsqueeze(1).broadcast_to([NF, NH, DS]),
                                    ALU.add).then_inc(mh_done, 1)
            nc.vector.tensor_copy(ind_r[:, :], const("ind", slice(0, 64))).then_inc(ind_ready, 1)
            nc.vector.tensor_copy(ind_ch[:, :, :], const("ind", slice(0, 64)).unsqueeze(2).broadcast_to([64, NH, HD])).then_inc(ind_ready, 1)
            nc.vector.tensor_scalar(ones_r[:, :], const("ident", slice(0, 64)), 0.0, 1.0, ALU.mult, ALU.add).then_inc(ind_ready, 1)
            nc.vector.memset(feat[96:128, :], 1.0).then_inc(ind_ready, 1)
            for i in range(KD):
                dve.wait_ge(stage_in[i % 2], 16 * (i // 2 + 1))
                nc.vector.tensor_reduce(scales[:, 4 + i:5 + i], stage[i % 2], AX_X, ALU.max,
                                        apply_absolute_value=True).then_inc(absmax_done, 1)
            dve.wait_ge(absmax_done, KD)
            nc.vector.tensor_reduce(scales[:, 8:9], scales[:, 4:8], AX_X, ALU.max).then_inc(scale_done, 1)
            dve.wait_ge(allmax_done, 1)
            nc.vector.tensor_scalar(scales[:, 10:11].bitcast(I32), scales[:, 9:10].bitcast(I32), 0x7F800000, None,
                                    ALU.bitwise_and).then_inc(scale_done, 1)
            dve.wait_ge(scale_done, 2)
            nc.vector.tensor_scalar(scales[:, 11:12].bitcast(I32), scales[:, 10:11].bitcast(I32), -1.0, float(254 << 23),
                                    ALU.mult, ALU.add).then_inc(scale_done, 1)
            undo = 1.0 / (XN_SCALE * W_SCALE)
            nc.vector.tensor_scalar(ds_col, scales[:, 10:11], undo, None, ALU.mult).then_inc(scale_done, 1)
            nc.vector.tensor_scalar(nds_col, scales[:, 10:11], -undo, None, ALU.mult).then_inc(scale_done, 1)
            nc.vector.tensor_scalar(wds_col, scales[:, 10:11], undo, col("normw"), ALU.mult, ALU.mult).then_inc(scale_done, 1)
            dve.wait_ge(scale_done, 6)
            for i, (k, s) in enumerate(split_blocks):
                dve.wait_ge(stage_in[s], 16 * (i // 2 + 2))
                nc.vector.tensor_scalar(stage[s], stage[s], scales[:, 11:12], W_SCALE, ALU.mult, ALU.mult).then_inc(stage_scaled, 1)
                dve.wait_ge(hi_done, i + 1)
                nc.vector.tensor_tensor(w_lo[:, k, :], stage[s], w_hi[:, k, :], ALU.subtract).then_inc(lo_done, 1)

            def norm(n):
                wait(dve, u_in, n, 1)
                for b in range(NB):
                    nc.vector.bn_stats(stats[:, b, :], xn[:, b, :]).then_inc(bn1.sem, 1)
                for b in range(NB):
                    wait(dve, bn1, n, b + 1)
                    dve.sem_inc(dve_step, 1)
                    nc.vector.bn_aggr(mv[:, b, :], stats[:, b, :]).then_inc(bn2.sem, 1)
                wait(dve, rstd0, n, 1)
                nc.vector.tensor_tensor(nt[:, 2, :], nt[:, 1, :], nt[:, 1, :], ALU.mult).then_inc(newton.sem, 1)
                wait(dve, newton, n, 1)
                nc.vector.scalar_tensor_tensor(out=nt[:, 3, :], in0=mv[:, :, 1], scalar=col("eps"), in1=nt[:, 2, :],
                                               op0=ALU.add, op1=ALU.mult).then_inc(newton.sem, 1)
                wait(dve, newton, n, 2)
                nc.vector.tensor_scalar(nt[:, 4, :], nt[:, 3, :], -0.5 * XN_SCALE, 1.5 * XN_SCALE, ALU.mult, ALU.add).then_inc(newton.sem, 1)
                wait(dve, newton, n, 3)
                nc.vector.tensor_tensor(nt[:, 0, :], nt[:, 4, :], nt[:, 1, :], ALU.mult).then_inc(newton.sem, 1)
                wait(dve, newton, n, 4)
                for b in range(NB):
                    nc.vector.tensor_scalar(xn[:, b, :], xn[:, b, :], mv[:, b, 0:1], nt[:, 0, b:b + 1],
                                            ALU.subtract, ALU.mult).then_inc(normed.sem, 1)

            def heads(it, g, q):
                slot, pair = g % 2, 2 * g + q
                if q == 0:
                    wait(dve, y_mm, it, 2 * g - 2)
                for which, (dst, base, ca, cb) in enumerate(((bh, bshare, "cA_B", "cB_B"), (ch, cshare, "cA_C", "cB_C"))):
                    k = 4 * g + 2 * q + which + 1
                    nc.vector.scalar_tensor_tensor(out=dst[:, slot, q, :], in0=cosx[:, :], scalar=col(ca, pair),
                                                   in1=base[:, :], op0=ALU.mult, op1=ALU.add).then_inc(h1_ok.sem, 1)
                    wait(dve, h1_ok, it, k)
                    nc.vector.scalar_tensor_tensor(out=dst[:, slot, q, :], in0=sinx[:, :], scalar=col(cb, pair),
                                                   in1=dst[:, slot, q, :], op0=ALU.mult, op1=ALU.add).then_inc(h2_ok.sem, 1)

            def scale_x(it, g):
                wait(dve, tr_mm, it, g + 1)
                wait(dve, f_mm, it, g - 1)
                wait(dve, gw_ok, it, 1)
                src = gp0[:, :].rearrange("p (b h d) -> p b h d", b=NB, h=HG)
                for i in range(2):
                    w = gw[:, :, i * NH + g * HG:i * NH + (g + 1) * HG].unsqueeze(3).broadcast_to([P, NB, HG, HD])
                    nc.vector.tensor_tensor(xs[:, g % 2, i].rearrange("p b (h d) -> p b h d", h=HG), src, w,
                                            ALU.mult).then_inc(xs_ok.sem, 1)

            def silu(it, g):
                wait(dve, sig_ok, it, 3 * g + 3)
                wait(dve, y_ok, it, g - 1)
                nc.vector.scalar_tensor_tensor(out=gate[:, g % 2, :], in0=gp1[:, :], scalar=ds_col, in1=sig[:, :],
                                               op0=ALU.mult, op1=ALU.mult).then_inc(gate_ok.sem, 1)

            def scores(it, n):
                wait(dve, cb_mm, it, n)
                wait(dve, mask_ok, it, n)
                for j in range(2):
                    v = decay[:, (n - 1) % 2, j].rearrange("p b q t -> p (b q t)")
                    m = nc.vector.tensor_tensor(v, cbank[j][:, :], v, ALU.mult)
                m.then_inc(s_mul.sem, 1)

            def combine(it, g, i):
                n = 2 * g + i + 1
                half = slice(i * 256, i * 256 + 256)
                wait(dve, y_mm, it, n)
                wait(dve, e_ok, it, g + 1)
                if i == 0:
                    wait(dve, ysum_ok, it, g)
                nc.vector.tensor_tensor(yc[:, half], ybank[i][:, 256:512], ecum[:, g % 2, half], ALU.mult).then_inc(t1_ok.sem, 1)
                wait(dve, t1_ok, it, n)
                nc.vector.tensor_tensor(yc[:, half], ybank[i][:, 0:256], yc[:, half], ALU.add).then_inc(yc_ok.sem, 1)

            def update_state(it, g):
                wait(dve, h_mm, it, g + 1)
                wait(dve, faded, it, g + 1)
                for j in range(2):
                    r = slice(DS * j, DS * j + DS)
                    s = state[r, g * HG + j:(g + 1) * HG:2].rearrange("p q b d -> p q (b d)")
                    nc.vector.tensor_tensor(s, gp1[r, 0:256].rearrange("p (q c) -> p q c", q=2), s,
                                            ALU.add).then_inc(state_ok.sem, 1)

            def hidden(it, j):
                wait(dve, relu_ok, it, j + 1)
                if j == 0:
                    wait(dve, out_mm, it, 0)
                    nc.vector.tensor_scalar(acc[:, :], relu[:, 0, :], col("W2", 0), col("b2"), ALU.mult, ALU.add).then_inc(acc_ok.sem, 1)
                else:
                    wait(dve, acc_ok, it, j)
                    nc.vector.scalar_tensor_tensor(out=acc[:, :], in0=relu[:, j % 2, :], scalar=col("W2", j), in1=acc[:, :],
                                                   op0=ALU.mult, op1=ALU.add).then_inc(acc_ok.sem, 1)

            def main(it, pre):
                for g in range(NG):
                    scores(it, 2 * g + 1)
                    if g:
                        update_state(it, g - 1)
                    if g + 1 < NG:
                        heads(it, g + 1, 0)
                    scores(it, 2 * g + 2)
                    combine(it, g, 0)
                    if g + 1 < NG:
                        scale_x(it, g + 1)
                        heads(it, g + 1, 1)
                        silu(it, g + 1)
                    hidden(it, 2 * g)
                    hidden(it, 2 * g + 1)
                    if g == NG - 2 and pre:
                        norm(it + 1)
                    combine(it, g, 1)

            def out_sum(it, b):
                wait(dve, out_mm, it, b + 1)
                wait(dve, res_ok, it, b + 1)
                nc.vector.tensor_tensor(res[:, b % 2, :], ybank[b % 2][:, :], res[:, b % 2, :], ALU.add).then_inc(out_ok.sem, 1)

            def tail(it, outs, pre):
                n = it + 1
                if outs and not pre:
                    update_state(it, NG - 1)
                    for b in range(NB):
                        out_sum(it, b)
                    return
                if not outs:
                    norm(n)
                for k in range(KD):
                    wait(dve, hi_ok, n, k + 1)
                    nc.vector.tensor_tensor(x_lo[:, k, :], xt_bank[k][:, :], x_hi[:, k, :], ALU.subtract).then_inc(lo_ok.sem, 1)
                if outs:
                    update_state(it, NG - 1)
                wait(dve, dta_mm, n, 1)
                nc.vector.tensor_scalar(th, gp0[96:128, :], scales[96:128, 0:1], col("phase", 0, slice(96, 128)),
                                        ALU.mult, ALU.add).then_inc(angle.sem, 1)
                wait(dve, angle, n, 1)
                nc.vector.tensor_scalar(kr, th, 1 / (2 * np.pi), MAGIC, ALU.mult, ALU.add).then_inc(angle.sem, 1)
                wait(dve, angle, n, 2)
                nc.vector.tensor_scalar(kk, kr, MAGIC, -TWO_PI_HI, ALU.subtract, ALU.mult).then_inc(angle.sem, 1)
                wait(dve, angle, n, 3)
                nc.vector.tensor_tensor(th, th, kk, ALU.add).then_inc(angle.sem, 1)
                nc.vector.tensor_scalar(kr, kr, MAGIC, -TWO_PI_LO, ALU.subtract, ALU.mult).then_inc(angle.sem, 1)
                wait(dve, angle, n, 5)
                nc.vector.tensor_tensor(th, th, kr, ALU.add).then_inc(angle.sem, 1)
                wait(dve, angle, n, 6)
                nc.vector.tensor_scalar(th, th, SIN_MAX, -SIN_MAX, ALU.min, ALU.max).then_inc(angle.sem, 1)
                wait(dve, soft, n, 3)
                wait(dve, y_mm, it, 2 * NG)
                nc.vector.scalar_tensor_tensor(out=dt_, in0=xb[0:NH], scalar=0.0, in1=lg[0:NH], op0=ALU.max,
                                               op1=ALU.add).then_inc(dt_ok.sem, 1)
                nc.vector.scalar_tensor_tensor(out=av, in0=xb[NH:64], scalar=0.0, in1=lg[NH:64], op0=ALU.max,
                                               op1=ALU.add).then_inc(dt_ok.sem, 1)
                wait(dve, dt_ok, n, 2)
                nc.vector.scalar_tensor_tensor(out=av, in0=av, scalar=A_FLOOR, in1=dt_, op0=ALU.max,
                                               op1=ALU.mult).then_inc(decay_rate.sem, 1)
                wait(dve, trap_e, n, 1)
                nc.vector.tensor_scalar(tr2, tr2, 1.0, None, ALU.add).then_inc(trap.sem, 1)
                wait(dve, trap, n, 1)
                nc.vector.reciprocal(tr2, tr2).then_inc(trap.sem, 1)
                wait(dve, trap, n, 2)
                nc.vector.tensor_scalar(gg, tr2, -0.5, 1.0, ALU.mult, ALU.add).then_inc(trap.sem, 1)
                nc.vector.tensor_scalar(tr2, tr2, 0.5, A_LEAST, ALU.mult, ALU.max).then_inc(trap.sem, 1)
                wait(dve, trap, n, 4)
                wait(dve, hm_mm, it, 1)
                nc.vector.tensor_tensor(hm[0:NH, :], gg, dt_, ALU.mult).then_inc(gdt_ok.sem, 1)
                wait(dve, ea_ok, n, 1)
                nc.vector.tensor_tensor(av, av, gg, ALU.mult).then_inc(a_ok.sem, 1)
                wait(dve, a_ok, n, 1)
                nc.vector.tensor_tensor(av, av, tr2, ALU.add).then_inc(a_ok.sem, 1)
                wait(dve, lna_ok, n, 1)
                nc.vector.tensor_tensor_scan(cum, scan_keep[:, :], av, 0.0, ALU.mult, ALU.add).then_inc(cum_ok.sem, 1)
                wait(dve, cum_hi, n, 2)
                nc.vector.tensor_tensor(cum_r[NH:64, :], cum, cum_r[0:NH, :].bitcast(F32), ALU.subtract).then_inc(cum_lo.sem, 1)
                nc.vector.tensor_tensor(ncum_r[NH:64, :], cum_r[0:NH, :].bitcast(F32), cum, ALU.subtract).then_inc(cum_lo.sem, 1)
                cum_b = cum.rearrange("p (b t) -> p b t", b=NB)
                nc.vector.tensor_tensor(wd.rearrange("p (b t) -> p b t", b=NB), cum_b[:, :, T - 1:T].broadcast_to([NH, NB, T]),
                                        cum_b, ALU.subtract).then_inc(wd_ok.sem, 1)
                wait(dve, cum_lo, n, 2)
                wait(dve, dend_mm, it, 1)
                for b in range(NB):
                    nc.vector.tensor_scalar(dend_r[:, b, :], ind_r[:, :].bitcast(F32),
                                            cum_r[:, (b + 1) * T - 1:(b + 1) * T].bitcast(F32), None, ALU.mult).then_inc(dend_ok.sem, 1)
                wait(dve, we_ok, n, 1)
                wait(dve, gdt_ok, n, 1)
                nc.vector.tensor_tensor(hm[NH:64, :], wd, hm[0:NH, :], ALU.mult).then_inc(hm_ok.sem, 1)
                if outs:
                    out_sum(it, 0)
                wait(dve, rms_ok, n, 1)
                nc.vector.scalar_tensor_tensor(out=rms_a[:, :], in0=gp1[:, :], scalar=wds_col, in1=rms_b[:, :],
                                               op0=ALU.mult, op1=ALU.mult).then_inc(bcn_ok.sem, 1)
                if outs:
                    out_sum(it, 1)
                for k, (straight, swapped, dst) in enumerate(((dB, cA, bshare), (cB, dA, cshare))):
                    wait(dve, sinx_ok, n, 1)
                    wait(dve, cos_ok, n, 1)
                    wait(dve, dup_mm, n, 2 * k + 2)
                    if k:
                        wait(dve, share, n, 3)
                    nc.vector.tensor_tensor(dst[:, :], swapped[:, :], sinx[:, :], ALU.mult).then_inc(share.sem, 1)
                    nc.vector.tensor_tensor(rms_b[:, :], straight[:, :], cosx[:, :], ALU.mult).then_inc(share.sem, 1)
                    wait(dve, share, n, 3 * k + 2)
                    nc.vector.tensor_tensor(dst[:, :], dst[:, :], rms_b[:, :], ALU.add).then_inc(share.sem, 1)
                wait(dve, share, n, 6)
                heads(n, 0, 0)
                heads(n, 0, 1)
                if outs:
                    out_sum(it, 2)
                    out_sum(it, 3)
                silu(n, 0)
                scale_x(n, 0)

            loop(dve, main, tail)

        @block.tensor
        def _(pe):
            mm = nc.tensor.matmul

            def project(bank, c0):
                for k in range(KD):
                    for i, (w, x) in enumerate(((w_hi, x_hi), (w_hi, x_lo), (w_lo, x_hi))):
                        m = mm(bank[:, :], w[:, k, c0:c0 + P], x[:, k, :], start=(k == 0 and i == 0),
                               stop=(k == KD - 1 and i == 2))
                return m

            def diff(it, n):
                g, i = (n - 1) // 2, (n - 1) % 2
                if g == 0 and i == 0:
                    wait(pe, cum_lo, it, 2)
                    wait(pe, share, it, 6)
                    wait(pe, ft_ok, it, 1)
                wait(pe, exp_ok, it, n - 1)
                for j in range(2):
                    for b in range(2):
                        tok = (2 * i + b) * T
                        dst = dbank[j][:, b * 256:b * 256 + 256]
                        mm(dst, ncum_r[:, tok:tok + T],
                           ind_r[:, g * HG + j:(g + 1) * HG:2].unsqueeze(2).broadcast_to([64, 2, T]),
                           start=True, stop=False, skip_group_check=True)
                        for q in range(2):
                            h = g * HG + 2 * q + j
                            m = mm(dst[:, q * T:q * T + T], ind_r[:, h:h + 1].broadcast_to([64, P]), cum_r[:, tok:tok + T],
                                   start=False, stop=(q == 1), skip_group_check=True)
                m.then_inc(diff_mm.sem, 1)

            def products(it, n):
                g, i = (n - 1) // 2, (n - 1) % 2
                wait(pe, s_mul, it, n - 1)
                if i == 0:
                    wait(pe, e_ok, it, g + 1)
                    wait(pe, h2_ok, it, 4 * g + 4)
                for b in range(2):
                    for q in range(2):
                        for j in range(2):
                            r = slice(DS * j, DS * j + DS)
                            tok = (2 * i + b) * T
                            m = mm(cbank[j][:, (2 * b + q) * T:(2 * b + q + 1) * T], bh[r, g % 2, q, tok:tok + T],
                                   ch[r, g % 2, q, tok:tok + T], start=True, stop=True, skip_group_check=True)
                m.then_inc(cb_mm.sem, 1)

            def outputs(it, n):
                g, i = (n - 1) // 2, (n - 1) % 2
                wait(pe, s_mul, it, n)
                if g == 0:
                    wait(pe, out_ok, it, i - 1)
                else:
                    wait(pe, yc_ok, it, n - 2)
                wait(pe, xs_ok, it, 2 * g + 1)
                wait(pe, state_ok, it, 2 * (g + 1) - 2 * NG)
                for b in range(2):
                    for h in range(HG):
                        q, j = h // 2, h % 2
                        tok = 2 * i + b
                        rows = slice(HD * h, HD * h + HD)
                        mm(ybank[i][rows, 256 + b * T:256 + (b + 1) * T], state[:, g * HG + h, tok, :],
                           ch[:, g % 2, q, tok * T:(tok + 1) * T], start=True, stop=True, skip_group_check=True)
                        m = mm(ybank[i][rows, b * T:(b + 1) * T], xs[:, g % 2, 0, tok, rows],
                               decay[:, i, j, b, q, :], start=True, stop=True, skip_group_check=True)
                m.then_inc(y_mm.sem, 1)

            def turn_x(it, g):
                wait(pe, xt_ok, it, g + 1)
                for b in range(NB):
                    m = nc.tensor.transpose(gp0[:, b * P:(b + 1) * P], x_t[:, g % 2, b * T:(b + 1) * T], const("ident"))
                m.then_inc(tr_mm.sem, 1)

            def spread_cum(it, g):
                mm(cA[:, :], ind_ch[:, g * HG:(g + 1) * HG, :].rearrange("p h d -> p (h d)"), cum_r[:, :],
                   start=True, stop=True).then_inc(e_mm.sem, 1)

            def to_heads(it, g):
                wait(pe, fs_ok, it, g + 1)
                for h in range(HG):
                    q, j = h // 2, h % 2
                    m = mm(gp1[DS * j:DS * j + DS, q * 128:q * 128 + 128].rearrange("p (b d) -> p b d", b=NB),
                           mh[:, g * HG + h, :], fs[:, :, HD * h:HD * h + HD], start=True, stop=True, skip_group_check=True)
                m.then_inc(h_mm.sem, 1)

            def main(it, pre):
                for g in range(NG):
                    diff(it, 2 * g + 1)
                    products(it, 2 * g + 1)
                    if g:
                        wait(pe, gate_ok, it, g + 1)
                        to_heads(it, g - 1)
                    if g + 1 < NG:
                        if g:
                            wait(pe, fs_ok, it, g)
                        else:
                            wait(pe, xs_ok, it, 2)
                        project(gp0, (g + 1) * P).then_inc(x_mm.sem, 1)
                    diff(it, 2 * g + 2)
                    outputs(it, 2 * g + 1)
                    products(it, 2 * g + 2)
                    if g + 1 < NG:
                        turn_x(it, g + 1)
                        if g:
                            wait(pe, state_ok, it, 2 * g)
                        else:
                            wait(pe, gate_ok, it, 1)
                        project(gp1, DI + (g + 1) * P).then_inc(z_mm.sem, 1)
                    outputs(it, 2 * g + 2)
                    if g + 1 < NG:
                        wait(pe, xs_ok, it, 2 * g + 4)
                    else:
                        wait(pe, fs_ok, it, g)
                    wait(pe, ft_ok, it, 1)
                    for b in range(NB):
                        m = mm(gp0[0:NF, b * P:(b + 1) * P], feat_t[:, b, :], xs[:, g % 2, 1, b, :], start=True,
                               stop=True, skip_group_check=True)
                    m.then_inc(f_mm.sem, 1)
                    if g + 1 < NG:
                        spread_cum(it, g + 1)

            def project_out(it, b):
                bank, tok = ybank[b % 2], b * T
                wait(pe, y_ok, it, NG)
                wait(pe, acc_ok, it, INNER)
                if b < 2:
                    wait(pe, yc_ok, it, 2 * NG - 1 + b)
                else:
                    wait(pe, out_ok, it, b - 1)
                for k in range(NG):
                    mm(bank[:, :], y[:, k, tok:tok + T], wo[:, k, :], start=(k == 0), stop=False)
                r = slice(MID * (b // 2), MID * (b // 2) + MID)
                mm(bank[:, :], acc[r, (b % 2) * T:(b % 2 + 1) * T], wf[r, :], start=False, stop=True).then_inc(out_mm.sem, 1)

            def tail(it, outs, pre):
                n = it + 1
                if pre:
                    wait(pe, normed, n, NB)
                    wait(pe, exp_ok, it, 2 * NG)
                    wait(pe, s_mul, it, 2 * NG)
                    for k in range(KD):
                        for b in range(NB):
                            m = nc.tensor.transpose(xt_bank[k][:, b * T:(b + 1) * T], xn[:, b, k * P:(k + 1) * P], const("ident"))
                        m.then_inc(xt_mm.sem, 1)
                if outs:
                    to_heads(it, NG - 1)
                if pre:
                    wait(pe, lo_ok, n, KD)
                    wait(pe, fs_ok, it, NG)
                    project(gp0, C_DTA).then_inc(dta_mm.sem, 1)
                    wait(pe, state_ok, it, 2 * NG)
                    project(gp1, C_BC).then_inc(bc_mm.sem, 1)
                    project(dA, C_FFN).then_inc(ffn_mm.sem, 1)
                if outs:
                    project_out(it, 0)
                if pre:
                    wait(pe, sq_ok, n, 1)
                    mm(dB[:, :], const("mean"), rms_a[:, :], start=True, stop=True).then_inc(ms_mm.sem, 1)
                if outs:
                    project_out(it, 1)
                if pre:
                    wait(pe, sin_ok, n, 1)
                    wait(pe, xb_ok, n, 1)
                    wait(pe, trap_e, n, 1)
                    wait(pe, angle, n, 1)
                    r = slice(DS, DS + 2 * ROPE)
                    mm(gp0[:, :], const("selcos", r), feat[r, :], start=True, stop=True).then_inc(cos_mm.sem, 1)
                    wait(pe, bcn_ok, n, 1)
                    mm(gp1[:, :], const("selsin", r), feat[r, :], start=True, stop=True).then_inc(sin_mm.sem, 1)
                    wait(pe, ms_ln, n, 1)
                    wait(pe, s_ok, n, 2)
                    for bank, name in ((dB, "dupB"), (cA, "dupBs"), (cB, "dupC"), (dA, "dupCs")):
                        mm(bank[:, :], const(name), rms_a[:, :], start=True, stop=True).then_inc(dup_mm.sem, 1)
                if outs:
                    project_out(it, 2)
                if pre:
                    wait(pe, cos_ok, n, 1)
                    wait(pe, hm_ok, n, 1)
                    wait(pe, sinx_ok, n, 1)
                    wait(pe, dend_ok, n, NB)
                    mm(gp1[:, 0:NB * NH], ones_r[:, :], dend_r[:, :, :].rearrange("p b h -> p (b h)"), start=True,
                       stop=True).then_inc(dend_mm.sem, 1)
                    for b in range(NB):
                        m = nc.tensor.transpose(gp0[:, b * 64:(b + 1) * 64], hm[:, b * T:(b + 1) * T], const("ident", slice(0, 64))[:, 0:64])
                    m.then_inc(hm_mm.sem, 1)
                    wait(pe, top_ok, n, 1)
                    for b in range(NB):
                        m = nc.tensor.transpose(dB[:, b * NF:(b + 1) * NF], feat[0:NF, b * T:(b + 1) * T],
                                                const("ident", slice(0, NF))[:, 0:NF])
                    m.then_inc(ft_mm.sem, 1)
                if outs:
                    project_out(it, 3)
                if pre:
                    wait(pe, gw_ok, n, 1)
                    project(gp0, 0).then_inc(x_mm.sem, 1)
                    wait(pe, dec_ok, n, 1)
                    project(gp1, DI).then_inc(z_mm.sem, 1)
                    wait(pe, share, n, 6)
                    spread_cum(n, 0)
                    turn_x(n, 0)

            pe.wait_ge(loaded, 16 * n_loads)
            pe.wait_ge(ind_ready, 4)
            pe.wait_ge(mh_done, 2)
            pe.wait_ge(lo_done, KD)
            pe.wait_ge(st_zero, 1)
            loop(pe, main, tail)


_OUTS = [((4, 4096, DM), 'float32')]


def layout(inp):
    i = {k: np.asarray(v) for k, v in inp.items()}
    w = i["L0_attn_W_in"]
    o = 2 * DI
    z, x, bc, dta, ang = w[0:DI], w[DI:o], w[o:o + 2 * DS], w[o + 2 * DS:o + 2 * DS + 3 * NH], w[o + 2 * DS + 3 * NH:]
    ffn = i["L0_ffn_Win"].T
    w_in = np.concatenate([x, z, dta, ang, ang, bc, ffn, ffn]).T
    pcols = np.zeros((P, N_PCOLS), np.float32)
    part = {k: pcols[:, a:a + n] for k, (a, n) in PC.items()}
    part["normw"][:, 0] = np.concatenate([i["L0_attn_Bn_w"], i["L0_attn_Cn_w"]])
    part["dtbias"][0:NH, 0] = i["L0_attn_dt_bias"]
    part["phase"][96 + ROPE:, 0] = np.pi / 2
    part["onerow"][:, 0] = np.arange(P) % DS >= 2 * ROPE
    part["eps"][:] = EPS
    twice = lambda a: np.concatenate([a, a])
    part["bin"][:, 0] = twice(i["L0_ffn_bin_"])
    part["b2"][:, 0] = twice(i["L0_ffn_b2"])
    part["W1"][:], part["b1"][:], part["W2"][:] = (twice(i["L0_ffn_" + k]) for k in ("W1", "b1", "W2"))
    part["D"][:] = np.repeat(i["L0_attn_D"], HD).reshape(NG, P).T
    swap = np.arange(DS)
    swap[:2 * ROPE] = (swap[:2 * ROPE] + ROPE) % (2 * ROPE)
    for k, name in (("B", "L0_attn_B_bias"), ("C", "L0_attn_C_bias")):
        b = i[name].reshape(16, 2, DS)
        part["cA_" + k][:] = b.transpose(1, 2, 0).reshape(P, 16)
        part["cB_" + k][:] = b[:, :, swap].transpose(1, 2, 0).reshape(P, 16)
    mh_bias = np.stack([i["L0_attn_B_bias"][:, swap], i["L0_attn_B_bias"]])
    scanmask = np.ones((NH, TOK), np.float32)
    scanmask[:, ::T] = 0
    return {"u": i["L0_attn_u"], "w_in": w_in, "w_out": i["L0_attn_W_out"].T, "w_ffn": twice(i["L0_ffn_Wout"]),
            "pcols": pcols, "bout": i["L0_ffn_bout"][None, :], "mh_bias": mh_bias, "consts": constants(),
            "scanmask": scanmask}


def kernel(**inputs):
    import concourse.bacc as _bacc
    from concourse.bass_utils import run_bass_kernel_spmd as _run

    nc = _bacc.Bacc("TRN2", target_bir_lowering=False, num_devices=1)
    arrays, args = {}, []
    for name, a in layout(inputs).items():
        a = np.ascontiguousarray(a)
        arrays[f"in_{name}_dram"] = a
        args.append(nc.dram_tensor(f"in_{name}_dram", a.shape, mybir.dt.from_np(a.dtype), kind="ExternalInput").ap())
    for i, (shape, dtype) in enumerate(_OUTS):
        args.append(nc.dram_tensor(f"out_{i}_dram", shape, mybir.dt.from_np(np.dtype(dtype)), kind="ExternalOutput").ap())
    mixer(nc, *args, n_iter=arrays["in_u_dram"].shape[1] // T)
    r = _run(nc, [arrays], core_ids=[0])
    return r.results[0]["out_0_dram"]
```

```python
from contextlib import ExitStack

import numpy as np

import concourse.bass as bass
from concourse import mybir

F32, F32R, F16, I32 = mybir.dt.float32, mybir.dt.float32r, mybir.dt.float16, mybir.dt.int32
ALU = mybir.AluOpType
ACT = mybir.ActivationFunctionType
AX_X = mybir.AxisListType.X
RMAX = bass.bass_isa.ReduceOp.max

P = 128
NB, T = 4, 128
TOK = NB * T
DM, KD = 512, 4
NH, HD, DS = 32, 32, 64
DI = NH * HD
HG = 4
NG = NH // HG
ROPE = 16
MID, INNER = 64, 16
NF = DS + 2 * ROPE + 1
WCOLS = 2 * DI + 3 * P
C_DTA, C_BC, C_FFN = 2 * DI, 2 * DI + P, 2 * DI + 2 * P
A_FLOOR, EPS = 1e-4, 1e-5
XN_SCALE, W_SCALE = 256.0, 4096.0
MAGIC = 1.5 * 2.0**23
TWO_PI_HI, TWO_PI_LO = 6.28125, 2 * np.pi - 6.28125
SIN_MAX = 3.1415925
A_LEAST = 1e-18

PC = {}
for _name, _n in (("normw", 1), ("dtbias", 1), ("phase", 1), ("onerow", 1), ("eps", 1), ("bin", 1), ("b2", 1),
                  ("W1", INNER), ("b1", INNER), ("W2", INNER), ("D", NG),
                  ("cA_B", 16), ("cB_B", 16), ("cA_C", 16), ("cB_C", 16)):
    PC[_name] = (sum(n for _, n in PC.values()), _n)
N_PCOLS = sum(n for _, n in PC.values())

CC = {}
for _name, _n in (("ident", P), ("swap", P), ("dupB", P), ("dupC", P), ("mean", P),
                  ("selcos", P), ("selsin", P), ("ind", NH), ("mmask", DS), ("mone", DS)):
    CC[_name] = (sum(n for _, n in CC.values()), _n)
N_CONST = sum(n for _, n in CC.values())


def constants():
    c = np.zeros((P, N_CONST), np.float32)
    part = {k: c[:, a:a + n] for k, (a, n) in CC.items()}
    part["ident"][:] = np.eye(P)
    for m in range(P):
        n = m % DS
        part["dupB"][n, m] = 1
        part["dupC"][DS + n, m] = 1
        part["mean"][m - n:m - n + DS, m] = 1 / DS
        if n < 2 * ROPE:
            part["swap"][m - n + (n + ROPE) % (2 * ROPE), m] = 1
            part["selsin"][DS + n % ROPE, m] = -1 if n < ROPE else 1
            part["selcos"][DS + ROPE + n % ROPE, m] = 1
    for k in range(2 * NH):
        part["ind"][k, k % NH] = 1
    for i in range(ROPE):
        part["mmask"][DS + i, i] = -1
        part["mmask"][DS + i, ROPE + i] = 1
        part["mmask"][DS + ROPE + i, i] = 1
        part["mmask"][DS + ROPE + i, ROPE + i] = 1
    part["mmask"][NF - 1, 2 * ROPE:] = 1
    part["mone"][:DS] = np.eye(DS)
    return c


class Count:

    def __init__(self, sem, events, unit=1):
        self.sem, self.events, self.unit = sem, events, unit

    def at(self, it, k):
        return it * (self.events * self.unit) + k * self.unit


def mixer(nc, u, w_in, w_out, w_ffn, pcols, bout, mh_bias, consts, out, n_iter):
    with ExitStack() as ctx:
        def sb(name, shape, dt=F32):
            return ctx.enter_context(nc.sbuf_tensor(name, shape, dt))

        def sem(name):
            return ctx.enter_context(nc.semaphore(name))

        counts = []

        def count(name, events, unit=1):
            c = Count(sem(name), events, unit)
            counts.append(c)
            return c

        w_hi = sb("w_hi", [P, KD, WCOLS], F16)
        w_lo = sb("w_lo", [P, KD, WCOLS], F16)
        wo = sb("wo", [P, NG, DM])
        wf = sb("wf", [P, DM])
        cst = sb("cst", [P, N_CONST])
        pc = sb("pc", [P, N_PCOLS])
        bout_bc = sb("bout_bc", [P, DM])
        mh = sb("mh", [NF, NH, DS])
        ind_r = sb("ind_r", [2 * NH, NH], F32R)
        ind_ch = sb("ind_ch", [2 * NH, NH, HD], F32R)
        ones_r = sb("ones_r", [2 * NH, P], F32R)
        scales = sb("scales", [P, 16])
        xn = sb("xn", [P, NB, DM])
        stats = sb("stats", [P, NB, 6])
        mv = sb("mv", [P, NB, 2])
        nt = sb("nt", [P, 5, NB])
        x_hi = sb("x_hi", [P, KD, TOK], F16)
        x_lo = sb("x_lo", [P, KD, TOK], F16)
        cum_r = sb("cum_r", [2 * NH, TOK], F32R)
        dend_r = sb("dend_r", [2 * NH, NB, NH], F32R)
        hm = sb("hm", [3 * NH, TOK])
        gw = sb("gw", [P, NB, 3 * NH])
        dec = sb("dec", [P, NB, NH // 2])
        cosx = sb("cosx", [P, TOK])
        sinx = sb("sinx", [P, TOK])
        bshare = sb("bshare", [P, TOK])
        cshare = sb("cshare", [P, TOK])
        feat = sb("feat", [P, TOK])
        feat_t = sb("feat_t", [P, NB, NF])
        s_mid = sb("s_mid", [P, TOK // 2])
        relu = sb("relu", [P, 2, TOK // 2])
        acc = sb("acc", [P, TOK // 2])
        arena = sb("arena", [P, 24 * TOK])
        y = arena[:, 0:8 * TOK].rearrange("p (g t) -> p g t", g=NG)
        bh = arena[:, 8 * TOK:12 * TOK].rearrange("p (s q t) -> p s q t", s=2, q=2)
        ch = arena[:, 12 * TOK:16 * TOK].rearrange("p (s q t) -> p s q t", s=2, q=2)
        lt = arena[:, 16 * TOK:20 * TOK]
        decay = lt.rearrange("p (u j b q t) -> p u j b q t", u=2, j=2, b=2, q=2)
        xs = arena[:, 20 * TOK:24 * TOK].rearrange("p (s i b c) -> p s i b c", s=2, i=2, b=NB)
        x_t = sb("x_t", [P, 2, TOK])
        sig = sb("sig", [P, TOK])
        gate = sb("gate", [P, 2, TOK])
        ecum = sb("ecum", [P, 2, TOK])
        yc = sb("yc", [P, TOK])
        dx = sb("dx", [P, TOK])
        fs = sb("fs", [NF, NB, P])
        state = sb("state", [P, NH // 2, NB, HD])
        res = sb("res", [P, 2, DM])

        rms_a, rms_b = yc, sig
        xb, lg = xn[0:64, 0, :], xn[0:64, 1, :]
        th, kr, kk = xn[64:96, 0, :], xn[64:96, 1, :], xn[64:96, 2, :]
        tr2, gg = xn[0:NH, 2, :], xn[0:NH, 3, :]
        dt_, av, cum, wd = (lt[0:NH, i * TOK:(i + 1) * TOK] for i in range(4))

        banks = [ctx.enter_context(nc.psum_tensor(f"bank{i}", [P, TOK], F32)) for i in range(8)]
        gp0, gp1, dA, dB, cA, cB, y0, y1 = banks
        dbank, cbank, ybank = (dA, dB), (cA, cB), (y0, y1)
        xt_bank = (gp0, gp1, dA, dB)

        def col(name, i=0, rows=slice(0, P)):
            a, _ = PC[name]
            return pc[rows, a + i:a + i + 1]

        def const(name, rows=slice(0, P)):
            a, n = CC[name]
            return cst[rows, a:a + n]

        ds_col = scales[:, 0:1]
        w_scale = scales[:, 12:13]
        nds_col = scales[:, 1:2]
        wds_col = scales[:, 2:3]

        loaded, ind_ready, st_zero = sem("loaded"), sem("ind_ready"), sem("st_zero")
        stage_in = [sem(f"stage_in{k}") for k in range(KD)]
        absmax_done, allmax_done, scale_done = sem("absmax_done"), sem("allmax_done"), sem("scale_done")
        hi_done, lo_done, mh_done = sem("hi_done"), sem("lo_done"), sem("mh_done")
        u_in = count("u_in", 1, 16)
        bn1, bn2 = count("bn1", NB), count("bn2", NB)
        var_ln, rstd0, newton, normed = count("var_ln", 1), count("rstd0", 1), count("newton", 4), count("normed", NB)
        xt_mm, hi_ok, lo_ok = count("xt_mm", KD), count("hi_ok", KD), count("lo_ok", KD)
        dta_mm, bc_mm, ffn_mm = count("dta_mm", 1), count("bc_mm", 1), count("ffn_mm", 1)
        xb_ok, soft, trap_e, trap = count("xb_ok", 1), count("soft", 3), count("trap_e", 3), count("trap", 2)
        angle, sin_ok = count("angle", 7), count("sin_ok", 1)
        dt_ok, decay_rate, ea_ok, a_ok, lna_ok = count("dt_ok", 2), count("decay_rate", 1), count("ea_ok", 1), count("a_ok", 2), count("lna_ok", 1)
        cum_ok, cum_hi, cum_lo = count("cum_ok", NB), count("cum_hi", 2), count("cum_lo", 1)
        wd_ok, we_ok, gdt_ok, hm_ok, hm_mm, gw_ok = count("wd_ok", 1), count("we_ok", 1), count("gdt_ok", 1), count("hm_ok", 1), count("hm_mm", 1), count("gw_ok", 1)
        dend_ok, dend_mm, dec_ok = count("dend_ok", NB), count("dend_mm", 1), count("dec_ok", 2)
        sq_ok, ms_mm, ms_ln, rms_ok, bcn_ok = count("sq_ok", 1), count("ms_mm", 1), count("ms_ln", 1), count("rms_ok", 1), count("bcn_ok", 1)
        cos_mm, sin_mm, cos_ok, sinx_ok = count("cos_mm", 1), count("sin_mm", 1), count("cos_ok", 1), count("sinx_ok", 1)
        base_ok, dup_mm, share, top_ok, ft_mm, ft_ok = count("base_ok", 2), count("dup_mm", 3), count("share", 3), count("top_ok", 1), count("ft_mm", 1), count("ft_ok", 1)
        s_ok, relu_ok, acc_ok = count("s_ok", 2), count("relu_ok", INNER), count("acc_ok", INNER)
        x_mm, z_mm, xt_ok, tr_mm, xs_ok = count("x_mm", NG), count("z_mm", NG), count("xt_ok", NG), count("tr_mm", NG), count("xs_ok", 2 * NG)
        sig_ok, gate_ok = count("sig_ok", 3 * NG), count("gate_ok", NG)
        h1_ok, h2_ok = count("h1_ok", 4 * NG), count("h2_ok", 4 * NG)
        diff_mm, cb_mm, exp_ok, mask_ok, s_mul = count("diff_mm", 2 * NG), count("cb_mm", 2 * NG), count("exp_ok", 2 * NG), count("mask_ok", 2 * NG), count("s_mul", 2 * NG)
        pool_step, dve_step, sp_step = sem("pool_step"), sem("dve_step"), sem("sp_step")
        y_mm, t1_ok, yc_ok = count("y_mm", 2 * NG), count("t1_ok", 2 * NG), count("yc_ok", 2 * NG)
        e_mm, e_ok = count("e_mm", NG), count("e_ok", NG)
        dx_ok, ysum_ok, y_ok = count("dx_ok", NG), count("ysum_ok", NG), count("y_ok", NG)
        f_mm, fs_ok, h_mm, faded, state_ok = count("f_mm", NG), count("fs_ok", NG), count("h_mm", NG), count("faded", NG), count("state_ok", NG)
        out_mm, res_ok, out_ok = count("out_mm", NB), count("res_ok", NB), count("out_ok", NB)
        res_in = [count(f"res_in{i}", 2, 16) for i in range(2)]
        stored = [count(f"stored{i}", 2, 16) for i in range(2)]

        def loop(eng, main, tail):
            tail(0, False, True)
            if n_iter > 1:
                with eng.Fori(1, n_iter) as it:
                    main(it, True)
                    tail(it, True, True)
            main(n_iter, False)
            tail(n_iter, True, False)

        u_chunk = u.rearrange("b (c t) d -> c t b d", t=T)
        out_chunk = out.rearrange("b (c t) d -> c t b d", t=T)
        w_in_k = w_in.rearrange("(k p) n -> k p n", p=P)
        n_loads = 8
        stage = [arena[:, k * WCOLS:(k + 1) * WCOLS] for k in range(KD)]

        block = ctx.enter_context(nc.Block())

        @block.sync
        def _(sp):
            for c in counts:
                sp.sem_inc(c.sem, c.events * c.unit)
            for k in range(KD):
                sp.dma_start(stage[k], w_in_k[k]).then_inc(stage_in[k], 16)
            sp.dma_start(cst[:, :], consts).then_inc(loaded, 16)
            sp.dma_start(pc[:, :], pcols).then_inc(loaded, 16)
            sp.dma_start(bout_bc[:, :], bout.broadcast_to([P, DM])).then_inc(loaded, 16)
            sp.dma_start(mh[DS:DS + ROPE, :, :], mh_bias[0:1].broadcast_to([ROPE, NH, DS])).then_inc(loaded, 16)
            sp.dma_start(mh[DS + ROPE:NF, :, :], mh_bias[1:2].broadcast_to([ROPE + 1, NH, DS])).then_inc(loaded, 16)
            sp.dma_start(mh[0:DS, :, :], mh_bias[1:2].broadcast_to([DS, NH, DS])).then_inc(loaded, 16)
            sp.dma_start(wo[:, :, :], w_out.rearrange("(k p) n -> p k n", p=P)).then_inc(loaded, 16)
            sp.dma_start(wf[:, :], w_ffn).then_inc(loaded, 16)
            def load_u(n):
                sp.wait_ge(normed.sem, normed.at(n - 1, NB))
                sp.sem_inc(sp_step, 1)
                sp.wait_ge(xt_mm.sem, xt_mm.at(n - 1, KD))
                sp.sem_inc(sp_step, 1)
                sp.wait_ge(gdt_ok.sem, gdt_ok.at(n - 1, 1))
                sp.sem_inc(sp_step, 1)
                sp.wait_ge(a_ok.sem, a_ok.at(n - 1, 2))
                sp.sem_inc(sp_step, 1)
                sp.wait_ge(sin_ok.sem, sin_ok.at(n - 1, 1))
                sp.sem_inc(sp_step, 1)
                sp.dma_start(xn[:, :, :], u_chunk[n - 1]).then_inc(u_in.sem, 16)

            def main(it, pre):
                if pre:
                    load_u(it + 1)
                for b in range(2):
                    sp.wait_ge(stored[b].sem, stored[b].at(it, 0))
                    sp.sem_inc(sp_step, 1)
                    sp.dma_start(res[:, b, :], u_chunk[it - 1, :, b, :]).then_inc(res_in[b].sem, 16)

            def tail(it, outs, pre):
                if not outs:
                    load_u(1)
                    return
                for b in range(NB):
                    sp.wait_ge(out_ok.sem, out_ok.at(it, b + 1))
                    sp.sem_inc(sp_step, 1)
                    sp.dma_start(out_chunk[it - 1, :, b, :], res[:, b % 2, :]).then_inc(stored[b % 2].sem, 16)
                    if b < 2:
                        sp.wait_ge(stored[b].sem, stored[b].at(it, 1))
                        sp.sem_inc(sp_step, 1)
                        sp.dma_start(res[:, b, :], u_chunk[it - 1, :, b + 2, :]).then_inc(res_in[b].sem, 16)

            loop(sp, main, tail)
            for b in range(2):
                sp.wait_ge(stored[b].sem, stored[b].at(n_iter, 2))
                sp.sem_inc(sp_step, 1)

        @block.gpsimd
        def _(pool):
            pool.wait_ge(absmax_done, KD)
            pool.wait_ge(scale_done, 1)
            nc.gpsimd.partition_all_reduce(scales[:, 9:10], scales[:, 8:9], P, RMAX).then_inc(allmax_done, 1)
            nc.gpsimd.memset(state[:, :, :, :], 0.0).then_inc(st_zero, 1)

            def mask(it, n):
                pool.wait_ge(exp_ok.sem, exp_ok.at(it, n))
                pool.sem_inc(pool_step, 1)
                v = decay[:, (n - 1) % 2].rearrange("p j b q t -> p (j b q) t")
                nc.gpsimd.affine_select(out=v, in_=v, compare_op=ALU.is_ge, fill=0.0, base=0,
                                        pattern=[[0, 8], [1, T]], channel_multiplier=-1).then_inc(mask_ok.sem, 1)

            def finish(it, g):
                pool.wait_ge(xt_ok.sem, xt_ok.at(it, g + 1))
                pool.wait_ge(y_ok.sem, y_ok.at(it, g))
                pool.sem_inc(pool_step, 1)
                nc.gpsimd.tensor_scalar(dx[:, :], x_t[:, g % 2, :], col("D", g), None, ALU.mult).then_inc(dx_ok.sem, 1)
                pool.wait_ge(dx_ok.sem, dx_ok.at(it, g + 1))
                pool.wait_ge(yc_ok.sem, yc_ok.at(it, 2 * g + 2))
                nc.gpsimd.tensor_tensor(dx[:, :], dx[:, :], yc[:, :], ALU.add).then_inc(ysum_ok.sem, 1)
                pool.wait_ge(ysum_ok.sem, ysum_ok.at(it, g + 1))
                pool.wait_ge(gate_ok.sem, gate_ok.at(it, g + 1))
                pool.wait_ge(out_mm.sem, out_mm.at(it, 0))
                nc.gpsimd.tensor_tensor(y[:, g, :], dx[:, :], gate[:, g % 2, :], ALU.mult).then_inc(y_ok.sem, 1)

            def main(it, pre):
                for g in range(NG):
                    if g:
                        finish(it, g - 1)
                    mask(it, 2 * g + 2)
                    if g + 1 < NG:
                        mask(it, 2 * g + 3)
                    pool.wait_ge(y_mm.sem, y_mm.at(it, 2 * g + 2))
                    pool.wait_ge(dec_ok.sem, dec_ok.at(it, 2))
                    pool.wait_ge(state_ok.sem, state_ok.at(it, g + 1 - NG))
                    s = state[:, 2 * g:2 * g + 2]
                    d = dec[:, :, 2 * g:2 * g + 2].rearrange("p b q -> p q b").unsqueeze(3).broadcast_to([P, 2, NB, HD])
                    nc.gpsimd.tensor_tensor(s, s, d, ALU.mult).then_inc(faded.sem, 1)
                finish(it, NG - 1)

            def tail(it, outs, pre):
                if not outs:
                    pool.wait_ge(st_zero, 1)
                else:
                    for b in range(NB):
                        pool.wait_ge(res_in[b % 2].sem, res_in[b % 2].at(it, b // 2 + 1))
                        nc.gpsimd.tensor_tensor(res[:, b % 2, :], res[:, b % 2, :], bout_bc[:, :], ALU.add).then_inc(res_ok.sem, 1)
                if pre:
                    mask(it + 1, 1)

            pool.wait_ge(loaded, 16 * n_loads)
            loop(pool, main, tail)

        @block.scalar
        def _(act):
            nc.scalar.preload_act_table_set("natural_log_exp_and_others")
            act.wait_ge(loaded, 16 * n_loads)
            act.wait_ge(scale_done, 4)
            for k in range(KD):
                act.wait_ge(stage_in[k], 16)
                nc.scalar.activation(w_hi[:, k, :], stage[k], ACT.Copy, scale=w_scale).then_inc(hi_done, 1)

            def norm(n):
                act.wait_ge(bn2.sem, bn2.at(n, NB))
                nc.scalar.activation(nt[:, 0, :], mv[:, :, 1], ACT.Ln, bias=col("eps")).then_inc(var_ln.sem, 1)
                act.wait_ge(var_ln.sem, var_ln.at(n, 1))
                act.wait_ge(normed.sem, normed.at(n - 1, NB))
                nc.scalar.activation(nt[:, 1, :], nt[:, 0, :], ACT.Exp, scale=-0.5).then_inc(rstd0.sem, 1)

            def exp_diff(it, n):
                act.wait_ge(diff_mm.sem, diff_mm.at(it, n))
                act.wait_ge(y_mm.sem, y_mm.at(it, n - 2))
                act.wait_ge(gw_ok.sem, gw_ok.at(it, 1))
                g, i = (n - 1) // 2, (n - 1) % 2
                for j in range(2):
                    for q in range(2):
                        for b in range(2):
                            h = 2 * NH + g * HG + 2 * q + j
                            e = nc.scalar.activation(decay[:, i, j, b, q, :], dbank[j][:, (2 * q + b) * T:(2 * q + b + 1) * T],
                                                     ACT.Exp, bias=gw[:, 2 * i + b, h:h + 1])
                e.then_inc(exp_ok.sem, 1)

            def x_out(it, g):
                act.wait_ge(x_mm.sem, x_mm.at(it, g + 1))
                act.wait_ge(dx_ok.sem, dx_ok.at(it, g - 1))
                act.wait_ge(tr_mm.sem, tr_mm.at(it, g - 1))
                nc.scalar.activation(x_t[:, g % 2, :], gp0[:, :], ACT.Copy, scale=ds_col).then_inc(xt_ok.sem, 1)

            def sigmoid(it, g):
                act.wait_ge(z_mm.sem, z_mm.at(it, g + 1))
                act.wait_ge(gate_ok.sem, gate_ok.at(it, g))
                nc.scalar.activation(sig[:, :], gp1[:, :], ACT.Exp, scale=nds_col).then_inc(sig_ok.sem, 1)
                act.wait_ge(sig_ok.sem, sig_ok.at(it, 3 * g + 1))
                nc.scalar.activation(sig[:, :], sig[:, :], ACT.Ln, bias=1.0).then_inc(sig_ok.sem, 1)
                act.wait_ge(sig_ok.sem, sig_ok.at(it, 3 * g + 2))
                nc.scalar.activation(sig[:, :], sig[:, :], ACT.Exp, scale=-1.0).then_inc(sig_ok.sem, 1)

            def e_out(it, g):
                act.wait_ge(e_mm.sem, e_mm.at(it, g + 1))
                act.wait_ge(yc_ok.sem, yc_ok.at(it, 2 * g - 2))
                nc.scalar.activation(ecum[:, g % 2, :], cA[:, :], ACT.Exp).then_inc(e_ok.sem, 1)

            def hidden(it, j):
                act.wait_ge(s_ok.sem, s_ok.at(it, 2))
                act.wait_ge(acc_ok.sem, acc_ok.at(it, j - 1))
                nc.scalar.activation(relu[:, j % 2, :], s_mid[:, :], ACT.Relu, bias=col("b1", j),
                                     scale=col("W1", j)).then_inc(relu_ok.sem, 1)

            def high_half(n, k):
                act.wait_ge(z_mm.sem, z_mm.at(n, 0))
                act.wait_ge(xt_mm.sem, xt_mm.at(n, k + 1))
                nc.scalar.activation(x_hi[:, k, :], xt_bank[k][:, :], ACT.Copy).then_inc(hi_ok.sem, 1)

            def main(it, pre):
                for g in range(NG):
                    exp_diff(it, 2 * g + 2)
                    if g + 1 < NG:
                        x_out(it, g + 1)
                    elif pre:
                        high_half(it + 1, 0)
                    hidden(it, 2 * g)
                    hidden(it, 2 * g + 1)
                    if g + 1 < NG:
                        exp_diff(it, 2 * g + 3)
                        e_out(it, g + 1)
                        sigmoid(it, g + 1)
                    elif pre:
                        for k in range(1, KD):
                            high_half(it + 1, k)
                    if g == NG - 4 and pre:
                        norm(it + 1)
                    act.wait_ge(f_mm.sem, f_mm.at(it, g + 1))
                    act.wait_ge(h_mm.sem, h_mm.at(it, g))
                    nc.scalar.activation(fs[:, :, :], gp0[0:NF, :].rearrange("p (b c) -> p b c", b=NB),
                                         ACT.Copy).then_inc(fs_ok.sem, 1)

            def tail(it, outs, pre):
                n = it + 1
                if not pre:
                    return
                if not outs:
                    norm(n)
                    for k in range(KD):
                        high_half(n, k)
                act.wait_ge(dta_mm.sem, dta_mm.at(n, 1))
                act.wait_ge(xt_mm.sem, xt_mm.at(n, KD))
                nc.scalar.activation(xb, gp0[0:64, :], ACT.Identity, bias=col("dtbias", 0, slice(0, 64)),
                                     scale=scales[0:64, 0:1]).then_inc(xb_ok.sem, 1)
                act.wait_ge(xb_ok.sem, xb_ok.at(n, 1))
                nc.scalar.activation(lg, xb, ACT.Abs).then_inc(soft.sem, 1)
                act.wait_ge(soft.sem, soft.at(n, 1))
                nc.scalar.activation(lg, lg, ACT.Exp, scale=-1.0).then_inc(soft.sem, 1)
                act.wait_ge(soft.sem, soft.at(n, 2))
                nc.scalar.activation(lg, lg, ACT.Ln, bias=1.0).then_inc(soft.sem, 1)
                nc.scalar.activation(tr2, gp0[64:96, :], ACT.Exp, scale=scales[64:96, 1:2]).then_inc(trap_e.sem, 1)
                act.wait_ge(trap_e.sem, trap_e.at(n, 1))
                nc.scalar.activation(tr2, tr2, ACT.Ln, bias=1.0).then_inc(trap_e.sem, 1)
                act.wait_ge(trap_e.sem, trap_e.at(n, 2))
                nc.scalar.activation(tr2, tr2, ACT.Exp, scale=-1.0).then_inc(trap_e.sem, 1)
                act.wait_ge(bc_mm.sem, bc_mm.at(n, 1))
                act.wait_ge(ysum_ok.sem, ysum_ok.at(it, NG))
                act.wait_ge(top_ok.sem, top_ok.at(n - 1, 1))
                act.wait_ge(dup_mm.sem, dup_mm.at(n - 1, 3))
                nc.scalar.activation(rms_a[:, :], gp1[:, :], ACT.Square, scale=ds_col).then_inc(sq_ok.sem, 1)
                act.wait_ge(angle.sem, angle.at(n, 7))
                act.wait_ge(ft_mm.sem, ft_mm.at(n - 1, 1))
                act.wait_ge(sin_mm.sem, sin_mm.at(n - 1, 1))
                nc.scalar.activation(feat[DS:DS + 2 * ROPE, :], th, ACT.Sin).then_inc(sin_ok.sem, 1)
                nc.scalar.preload_act_table_set("natural_log_exp_and_others")
                act.wait_ge(ffn_mm.sem, ffn_mm.at(n, 1))
                act.wait_ge(relu_ok.sem, relu_ok.at(it, INNER))
                for h in range(2):
                    r = slice(MID * h, MID * h + MID)
                    nc.scalar.activation(s_mid[r, :], dA[r, h * 256:h * 256 + 256], ACT.Identity,
                                         bias=col("bin", 0, r), scale=scales[r, 0:1]).then_inc(s_ok.sem, 1)
                act.wait_ge(decay_rate.sem, decay_rate.at(n, 1))
                nc.scalar.activation(av, av, ACT.Exp, scale=-1.0).then_inc(ea_ok.sem, 1)
                act.wait_ge(ms_mm.sem, ms_mm.at(n, 1))
                act.wait_ge(gate_ok.sem, gate_ok.at(it, NG))
                nc.scalar.activation(rms_b[:, :], dB[:, :], ACT.Ln, bias=col("eps")).then_inc(ms_ln.sem, 1)
                act.wait_ge(ms_ln.sem, ms_ln.at(n, 1))
                nc.scalar.activation(rms_b[:, :], rms_b[:, :], ACT.Exp, scale=-0.5).then_inc(rms_ok.sem, 1)
                act.wait_ge(a_ok.sem, a_ok.at(n, 2))
                nc.scalar.activation(av, av, ACT.Ln).then_inc(lna_ok.sem, 1)
                act.wait_ge(cos_mm.sem, cos_mm.at(n, 1))
                act.wait_ge(h2_ok.sem, h2_ok.at(it, 4 * NG))
                nc.scalar.activation(cosx[:, :], gp0[:, :], ACT.Identity, bias=col("onerow")).then_inc(cos_ok.sem, 1)
                act.wait_ge(sin_mm.sem, sin_mm.at(n, 1))
                nc.scalar.activation(sinx[:, :], cA[:, :], ACT.Copy).then_inc(sinx_ok.sem, 1)
                act.wait_ge(cum_ok.sem, cum_ok.at(n, NB))
                act.wait_ge(diff_mm.sem, diff_mm.at(it, 2 * NG))
                act.wait_ge(e_mm.sem, e_mm.at(it, NG))
                act.wait_ge(dend_ok.sem, dend_ok.at(it, NB))
                nc.scalar.activation(cum_r[0:NH, :], cum, ACT.Copy).then_inc(cum_hi.sem, 1)
                act.wait_ge(hm_mm.sem, hm_mm.at(it, 1))
                nc.scalar.activation(hm[2 * NH:, :], cum, ACT.Copy, scale=-1.0).then_inc(cum_hi.sem, 1)
                act.wait_ge(wd_ok.sem, wd_ok.at(n, 1))
                nc.scalar.activation(wd, wd, ACT.Exp).then_inc(we_ok.sem, 1)
                act.wait_ge(share.sem, share.at(n, 3))
                nc.scalar.activation(feat[0:DS, :], rms_a[0:DS, :], ACT.Copy).then_inc(top_ok.sem, 1)
                for k, (bank, dst) in enumerate(((dA, bshare), (dB, cshare))):
                    act.wait_ge(dup_mm.sem, dup_mm.at(n, k + 2))
                    nc.scalar.activation(dst[:, :], bank[:, :], ACT.Copy).then_inc(base_ok.sem, 1)
                act.wait_ge(hm_mm.sem, hm_mm.at(n, 1))
                act.wait_ge(xs_ok.sem, xs_ok.at(it, 2 * NG))
                act.wait_ge(exp_ok.sem, exp_ok.at(it, 2 * NG))
                nc.scalar.activation(gw[:, :, :], gp0[:, 0:NB * 3 * NH].rearrange("p (b h) -> p b h", b=NB),
                                     ACT.Copy).then_inc(gw_ok.sem, 1)
                act.wait_ge(dend_mm.sem, dend_mm.at(n, 1))
                act.wait_ge(faded.sem, faded.at(it, NG))
                for j in range(2):
                    r = slice(DS * j, DS * j + DS)
                    nc.scalar.activation(dec[r, :, :], gp1[r, 0:NB * NH].rearrange("p (b q j) -> p b q j", b=NB, j=2)[:, :, :, j],
                                         ACT.Exp).then_inc(dec_ok.sem, 1)
                act.wait_ge(ft_mm.sem, ft_mm.at(n, 1))
                act.wait_ge(f_mm.sem, f_mm.at(it, NG))
                nc.scalar.activation(feat_t[:, :, :], cB[:, 0:NB * NF].rearrange("p (b f) -> p b f", b=NB),
                                     ACT.Copy).then_inc(ft_ok.sem, 1)
                x_out(n, 0)
                exp_diff(n, 1)
                e_out(n, 0)
                act.wait_ge(share.sem, share.at(n, 3))
                sigmoid(n, 0)

            loop(act, main, tail)

        @block.vector
        def _(dve):
            for k in range(KD):
                dve.wait_ge(stage_in[k], 16)
                nc.vector.tensor_reduce(scales[:, 4 + k:5 + k], stage[k], AX_X, ALU.max,
                                        apply_absolute_value=True).then_inc(absmax_done, 1)
            dve.wait_ge(absmax_done, KD)
            nc.vector.tensor_reduce(scales[:, 8:9], scales[:, 4:8], AX_X, ALU.max).then_inc(scale_done, 1)
            dve.wait_ge(loaded, 16 * n_loads)
            nc.vector.tensor_tensor(mh[:, :, :], mh[:, :, :], const("mmask", slice(0, NF)).unsqueeze(1).broadcast_to([NF, NH, DS]),
                                    ALU.mult).then_inc(mh_done, 1)
            dve.wait_ge(mh_done, 1)
            nc.vector.tensor_tensor(mh[:, :, :], mh[:, :, :], const("mone", slice(0, NF)).unsqueeze(1).broadcast_to([NF, NH, DS]),
                                    ALU.add).then_inc(mh_done, 1)
            nc.vector.tensor_copy(ind_r[:, :], const("ind", slice(0, 64))).then_inc(ind_ready, 1)
            nc.vector.tensor_copy(ind_ch[:, :, :], const("ind", slice(0, 64)).unsqueeze(2).broadcast_to([64, NH, HD])).then_inc(ind_ready, 1)
            nc.vector.tensor_scalar(ones_r[:, :], const("ident", slice(0, 64)), 0.0, 1.0, ALU.mult, ALU.add).then_inc(ind_ready, 1)
            nc.vector.memset(feat[96:128, :], 1.0).then_inc(ind_ready, 1)
            dve.wait_ge(allmax_done, 1)
            nc.vector.tensor_scalar(scales[:, 10:11].bitcast(I32), scales[:, 9:10].bitcast(I32), 0x7F800000, None,
                                    ALU.bitwise_and).then_inc(scale_done, 1)
            dve.wait_ge(scale_done, 2)
            nc.vector.tensor_scalar(scales[:, 11:12].bitcast(I32), scales[:, 10:11].bitcast(I32), -1.0, float(254 << 23),
                                    ALU.mult, ALU.add).then_inc(scale_done, 1)
            dve.wait_ge(scale_done, 3)
            nc.vector.tensor_scalar(w_scale, scales[:, 11:12], W_SCALE, None, ALU.mult).then_inc(scale_done, 1)
            undo = 1.0 / (XN_SCALE * W_SCALE)
            nc.vector.tensor_scalar(ds_col, scales[:, 10:11], undo, None, ALU.mult).then_inc(scale_done, 1)
            nc.vector.tensor_scalar(nds_col, scales[:, 10:11], -undo, None, ALU.mult).then_inc(scale_done, 1)
            nc.vector.tensor_scalar(wds_col, scales[:, 10:11], undo, col("normw"), ALU.mult, ALU.mult).then_inc(scale_done, 1)
            dve.wait_ge(scale_done, 7)
            for k in range(KD):
                dve.wait_ge(hi_done, k + 1)
                nc.vector.scalar_tensor_tensor(out=w_lo[:, k, :], in0=stage[k], scalar=w_scale, in1=w_hi[:, k, :],
                                               op0=ALU.mult, op1=ALU.subtract).then_inc(lo_done, 1)

            def statistics(n, entries):
                dve.wait_ge(u_in.sem, u_in.at(n, 1))
                for b in entries:
                    nc.vector.bn_stats(stats[:, b, :], xn[:, b, :]).then_inc(bn1.sem, 1)
                for b in entries:
                    dve.wait_ge(bn1.sem, bn1.at(n, b + 1))
                    dve.sem_inc(dve_step, 1)
                    nc.vector.bn_aggr(mv[:, b, :], stats[:, b, :]).then_inc(bn2.sem, 1)

            def refine(n):
                dve.wait_ge(rstd0.sem, rstd0.at(n, 1))
                nc.vector.tensor_tensor(nt[:, 2, :], nt[:, 1, :], nt[:, 1, :], ALU.mult).then_inc(newton.sem, 1)
                dve.wait_ge(newton.sem, newton.at(n, 1))
                nc.vector.scalar_tensor_tensor(out=nt[:, 3, :], in0=mv[:, :, 1], scalar=col("eps"), in1=nt[:, 2, :],
                                               op0=ALU.add, op1=ALU.mult).then_inc(newton.sem, 1)
                dve.wait_ge(newton.sem, newton.at(n, 2))
                nc.vector.tensor_scalar(nt[:, 4, :], nt[:, 3, :], -0.5 * XN_SCALE, 1.5 * XN_SCALE, ALU.mult, ALU.add).then_inc(newton.sem, 1)
                dve.wait_ge(newton.sem, newton.at(n, 3))
                nc.vector.tensor_tensor(nt[:, 0, :], nt[:, 4, :], nt[:, 1, :], ALU.mult).then_inc(newton.sem, 1)

            def norm(n, entries):
                dve.wait_ge(newton.sem, newton.at(n, 4))
                for b in entries:
                    nc.vector.tensor_scalar(xn[:, b, :], xn[:, b, :], mv[:, b, 0:1], nt[:, 0, b:b + 1],
                                            ALU.subtract, ALU.mult).then_inc(normed.sem, 1)

            def low_half(n, k):
                dve.wait_ge(hi_ok.sem, hi_ok.at(n, k + 1))
                nc.vector.tensor_tensor(x_lo[:, k, :], xt_bank[k][:, :], x_hi[:, k, :], ALU.subtract).then_inc(lo_ok.sem, 1)

            def heads(it, g, q):
                slot, pair = g % 2, 2 * g + q
                if q == 0:
                    dve.wait_ge(y_mm.sem, y_mm.at(it, 2 * g - 2))
                for which, (dst, base, ca, cb) in enumerate(((bh, bshare, "cA_B", "cB_B"), (ch, cshare, "cA_C", "cB_C"))):
                    k = 4 * g + 2 * q + which + 1
                    nc.vector.scalar_tensor_tensor(out=dst[:, slot, q, :], in0=cosx[:, :], scalar=col(ca, pair),
                                                   in1=base[:, :], op0=ALU.mult, op1=ALU.add).then_inc(h1_ok.sem, 1)
                    dve.wait_ge(h1_ok.sem, h1_ok.at(it, k))
                    nc.vector.scalar_tensor_tensor(out=dst[:, slot, q, :], in0=sinx[:, :], scalar=col(cb, pair),
                                                   in1=dst[:, slot, q, :], op0=ALU.mult, op1=ALU.add).then_inc(h2_ok.sem, 1)

            def scale_x(it, g):
                dve.wait_ge(tr_mm.sem, tr_mm.at(it, g + 1))
                dve.wait_ge(f_mm.sem, f_mm.at(it, g - 1))
                dve.wait_ge(gw_ok.sem, gw_ok.at(it, 1))
                src = gp0[:, :].rearrange("p (b h d) -> p b h d", b=NB, h=HG)
                for i in range(2):
                    w = gw[:, :, i * NH + g * HG:i * NH + (g + 1) * HG].unsqueeze(3).broadcast_to([P, NB, HG, HD])
                    nc.vector.tensor_tensor(xs[:, g % 2, i].rearrange("p b (h d) -> p b h d", h=HG), src, w,
                                            ALU.mult).then_inc(xs_ok.sem, 1)

            def silu(it, g):
                dve.wait_ge(sig_ok.sem, sig_ok.at(it, 3 * g + 3))
                dve.wait_ge(y_ok.sem, y_ok.at(it, g - 1))
                nc.vector.scalar_tensor_tensor(out=gate[:, g % 2, :], in0=gp1[:, :], scalar=ds_col, in1=sig[:, :],
                                               op0=ALU.mult, op1=ALU.mult).then_inc(gate_ok.sem, 1)

            def scores(it, n):
                dve.wait_ge(cb_mm.sem, cb_mm.at(it, n))
                dve.wait_ge(mask_ok.sem, mask_ok.at(it, n))
                for j in range(2):
                    v = decay[:, (n - 1) % 2, j].rearrange("p b q t -> p (b q t)")
                    m = nc.vector.tensor_tensor(v, cbank[j][:, :], v, ALU.mult)
                m.then_inc(s_mul.sem, 1)

            def combine(it, g, i):
                n = 2 * g + i + 1
                half = slice(i * 256, i * 256 + 256)
                dve.wait_ge(y_mm.sem, y_mm.at(it, n))
                dve.wait_ge(e_ok.sem, e_ok.at(it, g + 1))
                if i == 0:
                    dve.wait_ge(ysum_ok.sem, ysum_ok.at(it, g))
                nc.vector.tensor_tensor(yc[:, half], ybank[i][:, 256:512], ecum[:, g % 2, half], ALU.mult).then_inc(t1_ok.sem, 1)
                dve.wait_ge(t1_ok.sem, t1_ok.at(it, n))
                nc.vector.tensor_tensor(yc[:, half], ybank[i][:, 0:256], yc[:, half], ALU.add).then_inc(yc_ok.sem, 1)

            def update_state(it, g):
                dve.wait_ge(h_mm.sem, h_mm.at(it, g + 1))
                dve.wait_ge(faded.sem, faded.at(it, g + 1))
                s = state[:, 2 * g:2 * g + 2].rearrange("p q b d -> p (q b d)")
                nc.vector.tensor_tensor(s, gp1[:, 0:256], s, ALU.add).then_inc(state_ok.sem, 1)

            def hidden(it, j):
                dve.wait_ge(relu_ok.sem, relu_ok.at(it, j + 1))
                if j == 0:
                    dve.wait_ge(out_mm.sem, out_mm.at(it, 0))
                    nc.vector.tensor_scalar(acc[:, :], relu[:, 0, :], col("W2", 0), col("b2"), ALU.mult, ALU.add).then_inc(acc_ok.sem, 1)
                else:
                    dve.wait_ge(acc_ok.sem, acc_ok.at(it, j))
                    nc.vector.scalar_tensor_tensor(out=acc[:, :], in0=relu[:, j % 2, :], scalar=col("W2", j), in1=acc[:, :],
                                                   op0=ALU.mult, op1=ALU.add).then_inc(acc_ok.sem, 1)

            dve.wait_ge(lo_done, KD)

            def main(it, pre):
                for g in range(NG):
                    scores(it, 2 * g + 1)
                    if g:
                        update_state(it, g - 1)
                    if g + 1 < NG:
                        heads(it, g + 1, 0)
                    elif pre:
                        low_half(it + 1, 0)
                    combine(it, g, 0)
                    hidden(it, 2 * g)
                    hidden(it, 2 * g + 1)
                    scores(it, 2 * g + 2)
                    if g + 1 < NG:
                        scale_x(it, g + 1)
                        heads(it, g + 1, 1)
                    elif pre:
                        for k in range(1, KD):
                            low_half(it + 1, k)
                    if NG - 5 <= g < NG - 3 and pre:
                        b = 2 * (g - NG + 5)
                        statistics(it + 1, range(b, b + 2))
                    if NG - 3 <= g < NG - 1 and pre:
                        b = 2 * (g - NG + 3)
                        if b == 0:
                            refine(it + 1)
                        norm(it + 1, range(b, b + 2))
                    combine(it, g, 1)
                    if g + 1 < NG:
                        silu(it, g + 1)

            def out_sum(it, b):
                dve.wait_ge(out_mm.sem, out_mm.at(it, b + 1))
                dve.wait_ge(res_ok.sem, res_ok.at(it, b + 1))
                nc.vector.tensor_tensor(res[:, b % 2, :], ybank[b % 2][:, :], res[:, b % 2, :], ALU.add).then_inc(out_ok.sem, 1)

            def tail(it, outs, pre):
                n = it + 1
                if outs and not pre:
                    update_state(it, NG - 1)
                    for b in range(NB):
                        out_sum(it, b)
                    return
                if not outs:
                    statistics(n, range(NB))
                    refine(n)
                    norm(n, range(NB))
                    for k in range(KD):
                        low_half(n, k)
                if outs:
                    update_state(it, NG - 1)
                dve.wait_ge(dta_mm.sem, dta_mm.at(n, 1))
                nc.vector.tensor_scalar(th, gp0[96:128, :], scales[96:128, 0:1], col("phase", 0, slice(96, 128)),
                                        ALU.mult, ALU.add).then_inc(angle.sem, 1)
                dve.wait_ge(angle.sem, angle.at(n, 1))
                nc.vector.tensor_scalar(kr, th, 1 / (2 * np.pi), MAGIC, ALU.mult, ALU.add).then_inc(angle.sem, 1)
                dve.wait_ge(angle.sem, angle.at(n, 2))
                nc.vector.tensor_scalar(kk, kr, MAGIC, -TWO_PI_HI, ALU.subtract, ALU.mult).then_inc(angle.sem, 1)
                dve.wait_ge(angle.sem, angle.at(n, 3))
                nc.vector.tensor_tensor(th, th, kk, ALU.add).then_inc(angle.sem, 1)
                nc.vector.tensor_scalar(kr, kr, MAGIC, -TWO_PI_LO, ALU.subtract, ALU.mult).then_inc(angle.sem, 1)
                dve.wait_ge(angle.sem, angle.at(n, 5))
                nc.vector.tensor_tensor(th, th, kr, ALU.add).then_inc(angle.sem, 1)
                dve.wait_ge(angle.sem, angle.at(n, 6))
                nc.vector.tensor_scalar(th, th, SIN_MAX, -SIN_MAX, ALU.min, ALU.max).then_inc(angle.sem, 1)
                dve.wait_ge(soft.sem, soft.at(n, 3))
                dve.wait_ge(y_mm.sem, y_mm.at(it, 2 * NG))
                nc.vector.scalar_tensor_tensor(out=dt_, in0=xb[0:NH], scalar=0.0, in1=lg[0:NH], op0=ALU.max,
                                               op1=ALU.add).then_inc(dt_ok.sem, 1)
                nc.vector.scalar_tensor_tensor(out=av, in0=xb[NH:64], scalar=0.0, in1=lg[NH:64], op0=ALU.max,
                                               op1=ALU.add).then_inc(dt_ok.sem, 1)
                dve.wait_ge(dt_ok.sem, dt_ok.at(n, 2))
                nc.vector.scalar_tensor_tensor(out=av, in0=av, scalar=A_FLOOR, in1=dt_, op0=ALU.max,
                                               op1=ALU.mult).then_inc(decay_rate.sem, 1)
                dve.wait_ge(trap_e.sem, trap_e.at(n, 3))
                nc.vector.tensor_scalar(gg, tr2, -0.5, 1.0, ALU.mult, ALU.add).then_inc(trap.sem, 1)
                nc.vector.tensor_scalar(tr2, tr2, 0.5, A_LEAST, ALU.mult, ALU.max).then_inc(trap.sem, 1)
                dve.wait_ge(trap.sem, trap.at(n, 2))
                dve.wait_ge(hm_mm.sem, hm_mm.at(it, 1))
                nc.vector.tensor_tensor(hm[0:NH, :], gg, dt_, ALU.mult).then_inc(gdt_ok.sem, 1)
                dve.wait_ge(ea_ok.sem, ea_ok.at(n, 1))
                nc.vector.tensor_tensor(av, av, gg, ALU.mult).then_inc(a_ok.sem, 1)
                dve.wait_ge(a_ok.sem, a_ok.at(n, 1))
                nc.vector.tensor_tensor(av, av, tr2, ALU.add).then_inc(a_ok.sem, 1)
                dve.wait_ge(rms_ok.sem, rms_ok.at(n, 1))
                nc.vector.scalar_tensor_tensor(out=rms_a[:, :], in0=gp1[:, :], scalar=wds_col, in1=rms_b[:, :],
                                               op0=ALU.mult, op1=ALU.mult).then_inc(bcn_ok.sem, 1)
                dve.wait_ge(lna_ok.sem, lna_ok.at(n, 1))
                for b in range(NB):
                    nc.vector.tensor_tensor_scan(cum[:, b * T:(b + 1) * T], ones_r[0:NH, :].bitcast(F32), av[:, b * T:(b + 1) * T],
                                                 0.0, ALU.mult, ALU.add).then_inc(cum_ok.sem, 1)
                dve.wait_ge(cum_ok.sem, cum_ok.at(n, NB))
                cum_b = cum.rearrange("p (b t) -> p b t", b=NB)
                nc.vector.tensor_tensor(wd.rearrange("p (b t) -> p b t", b=NB), cum_b[:, :, T - 1:T].broadcast_to([NH, NB, T]),
                                        cum_b, ALU.subtract).then_inc(wd_ok.sem, 1)
                dve.wait_ge(cos_ok.sem, cos_ok.at(n, 1))
                nc.vector.tensor_tensor(rms_b[:, :], rms_a[:, :], cosx[:, :], ALU.mult).then_inc(share.sem, 1)
                dve.wait_ge(cum_hi.sem, cum_hi.at(n, 1))
                nc.vector.tensor_tensor(cum_r[NH:64, :], cum, cum_r[0:NH, :].bitcast(F32), ALU.subtract).then_inc(cum_lo.sem, 1)
                dve.wait_ge(sinx_ok.sem, sinx_ok.at(n, 1))
                dve.wait_ge(dup_mm.sem, dup_mm.at(n, 1))
                nc.vector.tensor_tensor(bshare[:, :], cB[:, :], sinx[:, :], ALU.mult).then_inc(share.sem, 1)
                dve.wait_ge(share.sem, share.at(n, 2))
                nc.vector.tensor_tensor(rms_a[:, :], bshare[:, :], rms_b[:, :], ALU.add).then_inc(share.sem, 1)
                dve.wait_ge(cum_lo.sem, cum_lo.at(n, 1))
                dve.wait_ge(dend_mm.sem, dend_mm.at(it, 1))
                for b in range(NB):
                    nc.vector.tensor_scalar(dend_r[:, b, :], ind_r[:, :].bitcast(F32),
                                            cum_r[:, (b + 1) * T - 1:(b + 1) * T].bitcast(F32), None, ALU.mult).then_inc(dend_ok.sem, 1)
                dve.wait_ge(we_ok.sem, we_ok.at(n, 1))
                dve.wait_ge(gdt_ok.sem, gdt_ok.at(n, 1))
                nc.vector.tensor_tensor(hm[NH:64, :], wd, hm[0:NH, :], ALU.mult).then_inc(hm_ok.sem, 1)
                if outs:
                    out_sum(it, 0)
                dve.wait_ge(base_ok.sem, base_ok.at(n, 2))
                heads(n, 0, 0)
                heads(n, 0, 1)
                if outs:
                    out_sum(it, 1)
                    out_sum(it, 2)
                scale_x(n, 0)
                if outs:
                    out_sum(it, 3)
                silu(n, 0)

            loop(dve, main, tail)

        @block.tensor
        def _(pe):
            mm = nc.tensor.matmul

            def project(bank, c0):
                for k in range(KD):
                    for i, (w, x) in enumerate(((w_hi, x_hi), (w_hi, x_lo), (w_lo, x_hi))):
                        m = mm(bank[:, :], w[:, k, c0:c0 + P], x[:, k, :], start=(k == 0 and i == 0),
                               stop=(k == KD - 1 and i == 2))
                return m

            def diff(it, n):
                g, i = (n - 1) // 2, (n - 1) % 2
                if g == 0 and i == 0:
                    pe.wait_ge(cum_lo.sem, cum_lo.at(it, 1))
                    pe.wait_ge(base_ok.sem, base_ok.at(it, 2))
                pe.wait_ge(exp_ok.sem, exp_ok.at(it, n - 1))
                tok = 2 * i * T
                for j in range(2):
                    for q in range(2):
                        h = g * HG + 2 * q + j
                        m = mm(dbank[j][:, q * 256:q * 256 + 256], ind_r[:, h:h + 1].broadcast_to([64, P]), cum_r[:, tok:tok + 256],
                               start=True, stop=True, skip_group_check=True)
                m.then_inc(diff_mm.sem, 1)

            def products(it, n):
                g, i = (n - 1) // 2, (n - 1) % 2
                pe.wait_ge(s_mul.sem, s_mul.at(it, n - 1))
                if i == 0:
                    pe.wait_ge(e_ok.sem, e_ok.at(it, g + 1))
                    pe.wait_ge(h2_ok.sem, h2_ok.at(it, 4 * g + 4))
                    pe.wait_ge(ft_ok.sem, ft_ok.at(it, 1))
                for b in range(2):
                    for q in range(2):
                        for j in range(2):
                            r = slice(DS * j, DS * j + DS)
                            tok = (2 * i + b) * T
                            m = mm(cbank[j][:, (2 * b + q) * T:(2 * b + q + 1) * T], bh[r, g % 2, q, tok:tok + T],
                                   ch[r, g % 2, q, tok:tok + T], start=True, stop=True, skip_group_check=True)
                m.then_inc(cb_mm.sem, 1)

            def outputs(it, n):
                g, i = (n - 1) // 2, (n - 1) % 2
                pe.wait_ge(s_mul.sem, s_mul.at(it, n))
                if g == 0:
                    pe.wait_ge(out_ok.sem, out_ok.at(it, i - 1))
                else:
                    pe.wait_ge(yc_ok.sem, yc_ok.at(it, n - 2))
                pe.wait_ge(xs_ok.sem, xs_ok.at(it, 2 * g + 1))
                pe.wait_ge(state_ok.sem, state_ok.at(it, g + 1 - NG))
                for b in range(2):
                    for h in range(HG):
                        q, j = h // 2, h % 2
                        tok = 2 * i + b
                        rows = slice(HD * h, HD * h + HD)
                        r = slice(DS * j, DS * j + DS)
                        mm(ybank[i][rows, b * T:(b + 1) * T], xs[:, g % 2, 0, tok, rows],
                           decay[:, i, j, b, q, :], start=True, stop=True, skip_group_check=True)
                        m = mm(ybank[i][rows, 256 + b * T:256 + (b + 1) * T], state[r, 2 * g + q, tok, :],
                               ch[r, g % 2, q, tok * T:(tok + 1) * T], start=True, stop=True, skip_group_check=True)
                m.then_inc(y_mm.sem, 1)

            def turn_x(it, g):
                pe.wait_ge(xt_ok.sem, xt_ok.at(it, g + 1))
                for b in range(NB):
                    m = nc.tensor.transpose(gp0[:, b * P:(b + 1) * P], x_t[:, g % 2, b * T:(b + 1) * T], const("ident"))
                m.then_inc(tr_mm.sem, 1)

            def spread_cum(it, g):
                if g == 0:
                    pe.wait_ge(sinx_ok.sem, sinx_ok.at(it, 1))
                pe.wait_ge(s_mul.sem, s_mul.at(it, 2 * g))
                mm(cA[:, :], ind_ch[:, g * HG:(g + 1) * HG, :].rearrange("p h d -> p (h d)"), cum_r[:, :],
                   start=True, stop=True).then_inc(e_mm.sem, 1)

            def to_heads(it, g):
                pe.wait_ge(fs_ok.sem, fs_ok.at(it, g + 1))
                for h in range(HG):
                    q, j = h // 2, h % 2
                    m = mm(gp1[DS * j:DS * j + DS, q * 128:q * 128 + 128].rearrange("p (b d) -> p b d", b=NB),
                           mh[:, g * HG + h, :], fs[:, :, HD * h:HD * h + HD], start=True, stop=True, skip_group_check=True)
                m.then_inc(h_mm.sem, 1)

            def turn_u(n, k):
                pe.wait_ge(normed.sem, normed.at(n, NB))
                for b in range(NB):
                    m = nc.tensor.transpose(xt_bank[k][:, b * T:(b + 1) * T], xn[:, b, k * P:(k + 1) * P], const("ident"))
                m.then_inc(xt_mm.sem, 1)

            def main(it, pre):
                n = it + 1
                for g in range(NG):
                    products(it, 2 * g + 1)
                    diff(it, 2 * g + 2)
                    if g:
                        pe.wait_ge(gate_ok.sem, gate_ok.at(it, g + 1))
                        to_heads(it, g - 1)
                        pe.wait_ge(fs_ok.sem, fs_ok.at(it, g))
                    else:
                        pe.wait_ge(xs_ok.sem, xs_ok.at(it, 2))
                    if g + 1 < NG:
                        project(gp0, (g + 1) * P).then_inc(x_mm.sem, 1)
                    elif pre:
                        turn_u(n, 0)
                    outputs(it, 2 * g + 1)
                    products(it, 2 * g + 2)
                    if g + 1 < NG:
                        turn_x(it, g + 1)
                        diff(it, 2 * g + 3)
                    if g:
                        pe.wait_ge(state_ok.sem, state_ok.at(it, g))
                    else:
                        pe.wait_ge(gate_ok.sem, gate_ok.at(it, 1))
                    if g + 1 < NG:
                        project(gp1, DI + (g + 1) * P).then_inc(z_mm.sem, 1)
                        spread_cum(it, g + 1)
                    elif pre:
                        pe.wait_ge(exp_ok.sem, exp_ok.at(it, 2 * NG))
                        for k in range(1, KD):
                            turn_u(n, k)
                    outputs(it, 2 * g + 2)
                    if g + 1 < NG:
                        pe.wait_ge(xs_ok.sem, xs_ok.at(it, 2 * g + 4))
                    elif pre:
                        pe.wait_ge(lo_ok.sem, lo_ok.at(n, 1))
                    pe.wait_ge(ft_ok.sem, ft_ok.at(it, 1))
                    for b in range(NB):
                        m = mm(gp0[0:NF, b * P:(b + 1) * P], feat_t[:, b, :], xs[:, g % 2, 1, b, :], start=True,
                               stop=True, skip_group_check=True)
                    m.then_inc(f_mm.sem, 1)

            def project_out(it, b, half):
                bank, tok = ybank[b % 2], b * T
                if half == 0:
                    pe.wait_ge(y_ok.sem, y_ok.at(it, NG // 2))
                    if b < 2:
                        pe.wait_ge(yc_ok.sem, yc_ok.at(it, 2 * NG - 1 + b))
                    else:
                        pe.wait_ge(out_ok.sem, out_ok.at(it, b - 1))
                    for k in range(NG // 2):
                        mm(bank[:, :], y[:, k, tok:tok + T], wo[:, k, :], start=(k == 0), stop=False)
                else:
                    pe.wait_ge(y_ok.sem, y_ok.at(it, NG))
                    pe.wait_ge(acc_ok.sem, acc_ok.at(it, INNER))
                    for k in range(NG // 2, NG):
                        mm(bank[:, :], y[:, k, tok:tok + T], wo[:, k, :], start=False, stop=False)
                    r = slice(MID * (b // 2), MID * (b // 2) + MID)
                    mm(bank[:, :], acc[r, (b % 2) * T:(b % 2 + 1) * T], wf[r, :], start=False, stop=True).then_inc(out_mm.sem, 1)

            def tail(it, outs, pre):
                n = it + 1
                if not pre:
                    to_heads(it, NG - 1)
                    for b in range(NB):
                        project_out(it, b, 0)
                        project_out(it, b, 1)
                    return
                if outs:
                    pe.wait_ge(lo_ok.sem, lo_ok.at(n, 2))
                    to_heads(it, NG - 1)
                    pe.wait_ge(fs_ok.sem, fs_ok.at(it, NG))
                else:
                    for k in range(KD):
                        turn_u(n, k)
                pe.wait_ge(lo_ok.sem, lo_ok.at(n, KD))
                project(gp0, C_DTA).then_inc(dta_mm.sem, 1)
                pe.wait_ge(state_ok.sem, state_ok.at(it, NG))
                project(gp1, C_BC).then_inc(bc_mm.sem, 1)
                project(dA, C_FFN).then_inc(ffn_mm.sem, 1)
                pe.wait_ge(sq_ok.sem, sq_ok.at(n, 1))
                mm(dB[:, :], const("mean"), rms_a[:, :], start=True, stop=True).then_inc(ms_mm.sem, 1)
                if outs:
                    project_out(it, 0, 0)
                pe.wait_ge(sin_ok.sem, sin_ok.at(n, 1))
                pe.wait_ge(xb_ok.sem, xb_ok.at(n, 1))
                pe.wait_ge(trap_e.sem, trap_e.at(n, 1))
                pe.wait_ge(angle.sem, angle.at(n, 1))
                pe.wait_ge(s_mul.sem, s_mul.at(it, 2 * NG))
                r = slice(DS, DS + 2 * ROPE)
                mm(gp0[:, :], const("selcos", r), feat[r, :], start=True, stop=True).then_inc(cos_mm.sem, 1)
                mm(cA[:, :], const("selsin", r), feat[r, :], start=True, stop=True).then_inc(sin_mm.sem, 1)
                if outs:
                    project_out(it, 0, 1)
                pe.wait_ge(bcn_ok.sem, bcn_ok.at(n, 1))
                mm(cB[:, :], const("swap"), rms_a[:, :], start=True, stop=True).then_inc(dup_mm.sem, 1)
                if outs:
                    project_out(it, 1, 0)
                pe.wait_ge(s_ok.sem, s_ok.at(n, 2))
                pe.wait_ge(ms_ln.sem, ms_ln.at(n, 1))
                pe.wait_ge(share.sem, share.at(n, 3))
                for bank, name in ((dA, "dupB"), (dB, "dupC")):
                    mm(bank[:, :], const(name), rms_a[:, :], start=True, stop=True).then_inc(dup_mm.sem, 1)
                if outs:
                    project_out(it, 1, 1)
                pe.wait_ge(dend_ok.sem, dend_ok.at(n, NB))
                mm(gp1[:, 0:NB * NH], ones_r[:, :], dend_r[:, :, :].rearrange("p b h -> p (b h)"), start=True,
                   stop=True).then_inc(dend_mm.sem, 1)
                pe.wait_ge(cos_ok.sem, cos_ok.at(n, 1))
                pe.wait_ge(cum_hi.sem, cum_hi.at(n, 2))
                pe.wait_ge(hm_ok.sem, hm_ok.at(n, 1))
                for b in range(NB):
                    m = nc.tensor.transpose(gp0[:, b * 96:(b + 1) * 96], hm[:, b * T:(b + 1) * T], const("ident", slice(0, 96))[:, 0:96])
                m.then_inc(hm_mm.sem, 1)
                pe.wait_ge(top_ok.sem, top_ok.at(n, 1))
                for b in range(NB):
                    m = nc.tensor.transpose(cB[:, b * NF:(b + 1) * NF], feat[0:NF, b * T:(b + 1) * T],
                                            const("ident", slice(0, NF))[:, 0:NF])
                m.then_inc(ft_mm.sem, 1)
                if outs:
                    project_out(it, 2, 0)
                diff(n, 1)
                spread_cum(n, 0)
                if outs:
                    project_out(it, 2, 1)
                pe.wait_ge(gw_ok.sem, gw_ok.at(n, 1))
                project(gp0, 0).then_inc(x_mm.sem, 1)
                if outs:
                    project_out(it, 3, 0)
                turn_x(n, 0)
                if outs:
                    project_out(it, 3, 1)
                pe.wait_ge(dec_ok.sem, dec_ok.at(n, 2))
                project(gp1, DI).then_inc(z_mm.sem, 1)

            pe.wait_ge(loaded, 16 * n_loads)
            pe.wait_ge(ind_ready, 4)
            pe.wait_ge(mh_done, 2)
            pe.wait_ge(lo_done, KD)
            pe.wait_ge(st_zero, 1)
            loop(pe, main, tail)


_OUTS = [((4, 4096, DM), 'float32')]


def layout(inp):
    i = {k: np.asarray(v) for k, v in inp.items()}
    w = i["L0_attn_W_in"]
    o = 2 * DI
    z, x, bc, dta, ang = w[0:DI], w[DI:o], w[o:o + 2 * DS], w[o + 2 * DS:o + 2 * DS + 3 * NH], w[o + 2 * DS + 3 * NH:]
    ffn = i["L0_ffn_Win"].T
    w_in = np.concatenate([x, z, dta, ang, ang, bc, ffn, ffn]).T
    pcols = np.zeros((P, N_PCOLS), np.float32)
    part = {k: pcols[:, a:a + n] for k, (a, n) in PC.items()}
    part["normw"][:, 0] = np.concatenate([i["L0_attn_Bn_w"], i["L0_attn_Cn_w"]])
    part["dtbias"][0:NH, 0] = i["L0_attn_dt_bias"]
    part["phase"][96 + ROPE:, 0] = np.pi / 2
    part["onerow"][:, 0] = np.arange(P) % DS >= 2 * ROPE
    part["eps"][:] = EPS
    twice = lambda a: np.concatenate([a, a])
    part["bin"][:, 0] = twice(i["L0_ffn_bin_"])
    part["b2"][:, 0] = twice(i["L0_ffn_b2"])
    part["W1"][:], part["b1"][:], part["W2"][:] = (twice(i["L0_ffn_" + k]) for k in ("W1", "b1", "W2"))
    part["D"][:] = np.repeat(i["L0_attn_D"], HD).reshape(NG, P).T
    swap = np.arange(DS)
    swap[:2 * ROPE] = (swap[:2 * ROPE] + ROPE) % (2 * ROPE)
    for k, name in (("B", "L0_attn_B_bias"), ("C", "L0_attn_C_bias")):
        b = i[name].reshape(16, 2, DS)
        part["cA_" + k][:] = b.transpose(1, 2, 0).reshape(P, 16)
        part["cB_" + k][:] = b[:, :, swap].transpose(1, 2, 0).reshape(P, 16)
    mh_bias = np.stack([i["L0_attn_B_bias"][:, swap], i["L0_attn_B_bias"]])
    return {"u": i["L0_attn_u"], "w_in": w_in, "w_out": i["L0_attn_W_out"].T, "w_ffn": twice(i["L0_ffn_Wout"]),
            "pcols": pcols, "bout": i["L0_ffn_bout"][None, :], "mh_bias": mh_bias, "consts": constants()}


def kernel(**inputs):
    import concourse.bacc as _bacc
    from concourse.bass_utils import run_bass_kernel_spmd as _run

    nc = _bacc.Bacc("TRN2", target_bir_lowering=False, num_devices=1)
    arrays, args = {}, []
    for name, a in layout(inputs).items():
        a = np.ascontiguousarray(a)
        arrays[f"in_{name}_dram"] = a
        args.append(nc.dram_tensor(f"in_{name}_dram", a.shape, mybir.dt.from_np(a.dtype), kind="ExternalInput").ap())
    for i, (shape, dtype) in enumerate(_OUTS):
        args.append(nc.dram_tensor(f"out_{i}_dram", shape, mybir.dt.from_np(np.dtype(dtype)), kind="ExternalOutput").ap())
    mixer(nc, *args, n_iter=arrays["in_u_dram"].shape[1] // T)
    r = _run(nc, [arrays], core_ids=[0])
    return r.results[0]["out_0_dram"]
```

```python
from contextlib import ExitStack

import numpy as np

import concourse.bass as bass
from concourse import mybir

F32, F32R, F16, I32 = mybir.dt.float32, mybir.dt.float32r, mybir.dt.float16, mybir.dt.int32
ALU = mybir.AluOpType
ACT = mybir.ActivationFunctionType
AX_X = mybir.AxisListType.X
RMAX = bass.bass_isa.ReduceOp.max

P = 128
NB, T = 4, 128
TOK = NB * T
DM, KD = 512, 4
NH, HD, DS = 32, 32, 64
DI = NH * HD
HG = 4
NG = NH // HG
NS = NG - 1
NS_DVE = 4
ROPE = 16
MID, INNER = 64, 16
HIDDEN_UPTO = (2, 4, 6, 8, 10, 12, 14, INNER)
NF = DS + 2 * ROPE + 1
WCOLS = 2 * DI + 3 * P
C_DTA, C_BC, C_FFN = 2 * DI, 2 * DI + P, 2 * DI + 2 * P
A_FLOOR, EPS = 1e-4, 1e-5
XN_SCALE, W_SCALE = 256.0, 4096.0
MAGIC = 1.5 * 2.0**23
TWO_PI_HI, TWO_PI_LO = 6.28125, 2 * np.pi - 6.28125
SIN_MAX = 3.1415925
A_LEAST = 1e-18

PC = {}
for _name, _n in (("normw", 1), ("dtbias", 1), ("phase", 1), ("onerow", 1), ("eps", 1), ("bin", 1), ("b2", 1),
                  ("W1", INNER), ("b1", INNER), ("W2", INNER), ("D", NG),
                  ("cA_B", 16), ("cB_B", 16), ("cA_C", 16), ("cB_C", 16)):
    PC[_name] = (sum(n for _, n in PC.values()), _n)
N_PCOLS = sum(n for _, n in PC.values())

CC = {}
for _name, _n in (("ident", P), ("swap", P), ("mean", P),
                  ("selcos", P), ("selsin", P), ("ind", NH), ("mmask", DS), ("mone", DS)):
    CC[_name] = (sum(n for _, n in CC.values()), _n)
N_CONST = sum(n for _, n in CC.values())
N_KEEP = CC["selcos"][0]


def hidden_units(g):
    return range(HIDDEN_UPTO[g - 1] if g else 0, HIDDEN_UPTO[g])


def constants():
    c = np.zeros((P, N_CONST), np.float32)
    part = {k: c[:, a:a + n] for k, (a, n) in CC.items()}
    part["ident"][:] = np.eye(P)
    for m in range(P):
        n = m % DS
        part["mean"][m - n:m - n + DS, m] = 1 / DS
        if n < 2 * ROPE:
            part["swap"][m - n + (n + ROPE) % (2 * ROPE), m] = 1
            for half in (DS, DS + 2 * ROPE):
                part["selsin"][half + n % ROPE, m] = -1 if n < ROPE else 1
                part["selcos"][half + ROPE + n % ROPE, m] = 1
    for k in range(2 * NH):
        part["ind"][k, k % NH] = 1
    for i in range(ROPE):
        part["mmask"][DS + i, i] = -1
        part["mmask"][DS + i, ROPE + i] = 1
        part["mmask"][DS + ROPE + i, i] = 1
        part["mmask"][DS + ROPE + i, ROPE + i] = 1
    part["mmask"][NF - 1, 2 * ROPE:] = 1
    part["mone"][:DS] = np.eye(DS)
    return c


class Count:

    def __init__(self, sem, events, unit=1):
        self.sem, self.events, self.unit = sem, events, unit

    def at(self, it, k):
        return it * (self.events * self.unit) + k * self.unit


def mixer(nc, u, w_in, w_out, w_ffn, pcols, bout, mh_bias, consts, out, n_iter):
    with ExitStack() as ctx:
        def sb(name, shape, dt=F32):
            return ctx.enter_context(nc.sbuf_tensor(name, shape, dt))

        def sb_both(name, shape):
            with nc.sbuf_tensor(name + "_r", shape, F32R) as rounded:
                pass
            return sb(name, shape), rounded

        def sem(name):
            return ctx.enter_context(nc.semaphore(name))

        counts = []

        def count(name, events, unit=1):
            c = Count(sem(name), events, unit)
            counts.append(c)
            return c

        w_hi = sb("w_hi", [P, KD, WCOLS], F16)
        w_lo = sb("w_lo", [P, KD, WCOLS], F16)
        wo, wo_r = sb_both("wo", [P, NG, DM])
        wo_hi = sb("wo_hi", [P, NS, DM], F32R)
        wf, wf_r = sb_both("wf", [P, DM])
        wf_hi = sb("wf_hi", [P, DM], F32R)
        cst = sb("cst", [P, N_KEEP])
        sel_r = sb("sel_r", [P, 2, P], F32R)
        pc = sb("pc", [P, N_PCOLS])
        bout_bc = sb("bout_bc", [P, DM])
        mh = sb("mh", [NF, NH, DS])
        ind_r = sb("ind_r", [2 * NH, NH], F32R)
        ind_ch = sb("ind_ch", [2 * NH, NH, HD], F32R)
        ones_r = sb("ones_r", [2 * NH, P], F32R)
        scales = sb("scales", [P, 16])
        xn = sb("xn", [P, NB, DM])
        stats = sb("stats", [P, NB, 6])
        mv = sb("mv", [P, NB, 2])
        nt = sb("nt", [P, 5, NB])
        x_hi = sb("x_hi", [P, KD, TOK], F16)
        x_lo = sb("x_lo", [P, KD, TOK], F16)
        cum_r = sb("cum_r", [2 * NH, TOK], F32R)
        dend_r = sb("dend_r", [2 * NH, NB, NH], F32R)
        hm = sb("hm", [3 * NH, TOK])
        gw = sb("gw", [P, NB, 3 * NH])
        dec = sb("dec", [P, NB, NH // 2])
        cosx = sb("cosx", [P, TOK])
        sinx = sb("sinx", [P, TOK])
        bshare = sb("bshare", [P, TOK])
        cshare = sb("cshare", [P, TOK])
        feat = sb("feat", [P, TOK])
        feat_t = sb("feat_t", [P, NB, NF])
        s_mid = sb("s_mid", [P, TOK // 2])
        relu = sb("relu", [P, 2, TOK // 2])
        acc = sb("acc", [P, TOK // 2])
        arena, arena_r = sb_both("arena", [P, 24 * TOK])
        y_lo = arena_r[:, 0:8 * TOK].rearrange("p (g t) -> p g t", g=NG)
        y = arena[:, 0:8 * TOK].rearrange("p (g t) -> p g t", g=NG)
        bh = arena[:, 8 * TOK:12 * TOK].rearrange("p (s q t) -> p s q t", s=2, q=2)
        ch = arena[:, 12 * TOK:16 * TOK].rearrange("p (s q t) -> p s q t", s=2, q=2)
        y_hi = [arena_r[:, k * TOK:(k + 1) * TOK] for k in (20, 21, 10, 11, 14, 15, 22)]
        lt = arena[:, 16 * TOK:20 * TOK]
        decay = lt.rearrange("p (u j b q t) -> p u j b q t", u=2, j=2, b=2, q=2)
        xs = arena[:, 20 * TOK:24 * TOK].rearrange("p (s i b c) -> p s i b c", s=2, i=2, b=NB)
        x_t = sb("x_t", [P, 2, TOK])
        sig = sb("sig", [P, TOK])
        gate, gate_r = sb_both("gate", [P, 2, TOK])
        ecum = sb("ecum", [P, 2, TOK])
        yc = sb("yc", [P, TOK])
        dx = sb("dx", [P, TOK])
        fs = sb("fs", [NF, NB, P])
        state = sb("state", [P, NH // 2, NB, HD])
        res = sb("res", [P, 2, DM])

        rms_a, rms_b = yc, sig
        xb, lg = xn[0:64, 0, :], xn[0:64, 1, :]
        th, kr, kk = xn[64:96, 0, :], xn[64:96, 1, :], xn[64:96, 2, :]
        tr2, gg = xn[0:NH, 2, :], xn[0:NH, 3, :]
        dt_, av, cum, wd = (lt[0:NH, i * TOK:(i + 1) * TOK] for i in range(4))

        banks = [ctx.enter_context(nc.psum_tensor(f"bank{i}", [P, TOK], F32)) for i in range(8)]
        gp0, gp1, dA, dB, cA, cB, y0, y1 = banks
        dbank, cbank, ybank = (dA, dB), (cA, cB), (y0, y1)
        xt_bank = (gp0, gp1, dA, dB)

        def col(name, i=0, rows=slice(0, P)):
            a, _ = PC[name]
            return pc[rows, a + i:a + i + 1]

        def const(name, rows=slice(0, P)):
            a, n = CC[name]
            return cst[rows, a:a + n] if a < N_KEEP else bshare[rows, a - N_KEEP:a - N_KEEP + n]

        ds_col = scales[:, 0:1]
        w_scale = scales[:, 12:13]
        nds_col = scales[:, 1:2]
        wds_col = scales[:, 2:3]

        trig_r = arena_r[:, 23 * TOK:24 * TOK]
        acc_r = gate_r[:, 1, :].rearrange("p (s c) -> p s c", s=2)

        loaded, ind_ready, st_zero = sem("loaded"), sem("ind_ready"), sem("st_zero")
        stage_in = [sem(f"stage_in{k}") for k in range(KD)]
        absmax_done, allmax_done, scale_done = sem("absmax_done"), sem("allmax_done"), sem("scale_done")
        hi_done, lo_done, mh_done = sem("hi_done"), sem("lo_done"), sem("mh_done")
        wo_hi_done, wo_lo_done = sem("wo_hi_done"), sem("wo_lo_done")
        u_in = count("u_in", 1, 16)
        bn1, bn2 = count("bn1", NB), count("bn2", NB)
        var_ln, rstd0, newton, normed = count("var_ln", 1), count("rstd0", 1), count("newton", 4), count("normed", NB)
        xt_mm, hi_ok, lo_ok = count("xt_mm", KD), count("hi_ok", KD), count("lo_ok", KD)
        dta_mm, bc_mm, ffn_mm = count("dta_mm", 1), count("bc_mm", 1), count("ffn_mm", 1)
        xb_ok, soft, trap_e, trap = count("xb_ok", 1), count("soft", 3), count("trap_e", 3), count("trap", 2)
        angle, sin_ok, trig_hi, trig_lo = count("angle", 7), count("sin_ok", 1), count("trig_hi", 1), count("trig_lo", 1)
        dt_ok, decay_rate, ea_ok, a_ok, lna_ok = count("dt_ok", 2), count("decay_rate", 1), count("ea_ok", 1), count("a_ok", 2), count("lna_ok", 1)
        cum_ok, cum_hi, cum_lo = count("cum_ok", NB), count("cum_hi", 2), count("cum_lo", 1)
        wd_ok, we_ok, gdt_ok, hm_ok, hm_mm, gw_ok = count("wd_ok", 1), count("we_ok", 1), count("gdt_ok", 1), count("hm_ok", 1), count("hm_mm", 1), count("gw_ok", 1)
        dend_ok, dend_mm, dec_ok = count("dend_ok", NB), count("dend_mm", 1), count("dec_ok", 2)
        sq_ok, ms_mm, ms_ln, rms_ok, bcn_ok = count("sq_ok", 1), count("ms_mm", 1), count("ms_ln", 1), count("rms_ok", 1), count("bcn_ok", 1)
        cos_mm, sin_mm, cos_ok, sinx_ok = count("cos_mm", 1), count("sin_mm", 1), count("cos_ok", 1), count("sinx_ok", 1)
        base_ok, swap_mm, share, top_ok, ft_mm, ft_ok = count("base_ok", 2), count("swap_mm", 1), count("share", 4), count("top_ok", 1), count("ft_mm", 1), count("ft_ok", 1)
        s_ok, relu_ok, acc_ok = count("s_ok", 2), count("relu_ok", INNER), count("acc_ok", INNER)
        x_mm, z_mm, xt_ok, tr_mm, xs_ok = count("x_mm", NG), count("z_mm", NG), count("xt_ok", NG), count("tr_mm", NG), count("xs_ok", 2 * NG)
        sig_ok, gate_ok = count("sig_ok", 3 * NG), count("gate_ok", NG)
        h1_ok, h2_ok = count("h1_ok", 4 * NG), count("h2_ok", 4 * NG)
        diff_mm, cb_mm, exp_ok, mask_ok, s_mul = count("diff_mm", 2 * NG), count("cb_mm", 2 * NG), count("exp_ok", 2 * NG), count("mask_ok", 2 * NG), count("s_mul", 2 * NG)
        pool_step, dve_step, sp_step = sem("pool_step"), sem("dve_step"), sem("sp_step")
        y_mm, t1_ok, yc_ok = count("y_mm", 2 * NG), count("t1_ok", 2 * NG), count("yc_ok", 2 * NG)
        e_mm, e_ok = count("e_mm", NG), count("e_ok", NG)
        dx_ok, ysum_ok, y_ok = count("dx_ok", NG), count("ysum_ok", NG), count("y_ok", NG)
        f_mm, fs_ok, h_mm, faded, state_ok = count("f_mm", NG), count("fs_ok", NG), count("h_mm", NG), count("faded", NG), count("state_ok", NG)
        acc_hi, acc_lo = count("acc_hi", 2), count("acc_lo", 2)
        y_hi_ok, y_lo_dve, y_lo_pool = count("y_hi_ok", NS), count("y_lo_dve", NS_DVE), count("y_lo_pool", NS - NS_DVE)
        out_mm, res_ok, out_ok = count("out_mm", NB), count("res_ok", NB), count("out_ok", NB)
        res_in = [count(f"res_in{i}", 2, 16) for i in range(2)]
        stored = [count(f"stored{i}", 2, 16) for i in range(2)]

        def loop(eng, main, tail):
            tail(0, False, True)
            if n_iter > 1:
                with eng.Fori(1, n_iter) as it:
                    main(it, True)
                    tail(it, True, True)
            main(n_iter, False)
            tail(n_iter, True, False)

        u_chunk = u.rearrange("b (c t) d -> c t b d", t=T)
        out_chunk = out.rearrange("b (c t) d -> c t b d", t=T)
        w_in_k = w_in.rearrange("(k p) n -> k p n", p=P)
        n_loads = 9
        stage = [arena[:, k * WCOLS:(k + 1) * WCOLS] for k in range(KD)]

        block = ctx.enter_context(nc.Block())

        @block.sync
        def _(sp):
            for c in counts:
                sp.sem_inc(c.sem, c.events * c.unit)
            for k in range(KD):
                sp.dma_start(stage[k], w_in_k[k]).then_inc(stage_in[k], 16)
            sp.dma_start(cst[:, :], consts[:, 0:N_KEEP]).then_inc(loaded, 16)
            sp.dma_start(bshare[:, 0:N_CONST - N_KEEP], consts[:, N_KEEP:]).then_inc(loaded, 16)
            sp.dma_start(pc[:, :], pcols).then_inc(loaded, 16)
            sp.dma_start(bout_bc[:, :], bout.broadcast_to([P, DM])).then_inc(loaded, 16)
            sp.dma_start(mh[DS:DS + ROPE, :, :], mh_bias[0:1].broadcast_to([ROPE, NH, DS])).then_inc(loaded, 16)
            sp.dma_start(mh[DS + ROPE:NF, :, :], mh_bias[1:2].broadcast_to([ROPE + 1, NH, DS])).then_inc(loaded, 16)
            sp.dma_start(mh[0:DS, :, :], mh_bias[1:2].broadcast_to([DS, NH, DS])).then_inc(loaded, 16)
            sp.dma_start(wo[:, :, :], w_out.rearrange("(k p) n -> p k n", p=P)).then_inc(loaded, 16)
            sp.dma_start(wf[:, :], w_ffn).then_inc(loaded, 16)
            def load_u(n):
                sp.wait_ge(normed.sem, normed.at(n - 1, NB))
                sp.sem_inc(sp_step, 1)
                sp.wait_ge(xt_mm.sem, xt_mm.at(n - 1, KD))
                sp.sem_inc(sp_step, 1)
                sp.wait_ge(gdt_ok.sem, gdt_ok.at(n - 1, 1))
                sp.sem_inc(sp_step, 1)
                sp.wait_ge(a_ok.sem, a_ok.at(n - 1, 2))
                sp.sem_inc(sp_step, 1)
                sp.wait_ge(sin_ok.sem, sin_ok.at(n - 1, 1))
                sp.sem_inc(sp_step, 1)
                sp.dma_start(xn[:, :, :], u_chunk[n - 1]).then_inc(u_in.sem, 16)

            def main(it, pre):
                if pre:
                    load_u(it + 1)
                for b in range(2):
                    sp.wait_ge(stored[b].sem, stored[b].at(it, 0))
                    sp.sem_inc(sp_step, 1)
                    sp.dma_start(res[:, b, :], u_chunk[it - 1, :, b, :]).then_inc(res_in[b].sem, 16)

            def tail(it, outs, pre):
                if not outs:
                    load_u(1)
                    return
                for b in range(NB):
                    sp.wait_ge(out_ok.sem, out_ok.at(it, b + 1))
                    sp.sem_inc(sp_step, 1)
                    sp.dma_start(out_chunk[it - 1, :, b, :], res[:, b % 2, :]).then_inc(stored[b % 2].sem, 16)
                    if b < 2:
                        sp.wait_ge(stored[b].sem, stored[b].at(it, 1))
                        sp.sem_inc(sp_step, 1)
                        sp.dma_start(res[:, b, :], u_chunk[it - 1, :, b + 2, :]).then_inc(res_in[b].sem, 16)

            loop(sp, main, tail)
            for b in range(2):
                sp.wait_ge(stored[b].sem, stored[b].at(n_iter, 2))
                sp.sem_inc(sp_step, 1)

        @block.gpsimd
        def _(pool):
            pool.wait_ge(absmax_done, KD)
            pool.wait_ge(scale_done, 1)
            nc.gpsimd.partition_all_reduce(scales[:, 9:10], scales[:, 8:9], P, RMAX).then_inc(allmax_done, 1)
            nc.gpsimd.memset(state[:, :, :, :], 0.0).then_inc(st_zero, 1)
            pool.wait_ge(loaded, 16 * n_loads)
            nc.gpsimd.tensor_tensor(mh[:, :, :], mh[:, :, :], const("mmask", slice(0, NF)).unsqueeze(1).broadcast_to([NF, NH, DS]),
                                    ALU.mult).then_inc(mh_done, 1)
            pool.wait_ge(mh_done, 1)
            nc.gpsimd.tensor_tensor(mh[:, :, :], mh[:, :, :], const("mone", slice(0, NF)).unsqueeze(1).broadcast_to([NF, NH, DS]),
                                    ALU.add).then_inc(mh_done, 1)

            pool.wait_ge(wo_hi_done, 2)
            nc.gpsimd.tensor_tensor(wo_r[:, 0:NS, :], wo[:, 0:NS, :], wo_hi[:, :, :].bitcast(F32),
                                    ALU.subtract).then_inc(wo_lo_done, 1)
            nc.gpsimd.tensor_tensor(wf_r[:, :], wf[:, :], wf_hi[:, :].bitcast(F32), ALU.subtract).then_inc(wo_lo_done, 1)

            def mask(it, n):
                pool.wait_ge(exp_ok.sem, exp_ok.at(it, n))
                pool.sem_inc(pool_step, 1)
                v = decay[:, (n - 1) % 2].rearrange("p j b q t -> p (j b q) t")
                nc.gpsimd.affine_select(out=v, in_=v, compare_op=ALU.is_ge, fill=0.0, base=0,
                                        pattern=[[0, 8], [1, T]], channel_multiplier=-1).then_inc(mask_ok.sem, 1)

            def finish(it, g):
                pool.wait_ge(xt_ok.sem, xt_ok.at(it, g + 1))
                pool.wait_ge(y_ok.sem, y_ok.at(it, g))
                pool.sem_inc(pool_step, 1)
                nc.gpsimd.tensor_scalar(dx[:, :], x_t[:, g % 2, :], col("D", g), None, ALU.mult).then_inc(dx_ok.sem, 1)
                pool.wait_ge(dx_ok.sem, dx_ok.at(it, g + 1))
                pool.wait_ge(yc_ok.sem, yc_ok.at(it, 2 * g + 2))
                nc.gpsimd.tensor_tensor(dx[:, :], dx[:, :], yc[:, :], ALU.add).then_inc(ysum_ok.sem, 1)
                pool.wait_ge(ysum_ok.sem, ysum_ok.at(it, g + 1))
                pool.wait_ge(gate_ok.sem, gate_ok.at(it, g + 1))
                pool.wait_ge(out_mm.sem, out_mm.at(it, 0))
                nc.gpsimd.tensor_tensor(y[:, g, :], dx[:, :], gate[:, g % 2, :], ALU.mult).then_inc(y_ok.sem, 1)

            def main(it, pre):
                for g in range(NG):
                    if g:
                        finish(it, g - 1)
                    mask(it, 2 * g + 2)
                    if g + 1 < NG:
                        mask(it, 2 * g + 3)
                    pool.wait_ge(y_mm.sem, y_mm.at(it, 2 * g + 2))
                    pool.wait_ge(dec_ok.sem, dec_ok.at(it, 2))
                    pool.wait_ge(state_ok.sem, state_ok.at(it, g + 1 - NG))
                    s = state[:, 2 * g:2 * g + 2]
                    d = dec[:, :, 2 * g:2 * g + 2].rearrange("p b q -> p q b").unsqueeze(3).broadcast_to([P, 2, NB, HD])
                    nc.gpsimd.tensor_tensor(s, s, d, ALU.mult).then_inc(faded.sem, 1)
                finish(it, NG - 1)

            def tail(it, outs, pre):
                if not outs:
                    pool.wait_ge(st_zero, 1)
                else:
                    for k in range(NS_DVE, NS):
                        pool.wait_ge(y_hi_ok.sem, y_hi_ok.at(it, k + 1))
                        nc.gpsimd.tensor_tensor(y_lo[:, k, :], y[:, k, :], y_hi[k].bitcast(F32),
                                                ALU.subtract).then_inc(y_lo_pool.sem, 1)
                    for b in range(NB):
                        pool.wait_ge(res_in[b % 2].sem, res_in[b % 2].at(it, b // 2 + 1))
                        nc.gpsimd.tensor_tensor(res[:, b % 2, :], res[:, b % 2, :], bout_bc[:, :], ALU.add).then_inc(res_ok.sem, 1)
                if pre:
                    mask(it + 1, 1)

            pool.wait_ge(loaded, 16 * n_loads)
            loop(pool, main, tail)

        @block.scalar
        def _(act):
            nc.scalar.preload_act_table_set("natural_log_exp_and_others")
            act.wait_ge(scale_done, 4)
            for k in range(KD):
                act.wait_ge(stage_in[k], 16)
                nc.scalar.activation(w_hi[:, k, :], stage[k], ACT.Copy, scale=w_scale).then_inc(hi_done, 1)
            act.wait_ge(loaded, 16 * n_loads)
            nc.scalar.activation(wo_hi[:, :, :], wo[:, 0:NS, :], ACT.Copy).then_inc(wo_hi_done, 1)
            nc.scalar.activation(wf_hi[:, :], wf[:, :], ACT.Copy).then_inc(wo_hi_done, 1)

            def norm(n):
                act.wait_ge(bn2.sem, bn2.at(n, NB))
                nc.scalar.activation(nt[:, 0, :], mv[:, :, 1], ACT.Ln, bias=col("eps")).then_inc(var_ln.sem, 1)
                act.wait_ge(var_ln.sem, var_ln.at(n, 1))
                act.wait_ge(normed.sem, normed.at(n - 1, NB))
                nc.scalar.activation(nt[:, 1, :], nt[:, 0, :], ACT.Exp, scale=-0.5).then_inc(rstd0.sem, 1)

            def exp_diff(it, n):
                act.wait_ge(diff_mm.sem, diff_mm.at(it, n))
                act.wait_ge(y_mm.sem, y_mm.at(it, n - 2))
                act.wait_ge(gw_ok.sem, gw_ok.at(it, 1))
                g, i = (n - 1) // 2, (n - 1) % 2
                for j in range(2):
                    for q in range(2):
                        for b in range(2):
                            h = 2 * NH + g * HG + 2 * q + j
                            e = nc.scalar.activation(decay[:, i, j, b, q, :], dbank[j][:, (2 * q + b) * T:(2 * q + b + 1) * T],
                                                     ACT.Exp, bias=gw[:, 2 * i + b, h:h + 1])
                e.then_inc(exp_ok.sem, 1)

            def x_out(it, g):
                act.wait_ge(x_mm.sem, x_mm.at(it, g + 1))
                act.wait_ge(dx_ok.sem, dx_ok.at(it, g - 1))
                act.wait_ge(tr_mm.sem, tr_mm.at(it, g - 1))
                nc.scalar.activation(x_t[:, g % 2, :], gp0[:, :], ACT.Copy, scale=ds_col).then_inc(xt_ok.sem, 1)

            def sigmoid(it, g):
                act.wait_ge(z_mm.sem, z_mm.at(it, g + 1))
                act.wait_ge(gate_ok.sem, gate_ok.at(it, g))
                nc.scalar.activation(sig[:, :], gp1[:, :], ACT.Exp, scale=nds_col).then_inc(sig_ok.sem, 1)
                act.wait_ge(sig_ok.sem, sig_ok.at(it, 3 * g + 1))
                nc.scalar.activation(sig[:, :], sig[:, :], ACT.Ln, bias=1.0).then_inc(sig_ok.sem, 1)
                act.wait_ge(sig_ok.sem, sig_ok.at(it, 3 * g + 2))
                nc.scalar.activation(sig[:, :], sig[:, :], ACT.Exp, scale=-1.0).then_inc(sig_ok.sem, 1)

            def e_out(it, g):
                act.wait_ge(e_mm.sem, e_mm.at(it, g + 1))
                act.wait_ge(yc_ok.sem, yc_ok.at(it, 2 * g - 2))
                nc.scalar.activation(ecum[:, g % 2, :], cA[:, :], ACT.Exp).then_inc(e_ok.sem, 1)

            def hidden(it, j):
                act.wait_ge(s_ok.sem, s_ok.at(it, 2))
                act.wait_ge(acc_ok.sem, acc_ok.at(it, j - 1))
                nc.scalar.activation(relu[:, j % 2, :], s_mid[:, :], ACT.Relu, bias=col("b1", j),
                                     scale=col("W1", j)).then_inc(relu_ok.sem, 1)

            def high_y(it, blocks):
                for k in blocks:
                    act.wait_ge(y_ok.sem, y_ok.at(it, k + 1))
                    nc.scalar.activation(y_hi[k], y[:, k, :], ACT.Copy).then_inc(y_hi_ok.sem, 1)

            def high_acc(it):
                act.wait_ge(acc_ok.sem, acc_ok.at(it, INNER))
                act.wait_ge(y_ok.sem, y_ok.at(it, NG))
                for h in range(2):
                    r = slice(MID * h, MID * h + MID)
                    nc.scalar.activation(acc_r[r, h, :], acc[r, :], ACT.Copy).then_inc(acc_hi.sem, 1)

            def high_half(n, k):
                act.wait_ge(z_mm.sem, z_mm.at(n, 0))
                act.wait_ge(xt_mm.sem, xt_mm.at(n, k + 1))
                nc.scalar.activation(x_hi[:, k, :], xt_bank[k][:, :], ACT.Copy).then_inc(hi_ok.sem, 1)

            def main(it, pre):
                for g in range(NG):
                    exp_diff(it, 2 * g + 2)
                    if g + 1 < NG:
                        x_out(it, g + 1)
                    elif pre:
                        high_half(it + 1, 0)
                    for j in hidden_units(g):
                        hidden(it, j)
                    if g + 1 < NG:
                        exp_diff(it, 2 * g + 3)
                        e_out(it, g + 1)
                        sigmoid(it, g + 1)
                    elif pre:
                        for k in range(1, KD):
                            high_half(it + 1, k)
                    if g == NG - 4 and pre:
                        norm(it + 1)
                    act.wait_ge(f_mm.sem, f_mm.at(it, g + 1))
                    act.wait_ge(h_mm.sem, h_mm.at(it, g))
                    nc.scalar.activation(fs[:, :, :], gp0[0:NF, :].rearrange("p (b c) -> p b c", b=NB),
                                         ACT.Copy).then_inc(fs_ok.sem, 1)

            def tail(it, outs, pre):
                n = it + 1
                if outs:
                    act.wait_ge(f_mm.sem, f_mm.at(it, NG))
                    high_y(it, range(NS_DVE))
                    if not pre:
                        high_y(it, range(NS_DVE, NS))
                        high_acc(it)
                if not pre:
                    return
                if not outs:
                    norm(n)
                    for k in range(KD):
                        high_half(n, k)
                act.wait_ge(dta_mm.sem, dta_mm.at(n, 1))
                act.wait_ge(xt_mm.sem, xt_mm.at(n, KD))
                nc.scalar.activation(xb, cA[0:64, :], ACT.Identity, bias=col("dtbias", 0, slice(0, 64)),
                                     scale=scales[0:64, 0:1]).then_inc(xb_ok.sem, 1)
                act.wait_ge(xb_ok.sem, xb_ok.at(n, 1))
                nc.scalar.activation(lg, xb, ACT.Abs).then_inc(soft.sem, 1)
                act.wait_ge(soft.sem, soft.at(n, 1))
                nc.scalar.activation(lg, lg, ACT.Exp, scale=-1.0).then_inc(soft.sem, 1)
                act.wait_ge(soft.sem, soft.at(n, 2))
                nc.scalar.activation(lg, lg, ACT.Ln, bias=1.0).then_inc(soft.sem, 1)
                if outs:
                    high_y(it, range(NS_DVE, NS))
                    high_acc(it)
                act.wait_ge(bc_mm.sem, bc_mm.at(n, 1))
                act.wait_ge(ysum_ok.sem, ysum_ok.at(it, NG))
                act.wait_ge(share.sem, share.at(n - 1, 1))
                act.wait_ge(swap_mm.sem, swap_mm.at(n - 1, 1))
                nc.scalar.activation(rms_a[:, :], gp0[:, :], ACT.Square, scale=ds_col).then_inc(sq_ok.sem, 1)
                nc.scalar.activation(tr2, cA[64:96, :], ACT.Exp, scale=scales[64:96, 1:2]).then_inc(trap_e.sem, 1)
                act.wait_ge(trap_e.sem, trap_e.at(n, 1))
                nc.scalar.activation(tr2, tr2, ACT.Ln, bias=1.0).then_inc(trap_e.sem, 1)
                act.wait_ge(trap_e.sem, trap_e.at(n, 2))
                nc.scalar.activation(tr2, tr2, ACT.Exp, scale=-1.0).then_inc(trap_e.sem, 1)
                act.wait_ge(angle.sem, angle.at(n, 7))
                act.wait_ge(ft_mm.sem, ft_mm.at(n - 1, 1))
                act.wait_ge(sin_mm.sem, sin_mm.at(n - 1, 1))
                nc.scalar.activation(feat[DS:DS + 2 * ROPE, :], th, ACT.Sin).then_inc(sin_ok.sem, 1)
                nc.scalar.preload_act_table_set("natural_log_exp_and_others")
                act.wait_ge(sin_ok.sem, sin_ok.at(n, 1))
                nc.scalar.activation(trig_r[DS:DS + 2 * ROPE, :], feat[DS:DS + 2 * ROPE, :], ACT.Copy).then_inc(trig_hi.sem, 1)
                act.wait_ge(ffn_mm.sem, ffn_mm.at(n, 1))
                act.wait_ge(relu_ok.sem, relu_ok.at(it, INNER))
                for h in range(2):
                    r = slice(MID * h, MID * h + MID)
                    nc.scalar.activation(s_mid[r, :], dA[r, h * 256:h * 256 + 256], ACT.Identity,
                                         bias=col("bin", 0, r), scale=scales[r, 0:1]).then_inc(s_ok.sem, 1)
                act.wait_ge(decay_rate.sem, decay_rate.at(n, 1))
                nc.scalar.activation(av, av, ACT.Exp, scale=-1.0).then_inc(ea_ok.sem, 1)
                act.wait_ge(ms_mm.sem, ms_mm.at(n, 1))
                act.wait_ge(gate_ok.sem, gate_ok.at(it, NG))
                nc.scalar.activation(rms_b[:, :], dB[:, :], ACT.Ln, bias=col("eps")).then_inc(ms_ln.sem, 1)
                act.wait_ge(ms_ln.sem, ms_ln.at(n, 1))
                nc.scalar.activation(rms_b[:, :], rms_b[:, :], ACT.Exp, scale=-0.5).then_inc(rms_ok.sem, 1)
                act.wait_ge(a_ok.sem, a_ok.at(n, 2))
                nc.scalar.activation(av, av, ACT.Ln).then_inc(lna_ok.sem, 1)
                act.wait_ge(cos_mm.sem, cos_mm.at(n, 1))
                act.wait_ge(h2_ok.sem, h2_ok.at(it, 4 * NG))
                nc.scalar.activation(cosx[:, :], cA[:, :], ACT.Identity, bias=col("onerow")).then_inc(cos_ok.sem, 1)
                act.wait_ge(sin_mm.sem, sin_mm.at(n, 1))
                nc.scalar.activation(sinx[:, :], gp1[:, :], ACT.Copy).then_inc(sinx_ok.sem, 1)
                act.wait_ge(cum_ok.sem, cum_ok.at(n, NB))
                act.wait_ge(diff_mm.sem, diff_mm.at(it, 2 * NG))
                act.wait_ge(e_mm.sem, e_mm.at(it, NG))
                act.wait_ge(dend_ok.sem, dend_ok.at(it, NB))
                nc.scalar.activation(cum_r[0:NH, :], cum, ACT.Copy).then_inc(cum_hi.sem, 1)
                act.wait_ge(hm_mm.sem, hm_mm.at(it, 1))
                nc.scalar.activation(hm[2 * NH:, :], cum, ACT.Copy, scale=-1.0).then_inc(cum_hi.sem, 1)
                act.wait_ge(wd_ok.sem, wd_ok.at(n, 1))
                nc.scalar.activation(wd, wd, ACT.Exp).then_inc(we_ok.sem, 1)
                act.wait_ge(share.sem, share.at(n, 4))
                nc.scalar.activation(feat[0:DS, :], bshare[0:DS, :], ACT.Copy).then_inc(top_ok.sem, 1)
                nc.scalar.activation(bshare[DS:, :], bshare[0:DS, :], ACT.Copy).then_inc(base_ok.sem, 1)
                nc.scalar.activation(cshare[0:DS, :], cshare[DS:, :], ACT.Copy).then_inc(base_ok.sem, 1)
                act.wait_ge(hm_mm.sem, hm_mm.at(n, 1))
                act.wait_ge(xs_ok.sem, xs_ok.at(it, 2 * NG))
                act.wait_ge(exp_ok.sem, exp_ok.at(it, 2 * NG))
                nc.scalar.activation(gw[:, :, :], gp0[:, 0:NB * 3 * NH].rearrange("p (b h) -> p b h", b=NB),
                                     ACT.Copy).then_inc(gw_ok.sem, 1)
                act.wait_ge(dend_mm.sem, dend_mm.at(n, 1))
                act.wait_ge(faded.sem, faded.at(it, NG))
                for j in range(2):
                    r = slice(DS * j, DS * j + DS)
                    nc.scalar.activation(dec[r, :, :], gp1[r, 0:NB * NH].rearrange("p (b q j) -> p b q j", b=NB, j=2)[:, :, :, j],
                                         ACT.Exp).then_inc(dec_ok.sem, 1)
                act.wait_ge(ft_mm.sem, ft_mm.at(n, 1))
                act.wait_ge(f_mm.sem, f_mm.at(it, NG))
                nc.scalar.activation(feat_t[:, :, :], cB[:, 0:NB * NF].rearrange("p (b f) -> p b f", b=NB),
                                     ACT.Copy).then_inc(ft_ok.sem, 1)
                x_out(n, 0)
                exp_diff(n, 1)
                e_out(n, 0)
                act.wait_ge(share.sem, share.at(n, 4))
                sigmoid(n, 0)

            loop(act, main, tail)

        @block.vector
        def _(dve):
            for k in range(KD):
                dve.wait_ge(stage_in[k], 16)
                nc.vector.tensor_reduce(scales[:, 4 + k:5 + k], stage[k], AX_X, ALU.max,
                                        apply_absolute_value=True).then_inc(absmax_done, 1)
            dve.wait_ge(absmax_done, KD)
            nc.vector.tensor_reduce(scales[:, 8:9], scales[:, 4:8], AX_X, ALU.max).then_inc(scale_done, 1)
            dve.wait_ge(allmax_done, 1)
            nc.vector.tensor_scalar(scales[:, 10:11].bitcast(I32), scales[:, 9:10].bitcast(I32), 0x7F800000, None,
                                    ALU.bitwise_and).then_inc(scale_done, 1)
            dve.wait_ge(scale_done, 2)
            nc.vector.tensor_scalar(scales[:, 11:12].bitcast(I32), scales[:, 10:11].bitcast(I32), -1.0, float(254 << 23),
                                    ALU.mult, ALU.add).then_inc(scale_done, 1)
            dve.wait_ge(scale_done, 3)
            nc.vector.tensor_scalar(w_scale, scales[:, 11:12], W_SCALE, None, ALU.mult).then_inc(scale_done, 1)
            undo = 1.0 / (XN_SCALE * W_SCALE)
            nc.vector.tensor_scalar(ds_col, scales[:, 10:11], undo, None, ALU.mult).then_inc(scale_done, 1)
            nc.vector.tensor_scalar(nds_col, scales[:, 10:11], -undo, None, ALU.mult).then_inc(scale_done, 1)
            def split_weights(blocks):
                for k in blocks:
                    dve.wait_ge(hi_done, k + 1)
                    nc.vector.scalar_tensor_tensor(out=w_lo[:, k, :], in0=stage[k], scalar=w_scale, in1=w_hi[:, k, :],
                                                   op0=ALU.mult, op1=ALU.subtract).then_inc(lo_done, 1)

            split_weights((0, 1))
            dve.wait_ge(loaded, 16 * n_loads)
            nc.vector.tensor_copy(ind_r[:, :], const("ind", slice(0, 64))).then_inc(ind_ready, 1)
            nc.vector.tensor_copy(ind_ch[:, :, :], const("ind", slice(0, 64)).unsqueeze(2).broadcast_to([64, NH, HD])).then_inc(ind_ready, 1)
            nc.vector.tensor_scalar(ones_r[:, :], const("ident", slice(0, 64)), 0.0, 1.0, ALU.mult, ALU.add).then_inc(ind_ready, 1)
            nc.vector.memset(feat[96:128, :], 1.0).then_inc(ind_ready, 1)
            half = slice(DS, P)
            nc.vector.tensor_copy(sel_r[half, 0, :], const("selcos", half)).then_inc(ind_ready, 1)
            nc.vector.tensor_copy(sel_r[half, 1, :], const("selsin", half)).then_inc(ind_ready, 1)
            dve.wait_ge(ind_ready, 6)
            nc.vector.tensor_scalar(wds_col, scales[:, 10:11], undo, col("normw"), ALU.mult, ALU.mult).then_inc(scale_done, 1)
            dve.wait_ge(scale_done, 7)
            def statistics(n, entries):
                dve.wait_ge(u_in.sem, u_in.at(n, 1))
                for b in entries:
                    nc.vector.bn_stats(stats[:, b, :], xn[:, b, :]).then_inc(bn1.sem, 1)
                for b in entries:
                    dve.wait_ge(bn1.sem, bn1.at(n, b + 1))
                    dve.sem_inc(dve_step, 1)
                    nc.vector.bn_aggr(mv[:, b, :], stats[:, b, :]).then_inc(bn2.sem, 1)

            def refine(n):
                dve.wait_ge(rstd0.sem, rstd0.at(n, 1))
                nc.vector.tensor_tensor(nt[:, 2, :], nt[:, 1, :], nt[:, 1, :], ALU.mult).then_inc(newton.sem, 1)
                dve.wait_ge(newton.sem, newton.at(n, 1))
                nc.vector.scalar_tensor_tensor(out=nt[:, 3, :], in0=mv[:, :, 1], scalar=col("eps"), in1=nt[:, 2, :],
                                               op0=ALU.add, op1=ALU.mult).then_inc(newton.sem, 1)
                dve.wait_ge(newton.sem, newton.at(n, 2))
                nc.vector.tensor_scalar(nt[:, 4, :], nt[:, 3, :], -0.5 * XN_SCALE, 1.5 * XN_SCALE, ALU.mult, ALU.add).then_inc(newton.sem, 1)
                dve.wait_ge(newton.sem, newton.at(n, 3))
                nc.vector.tensor_tensor(nt[:, 0, :], nt[:, 4, :], nt[:, 1, :], ALU.mult).then_inc(newton.sem, 1)

            def norm(n, entries):
                dve.wait_ge(newton.sem, newton.at(n, 4))
                for b in entries:
                    nc.vector.tensor_scalar(xn[:, b, :], xn[:, b, :], mv[:, b, 0:1], nt[:, 0, b:b + 1],
                                            ALU.subtract, ALU.mult).then_inc(normed.sem, 1)

            def low_half(n, k):
                dve.wait_ge(hi_ok.sem, hi_ok.at(n, k + 1))
                nc.vector.tensor_tensor(x_lo[:, k, :], xt_bank[k][:, :], x_hi[:, k, :], ALU.subtract).then_inc(lo_ok.sem, 1)

            def heads(it, g, q):
                slot, pair = g % 2, 2 * g + q
                if q == 0:
                    dve.wait_ge(y_mm.sem, y_mm.at(it, 2 * g - 2))
                for which, (dst, base, ca, cb) in enumerate(((bh, bshare, "cA_B", "cB_B"), (ch, cshare, "cA_C", "cB_C"))):
                    k = 4 * g + 2 * q + which + 1
                    nc.vector.scalar_tensor_tensor(out=dst[:, slot, q, :], in0=cosx[:, :], scalar=col(ca, pair),
                                                   in1=base[:, :], op0=ALU.mult, op1=ALU.add).then_inc(h1_ok.sem, 1)
                    dve.wait_ge(h1_ok.sem, h1_ok.at(it, k))
                    nc.vector.scalar_tensor_tensor(out=dst[:, slot, q, :], in0=sinx[:, :], scalar=col(cb, pair),
                                                   in1=dst[:, slot, q, :], op0=ALU.mult, op1=ALU.add).then_inc(h2_ok.sem, 1)

            def scale_x(it, g):
                dve.wait_ge(tr_mm.sem, tr_mm.at(it, g + 1))
                dve.wait_ge(f_mm.sem, f_mm.at(it, g - 1))
                dve.wait_ge(gw_ok.sem, gw_ok.at(it, 1))
                src = gp0[:, :].rearrange("p (b h d) -> p b h d", b=NB, h=HG)
                for i in range(2):
                    w = gw[:, :, i * NH + g * HG:i * NH + (g + 1) * HG].unsqueeze(3).broadcast_to([P, NB, HG, HD])
                    nc.vector.tensor_tensor(xs[:, g % 2, i].rearrange("p b (h d) -> p b h d", h=HG), src, w,
                                            ALU.mult).then_inc(xs_ok.sem, 1)

            def silu(it, g):
                dve.wait_ge(sig_ok.sem, sig_ok.at(it, 3 * g + 3))
                dve.wait_ge(y_ok.sem, y_ok.at(it, g - 1))
                nc.vector.scalar_tensor_tensor(out=gate[:, g % 2, :], in0=gp1[:, :], scalar=ds_col, in1=sig[:, :],
                                               op0=ALU.mult, op1=ALU.mult).then_inc(gate_ok.sem, 1)

            def scores(it, n):
                dve.wait_ge(cb_mm.sem, cb_mm.at(it, n))
                dve.wait_ge(mask_ok.sem, mask_ok.at(it, n))
                for j in range(2):
                    v = decay[:, (n - 1) % 2, j].rearrange("p b q t -> p (b q t)")
                    m = nc.vector.tensor_tensor(v, cbank[j][:, :], v, ALU.mult)
                m.then_inc(s_mul.sem, 1)

            def combine(it, g, i):
                n = 2 * g + i + 1
                half = slice(i * 256, i * 256 + 256)
                dve.wait_ge(y_mm.sem, y_mm.at(it, n))
                dve.wait_ge(e_ok.sem, e_ok.at(it, g + 1))
                if i == 0:
                    dve.wait_ge(ysum_ok.sem, ysum_ok.at(it, g))
                nc.vector.tensor_tensor(yc[:, half], ybank[i][:, 256:512], ecum[:, g % 2, half], ALU.mult).then_inc(t1_ok.sem, 1)
                dve.wait_ge(t1_ok.sem, t1_ok.at(it, n))
                nc.vector.tensor_tensor(yc[:, half], ybank[i][:, 0:256], yc[:, half], ALU.add).then_inc(yc_ok.sem, 1)

            def update_state(it, g):
                dve.wait_ge(h_mm.sem, h_mm.at(it, g + 1))
                dve.wait_ge(faded.sem, faded.at(it, g + 1))
                s = state[:, 2 * g:2 * g + 2].rearrange("p q b d -> p (q b d)")
                nc.vector.tensor_tensor(s, gp1[:, 0:256], s, ALU.add).then_inc(state_ok.sem, 1)

            def hidden(it, j):
                dve.wait_ge(relu_ok.sem, relu_ok.at(it, j + 1))
                if j == 0:
                    dve.wait_ge(out_mm.sem, out_mm.at(it, 0))
                    nc.vector.tensor_scalar(acc[:, :], relu[:, 0, :], col("W2", 0), col("b2"), ALU.mult, ALU.add).then_inc(acc_ok.sem, 1)
                else:
                    dve.wait_ge(acc_ok.sem, acc_ok.at(it, j))
                    nc.vector.scalar_tensor_tensor(out=acc[:, :], in0=relu[:, j % 2, :], scalar=col("W2", j), in1=acc[:, :],
                                                   op0=ALU.mult, op1=ALU.add).then_inc(acc_ok.sem, 1)

            def main(it, pre):
                for g in range(NG):
                    scores(it, 2 * g + 1)
                    if g == 0:
                        silu(it, 0)
                    else:
                        update_state(it, g - 1)
                    if g + 1 < NG:
                        heads(it, g + 1, 0)
                    elif pre:
                        low_half(it + 1, 0)
                    combine(it, g, 0)
                    if g + 1 < NG:
                        for j in hidden_units(g):
                            hidden(it, j)
                    scores(it, 2 * g + 2)
                    if g + 1 < NG:
                        scale_x(it, g + 1)
                        heads(it, g + 1, 1)
                    else:
                        if pre:
                            for k in range(1, KD):
                                low_half(it + 1, k)
                        for j in hidden_units(g):
                            hidden(it, j)
                    early = g == NG - 3
                    if 1 <= g <= NB and pre:
                        statistics(it + 1, [g - 1])
                    if NG - 3 <= g < NG - 1 and pre:
                        b = 2 * (g - NG + 3)
                        if b == 0:
                            refine(it + 1)
                        norm(it + 1, range(b, b + 2))
                    if early and g + 1 < NG:
                        silu(it, g + 1)
                    combine(it, g, 1)
                    if g + 1 < NG and not early:
                        silu(it, g + 1)

            def out_sum(it, b):
                dve.wait_ge(out_mm.sem, out_mm.at(it, b + 1))
                dve.wait_ge(res_ok.sem, res_ok.at(it, b + 1))
                nc.vector.tensor_tensor(res[:, b % 2, :], ybank[b % 2][:, :], res[:, b % 2, :], ALU.add).then_inc(out_ok.sem, 1)

            def low_acc(it):
                for h in range(2):
                    r, other = slice(MID * h, MID * h + MID), slice(MID * (1 - h), MID * (1 - h) + MID)
                    dve.wait_ge(acc_hi.sem, acc_hi.at(it, h + 1))
                    nc.vector.tensor_tensor(acc_r[other, h, :], acc[r, :], acc_r[r, h, :].bitcast(F32),
                                            ALU.subtract).then_inc(acc_lo.sem, 1)

            def low_y(it):
                for k in range(NS_DVE):
                    dve.wait_ge(y_hi_ok.sem, y_hi_ok.at(it, k + 1))
                    nc.vector.tensor_tensor(y_lo[:, k, :], y[:, k, :], y_hi[k].bitcast(F32),
                                            ALU.subtract).then_inc(y_lo_dve.sem, 1)

            def tail(it, outs, pre):
                n = it + 1
                if outs and not pre:
                    update_state(it, NG - 1)
                    low_y(it)
                    low_acc(it)
                    for b in range(NB):
                        out_sum(it, b)
                    return
                if not outs:
                    statistics(n, range(NB))
                    refine(n)
                    norm(n, range(NB))
                    for k in range(KD):
                        low_half(n, k)
                    split_weights((2, 3))
                    dve.wait_ge(lo_done, KD)
                    dve.wait_ge(mh_done, 2)
                if outs:
                    update_state(it, NG - 1)
                    low_y(it)
                dve.wait_ge(dta_mm.sem, dta_mm.at(n, 1))
                nc.vector.tensor_scalar(th, cA[96:128, :], scales[96:128, 0:1], col("phase", 0, slice(96, 128)),
                                        ALU.mult, ALU.add).then_inc(angle.sem, 1)
                dve.wait_ge(angle.sem, angle.at(n, 1))
                nc.vector.tensor_scalar(kr, th, 1 / (2 * np.pi), MAGIC, ALU.mult, ALU.add).then_inc(angle.sem, 1)
                dve.wait_ge(angle.sem, angle.at(n, 2))
                nc.vector.tensor_scalar(kk, kr, MAGIC, -TWO_PI_HI, ALU.subtract, ALU.mult).then_inc(angle.sem, 1)
                dve.wait_ge(angle.sem, angle.at(n, 3))
                nc.vector.tensor_tensor(th, th, kk, ALU.add).then_inc(angle.sem, 1)
                nc.vector.tensor_scalar(kr, kr, MAGIC, -TWO_PI_LO, ALU.subtract, ALU.mult).then_inc(angle.sem, 1)
                dve.wait_ge(angle.sem, angle.at(n, 5))
                nc.vector.tensor_tensor(th, th, kr, ALU.add).then_inc(angle.sem, 1)
                dve.wait_ge(angle.sem, angle.at(n, 6))
                nc.vector.tensor_scalar(th, th, SIN_MAX, -SIN_MAX, ALU.min, ALU.max).then_inc(angle.sem, 1)
                dve.wait_ge(soft.sem, soft.at(n, 3))
                dve.wait_ge(y_mm.sem, y_mm.at(it, 2 * NG))
                nc.vector.scalar_tensor_tensor(out=dt_, in0=xb[0:NH], scalar=0.0, in1=lg[0:NH], op0=ALU.max,
                                               op1=ALU.add).then_inc(dt_ok.sem, 1)
                nc.vector.scalar_tensor_tensor(out=av, in0=xb[NH:64], scalar=0.0, in1=lg[NH:64], op0=ALU.max,
                                               op1=ALU.add).then_inc(dt_ok.sem, 1)
                dve.wait_ge(dt_ok.sem, dt_ok.at(n, 2))
                nc.vector.scalar_tensor_tensor(out=av, in0=av, scalar=A_FLOOR, in1=dt_, op0=ALU.max,
                                               op1=ALU.mult).then_inc(decay_rate.sem, 1)
                if outs:
                    low_acc(it)
                dve.wait_ge(trap_e.sem, trap_e.at(n, 3))
                nc.vector.tensor_scalar(gg, tr2, -0.5, 1.0, ALU.mult, ALU.add).then_inc(trap.sem, 1)
                nc.vector.tensor_scalar(tr2, tr2, 0.5, A_LEAST, ALU.mult, ALU.max).then_inc(trap.sem, 1)
                dve.wait_ge(trap.sem, trap.at(n, 2))
                dve.wait_ge(hm_mm.sem, hm_mm.at(it, 1))
                nc.vector.tensor_tensor(hm[0:NH, :], gg, dt_, ALU.mult).then_inc(gdt_ok.sem, 1)
                dve.wait_ge(trig_hi.sem, trig_hi.at(n, 1))
                nc.vector.tensor_tensor(trig_r[96:128, :], feat[64:96, :], trig_r[64:96, :].bitcast(F32),
                                        ALU.subtract).then_inc(trig_lo.sem, 1)
                dve.wait_ge(ea_ok.sem, ea_ok.at(n, 1))
                nc.vector.tensor_tensor(av, av, gg, ALU.mult).then_inc(a_ok.sem, 1)
                dve.wait_ge(a_ok.sem, a_ok.at(n, 1))
                nc.vector.tensor_tensor(av, av, tr2, ALU.add).then_inc(a_ok.sem, 1)
                dve.wait_ge(rms_ok.sem, rms_ok.at(n, 1))
                nc.vector.scalar_tensor_tensor(out=rms_a[:, :], in0=gp0[:, :], scalar=wds_col, in1=rms_b[:, :],
                                               op0=ALU.mult, op1=ALU.mult).then_inc(bcn_ok.sem, 1)
                dve.wait_ge(lna_ok.sem, lna_ok.at(n, 1))
                for b in range(NB):
                    nc.vector.tensor_tensor_scan(cum[:, b * T:(b + 1) * T], ones_r[0:NH, :].bitcast(F32), av[:, b * T:(b + 1) * T],
                                                 0.0, ALU.mult, ALU.add).then_inc(cum_ok.sem, 1)
                dve.wait_ge(cum_ok.sem, cum_ok.at(n, NB))
                cum_b = cum.rearrange("p (b t) -> p b t", b=NB)
                nc.vector.tensor_tensor(wd.rearrange("p (b t) -> p b t", b=NB), cum_b[:, :, T - 1:T].broadcast_to([NH, NB, T]),
                                        cum_b, ALU.subtract).then_inc(wd_ok.sem, 1)
                if outs:
                    out_sum(it, 0)
                dve.wait_ge(cos_ok.sem, cos_ok.at(n, 1))
                nc.vector.tensor_tensor(rms_b[:, :], rms_a[:, :], cosx[:, :], ALU.mult).then_inc(share.sem, 1)
                dve.wait_ge(cum_hi.sem, cum_hi.at(n, 1))
                nc.vector.tensor_tensor(cum_r[NH:64, :], cum, cum_r[0:NH, :].bitcast(F32), ALU.subtract).then_inc(cum_lo.sem, 1)
                dve.wait_ge(sinx_ok.sem, sinx_ok.at(n, 1))
                dve.wait_ge(swap_mm.sem, swap_mm.at(n, 1))
                nc.vector.tensor_tensor(bshare[:, :], cB[:, :], sinx[:, :], ALU.mult).then_inc(share.sem, 1)
                dve.wait_ge(share.sem, share.at(n, 2))
                nc.vector.tensor_tensor(bshare[0:DS, :], bshare[0:DS, :], rms_b[0:DS, :], ALU.add).then_inc(share.sem, 1)
                nc.vector.tensor_tensor(cshare[DS:, :], bshare[DS:, :], rms_b[DS:, :], ALU.add).then_inc(share.sem, 1)
                dve.wait_ge(cum_lo.sem, cum_lo.at(n, 1))
                dve.wait_ge(dend_mm.sem, dend_mm.at(it, 1))
                for b in range(NB):
                    nc.vector.tensor_scalar(dend_r[:, b, :], ind_r[:, :].bitcast(F32),
                                            cum_r[:, (b + 1) * T - 1:(b + 1) * T].bitcast(F32), None, ALU.mult).then_inc(dend_ok.sem, 1)
                dve.wait_ge(we_ok.sem, we_ok.at(n, 1))
                dve.wait_ge(gdt_ok.sem, gdt_ok.at(n, 1))
                nc.vector.tensor_tensor(hm[NH:64, :], wd, hm[0:NH, :], ALU.mult).then_inc(hm_ok.sem, 1)
                dve.wait_ge(base_ok.sem, base_ok.at(n, 2))
                heads(n, 0, 0)
                heads(n, 0, 1)
                if outs:
                    out_sum(it, 1)
                    out_sum(it, 2)
                scale_x(n, 0)
                if outs:
                    out_sum(it, 3)

            loop(dve, main, tail)

        @block.tensor
        def _(pe):
            mm = nc.tensor.matmul

            def project(bank, c0):
                for k in range(KD):
                    for i, (w, x) in enumerate(((w_hi, x_hi), (w_hi, x_lo), (w_lo, x_hi))):
                        m = mm(bank[:, :], w[:, k, c0:c0 + P], x[:, k, :], start=(k == 0 and i == 0),
                               stop=(k == KD - 1 and i == 2))
                return m

            def diff(it, n):
                g, i = (n - 1) // 2, (n - 1) % 2
                if g == 0 and i == 0:
                    pe.wait_ge(cum_lo.sem, cum_lo.at(it, 1))
                    pe.wait_ge(s_ok.sem, s_ok.at(it, 2))
                    pe.wait_ge(ms_ln.sem, ms_ln.at(it, 1))
                pe.wait_ge(exp_ok.sem, exp_ok.at(it, n - 1))
                tok = 2 * i * T
                for j in range(2):
                    for q in range(2):
                        h = g * HG + 2 * q + j
                        m = mm(dbank[j][:, q * 256:q * 256 + 256], ind_r[:, h:h + 1].broadcast_to([64, P]), cum_r[:, tok:tok + 256],
                               start=True, stop=True, skip_group_check=True)
                m.then_inc(diff_mm.sem, 1)

            def products(it, n):
                g, i = (n - 1) // 2, (n - 1) % 2
                pe.wait_ge(s_mul.sem, s_mul.at(it, n - 1))
                if i == 0:
                    pe.wait_ge(e_ok.sem, e_ok.at(it, g + 1))
                    pe.wait_ge(h2_ok.sem, h2_ok.at(it, 4 * g + 4))
                    pe.wait_ge(ft_ok.sem, ft_ok.at(it, 1))
                for b in range(2):
                    for q in range(2):
                        for j in range(2):
                            r = slice(DS * j, DS * j + DS)
                            tok = (2 * i + b) * T
                            m = mm(cbank[j][:, (2 * b + q) * T:(2 * b + q + 1) * T], bh[r, g % 2, q, tok:tok + T],
                                   ch[r, g % 2, q, tok:tok + T], start=True, stop=True, skip_group_check=True)
                m.then_inc(cb_mm.sem, 1)

            def outputs(it, n):
                g, i = (n - 1) // 2, (n - 1) % 2
                pe.wait_ge(s_mul.sem, s_mul.at(it, n))
                if g == 0:
                    pe.wait_ge(out_ok.sem, out_ok.at(it, i - 1))
                else:
                    pe.wait_ge(yc_ok.sem, yc_ok.at(it, n - 2))
                pe.wait_ge(xs_ok.sem, xs_ok.at(it, 2 * g + 1))
                pe.wait_ge(state_ok.sem, state_ok.at(it, g + 1 - NG))
                for b in range(2):
                    for h in range(HG):
                        q, j = h // 2, h % 2
                        tok = 2 * i + b
                        rows = slice(HD * h, HD * h + HD)
                        r = slice(DS * j, DS * j + DS)
                        mm(ybank[i][rows, b * T:(b + 1) * T], xs[:, g % 2, 0, tok, rows],
                           decay[:, i, j, b, q, :], start=True, stop=True, skip_group_check=True)
                        m = mm(ybank[i][rows, 256 + b * T:256 + (b + 1) * T], state[r, 2 * g + q, tok, :],
                               ch[r, g % 2, q, tok * T:(tok + 1) * T], start=True, stop=True, skip_group_check=True)
                m.then_inc(y_mm.sem, 1)

            def turn_x(it, g):
                pe.wait_ge(xt_ok.sem, xt_ok.at(it, g + 1))
                for b in range(NB):
                    m = nc.tensor.transpose(gp0[:, b * P:(b + 1) * P], x_t[:, g % 2, b * T:(b + 1) * T], const("ident"))
                m.then_inc(tr_mm.sem, 1)

            def spread_cum(it, g):
                if g == 0:
                    pe.wait_ge(cos_ok.sem, cos_ok.at(it, 1))
                pe.wait_ge(s_mul.sem, s_mul.at(it, 2 * g))
                mm(cA[:, :], ind_ch[:, g * HG:(g + 1) * HG, :].rearrange("p h d -> p (h d)"), cum_r[:, :],
                   start=True, stop=True).then_inc(e_mm.sem, 1)

            def to_heads(it, g):
                pe.wait_ge(fs_ok.sem, fs_ok.at(it, g + 1))
                for h in range(HG):
                    q, j = h // 2, h % 2
                    m = mm(gp1[DS * j:DS * j + DS, q * 128:q * 128 + 128].rearrange("p (b d) -> p b d", b=NB),
                           mh[:, g * HG + h, :], fs[:, :, HD * h:HD * h + HD], start=True, stop=True, skip_group_check=True)
                m.then_inc(h_mm.sem, 1)

            def turn_u(n, k):
                pe.wait_ge(normed.sem, normed.at(n, NB))
                for b in range(NB):
                    m = nc.tensor.transpose(xt_bank[k][:, b * T:(b + 1) * T], xn[:, b, k * P:(k + 1) * P], const("ident"))
                m.then_inc(xt_mm.sem, 1)

            def main(it, pre):
                n = it + 1
                for g in range(NG):
                    products(it, 2 * g + 1)
                    diff(it, 2 * g + 2)
                    if g:
                        pe.wait_ge(gate_ok.sem, gate_ok.at(it, g + 1))
                        to_heads(it, g - 1)
                        pe.wait_ge(fs_ok.sem, fs_ok.at(it, g))
                    else:
                        pe.wait_ge(xs_ok.sem, xs_ok.at(it, 2))
                    if g + 1 < NG:
                        project(gp0, (g + 1) * P).then_inc(x_mm.sem, 1)
                    elif pre:
                        turn_u(n, 0)
                    outputs(it, 2 * g + 1)
                    products(it, 2 * g + 2)
                    if g + 1 < NG:
                        turn_x(it, g + 1)
                        diff(it, 2 * g + 3)
                    if g:
                        pe.wait_ge(state_ok.sem, state_ok.at(it, g))
                    else:
                        pe.wait_ge(gate_ok.sem, gate_ok.at(it, 1))
                    if g + 1 < NG:
                        project(gp1, DI + (g + 1) * P).then_inc(z_mm.sem, 1)
                        spread_cum(it, g + 1)
                    elif pre:
                        pe.wait_ge(exp_ok.sem, exp_ok.at(it, 2 * NG))
                        for k in range(1, KD):
                            turn_u(n, k)
                    outputs(it, 2 * g + 2)
                    if g + 1 < NG:
                        pe.wait_ge(xs_ok.sem, xs_ok.at(it, 2 * g + 4))
                    elif pre:
                        pe.wait_ge(lo_ok.sem, lo_ok.at(n, 1))
                    pe.wait_ge(ft_ok.sem, ft_ok.at(it, 1))
                    for b in range(NB):
                        m = mm(gp0[0:NF, b * P:(b + 1) * P], feat_t[:, b, :], xs[:, g % 2, 1, b, :], start=True,
                               stop=True, skip_group_check=True)
                    m.then_inc(f_mm.sem, 1)

            def project_out(it, b, half):
                bank, tok = ybank[b % 2], b * T
                for k in range(4 * half, min(4 * half + 4, NS)):
                    if k == 0:
                        if b < 2:
                            pe.wait_ge(yc_ok.sem, yc_ok.at(it, 2 * NG - 1 + b))
                        else:
                            pe.wait_ge(out_ok.sem, out_ok.at(it, b - 1))
                    if k < NS_DVE:
                        pe.wait_ge(y_lo_dve.sem, y_lo_dve.at(it, k + 1))
                    else:
                        pe.wait_ge(y_lo_pool.sem, y_lo_pool.at(it, k - NS_DVE + 1))
                    hi, lo = y_hi[k][:, tok:tok + T], y_lo[:, k, tok:tok + T]
                    for i, (a, w) in enumerate(((hi, wo_hi[:, k, :]), (hi, wo_r[:, k, :]), (lo, wo_hi[:, k, :]))):
                        mm(bank[:, :], a, w, start=(k == 0 and i == 0), stop=False)
                if half == 1:
                    pe.wait_ge(y_ok.sem, y_ok.at(it, NG))
                    mm(bank[:, :], y[:, NG - 1, tok:tok + T], wo[:, NG - 1, :], start=False, stop=False)
                    h, cols = b // 2, slice((b % 2) * T, (b % 2 + 1) * T)
                    r = slice(MID * h, MID * h + MID)
                    pe.wait_ge(acc_lo.sem, acc_lo.at(it, h + 1))
                    mm(bank[:, :], acc_r[:, h, cols], wf_hi[:, :], start=False, stop=False)
                    mm(bank[:, :], acc_r[r, h, cols], wf_r[r, :], start=False, stop=True).then_inc(out_mm.sem, 1)

            def tail(it, outs, pre):
                n = it + 1
                if not pre:
                    to_heads(it, NG - 1)
                    for b in range(NB):
                        project_out(it, b, 0)
                        project_out(it, b, 1)
                    return
                if not outs:
                    for k in range(KD):
                        turn_u(n, k)
                    pe.wait_ge(lo_done, KD)
                    pe.wait_ge(wo_lo_done, 2)
                    pe.wait_ge(mh_done, 2)
                    pe.wait_ge(st_zero, 1)
                pe.wait_ge(lo_ok.sem, lo_ok.at(n, KD))
                pe.wait_ge(s_mul.sem, s_mul.at(it, 2 * NG))
                project(cA, C_DTA).then_inc(dta_mm.sem, 1)
                if outs:
                    to_heads(it, NG - 1)
                project(gp0, C_BC).then_inc(bc_mm.sem, 1)
                project(dA, C_FFN).then_inc(ffn_mm.sem, 1)
                pe.wait_ge(sq_ok.sem, sq_ok.at(n, 1))
                mm(dB[:, :], const("mean"), rms_a[:, :], start=True, stop=True).then_inc(ms_mm.sem, 1)
                if outs:
                    project_out(it, 0, 0)
                if outs:
                    project_out(it, 0, 1)
                pe.wait_ge(trig_lo.sem, trig_lo.at(n, 1))
                pe.wait_ge(xb_ok.sem, xb_ok.at(n, 1))
                pe.wait_ge(trap_e.sem, trap_e.at(n, 1))
                pe.wait_ge(angle.sem, angle.at(n, 1))
                pe.wait_ge(state_ok.sem, state_ok.at(it, NG))
                mm(cA[:, :], sel_r[DS:, 0, :], trig_r[DS:, :], start=True, stop=True).then_inc(cos_mm.sem, 1)
                mm(gp1[:, :], sel_r[DS:, 1, :], trig_r[DS:, :], start=True, stop=True).then_inc(sin_mm.sem, 1)
                if outs:
                    project_out(it, 1, 0)
                pe.wait_ge(bcn_ok.sem, bcn_ok.at(n, 1))
                mm(cB[:, :], const("swap"), rms_a[:, :], start=True, stop=True).then_inc(swap_mm.sem, 1)
                if outs:
                    project_out(it, 1, 1)
                if outs:
                    project_out(it, 2, 0)
                pe.wait_ge(dend_ok.sem, dend_ok.at(n, NB))
                pe.wait_ge(sinx_ok.sem, sinx_ok.at(n, 1))
                mm(gp1[:, 0:NB * NH], ones_r[:, :], dend_r[:, :, :].rearrange("p b h -> p (b h)"), start=True,
                   stop=True).then_inc(dend_mm.sem, 1)
                pe.wait_ge(cum_hi.sem, cum_hi.at(n, 2))
                pe.wait_ge(hm_ok.sem, hm_ok.at(n, 1))
                for b in range(NB):
                    m = nc.tensor.transpose(gp0[:, b * 96:(b + 1) * 96], hm[:, b * T:(b + 1) * T], const("ident", slice(0, 96))[:, 0:96])
                m.then_inc(hm_mm.sem, 1)
                pe.wait_ge(top_ok.sem, top_ok.at(n, 1))
                for b in range(NB):
                    m = nc.tensor.transpose(cB[:, b * NF:(b + 1) * NF], feat[0:NF, b * T:(b + 1) * T],
                                            const("ident", slice(0, NF))[:, 0:NF])
                m.then_inc(ft_mm.sem, 1)
                diff(n, 1)
                spread_cum(n, 0)
                if outs:
                    project_out(it, 2, 1)
                pe.wait_ge(gw_ok.sem, gw_ok.at(n, 1))
                project(gp0, 0).then_inc(x_mm.sem, 1)
                if outs:
                    project_out(it, 3, 0)
                turn_x(n, 0)
                if outs:
                    project_out(it, 3, 1)
                pe.wait_ge(dec_ok.sem, dec_ok.at(n, 2))
                project(gp1, DI).then_inc(z_mm.sem, 1)

            pe.wait_ge(loaded, 16 * n_loads)
            pe.wait_ge(ind_ready, 6)
            loop(pe, main, tail)


_OUTS = [((4, 4096, DM), 'float32')]


def layout(inp):
    i = {k: np.asarray(v) for k, v in inp.items()}
    w = i["L0_attn_W_in"]
    o = 2 * DI
    z, x, bc, dta, ang = w[0:DI], w[DI:o], w[o:o + 2 * DS], w[o + 2 * DS:o + 2 * DS + 3 * NH], w[o + 2 * DS + 3 * NH:]
    ffn = i["L0_ffn_Win"].T
    w_in = np.concatenate([x, z, dta, ang, ang, bc, ffn, ffn]).T
    pcols = np.zeros((P, N_PCOLS), np.float32)
    part = {k: pcols[:, a:a + n] for k, (a, n) in PC.items()}
    part["normw"][:, 0] = np.concatenate([i["L0_attn_Bn_w"], i["L0_attn_Cn_w"]])
    part["dtbias"][0:NH, 0] = i["L0_attn_dt_bias"]
    part["phase"][96 + ROPE:, 0] = np.pi / 2
    part["onerow"][:, 0] = np.arange(P) % DS >= 2 * ROPE
    part["eps"][:] = EPS
    twice = lambda a: np.concatenate([a, a])
    part["bin"][:, 0] = twice(i["L0_ffn_bin_"])
    part["b2"][:, 0] = twice(i["L0_ffn_b2"])
    part["W1"][:], part["b1"][:], part["W2"][:] = (twice(i["L0_ffn_" + k]) for k in ("W1", "b1", "W2"))
    part["D"][:] = np.repeat(i["L0_attn_D"], HD).reshape(NG, P).T
    swap = np.arange(DS)
    swap[:2 * ROPE] = (swap[:2 * ROPE] + ROPE) % (2 * ROPE)
    for k, name in (("B", "L0_attn_B_bias"), ("C", "L0_attn_C_bias")):
        b = i[name].reshape(16, 2, DS)
        part["cA_" + k][:] = b.transpose(1, 2, 0).reshape(P, 16)
        part["cB_" + k][:] = b[:, :, swap].transpose(1, 2, 0).reshape(P, 16)
    mh_bias = np.stack([i["L0_attn_B_bias"][:, swap], i["L0_attn_B_bias"]])
    return {"u": i["L0_attn_u"], "w_in": w_in, "w_out": i["L0_attn_W_out"].T, "w_ffn": twice(i["L0_ffn_Wout"]),
            "pcols": pcols, "bout": i["L0_ffn_bout"][None, :], "mh_bias": mh_bias, "consts": constants()}


def kernel(**inputs):
    import concourse.bacc as _bacc
    from concourse.bass_utils import run_bass_kernel_spmd as _run

    nc = _bacc.Bacc("TRN2", target_bir_lowering=False, num_devices=1)
    arrays, args = {}, []
    for name, a in layout(inputs).items():
        a = np.ascontiguousarray(a)
        arrays[f"in_{name}_dram"] = a
        args.append(nc.dram_tensor(f"in_{name}_dram", a.shape, mybir.dt.from_np(a.dtype), kind="ExternalInput").ap())
    for i, (shape, dtype) in enumerate(_OUTS):
        args.append(nc.dram_tensor(f"out_{i}_dram", shape, mybir.dt.from_np(np.dtype(dtype)), kind="ExternalOutput").ap())
    mixer(nc, *args, n_iter=arrays["in_u_dram"].shape[1] // T)
    r = _run(nc, [arrays], core_ids=[0])
    return r.results[0]["out_0_dram"]
```
